# Optimizing a Trainium2 kernel written in Bass

```python
import numpy as np
import jax
import jax.numpy as jnp

def _softmax(x, axis=-1):
    return jax.nn.softmax(x, axis=axis)

def _gelu(x):
    return jax.nn.gelu(x, approximate=True)

def _silu(x):
    return jax.nn.silu(x)

def _sigmoid(x):
    return jax.nn.sigmoid(x)

def _layernorm(x, axis=-1, eps=1e-05):
    m = jnp.mean(x, axis=axis, keepdims=True)
    v = jnp.var(x, axis=axis, keepdims=True)
    return (x - m) / jnp.sqrt(v + eps)

def _scatter_add(tgt, idx, src, axis=0):
    return tgt.at[idx].add(src)

def _segment_sum(src, seg, n):
    return jax.ops.segment_sum(src, seg, n)
kernel_name = 'mk_vit_tower_cls_d4_tok_img1024_r4_5d55a5'

def setup_inputs(seed: int=0):
    np.random.seed(seed)
    _w = jnp.asarray

    def _rec_inputs():
        import jax
        import jax.numpy as jnp
        _rk = jax.random.key(seed)
        x = 7.22013e-05 + 1.00017 * jax.random.normal(jax.random.fold_in(_rk, 1), (4, 1, 512, 256), jnp.float32)
        cls_tok = 0.02 * jax.random.normal(jax.random.fold_in(_rk, 5), (1, 1, 256), jnp.float32)
        return (x, cls_tok)
    x, cls_tok = _rec_inputs()

    def _L0_tok_setup():
        import jax, jax.numpy as jnp
        import numpy as np
        import math
        EMBED_DIM = 256
        NUM_HEADS = 16
        HEAD_DIM = EMBED_DIM // NUM_HEADS
        INPUT_DIM = 256
        key = jax.random.key(seed)
        k_x, k_wqkv, k_wout = jax.random.split(key, 3)
        x = jax.random.normal(k_x, (4, 1, 512, INPUT_DIM), dtype=jnp.float32)

        def xavier(k, shape):
            fan_out, fan_in = shape
            bound = math.sqrt(6.0 / (fan_in + fan_out))
            return jax.random.uniform(k, shape, jnp.float32, -bound, bound)
        w_qkv = xavier(k_wqkv, (3 * EMBED_DIM, INPUT_DIM))
        b_qkv = jnp.zeros((3 * EMBED_DIM,), jnp.float32)
        w_out = xavier(k_wout, (EMBED_DIM, EMBED_DIM))
        b_out = jnp.zeros((EMBED_DIM,), jnp.float32)
        return {'x': x, 'w_qkv': w_qkv, 'b_qkv': b_qkv, 'w_out': w_out, 'b_out': b_out}
    _L0_tok_all = _L0_tok_setup()
    _L0_tok_in = {k: v for k, v in _L0_tok_all.items() if k in ('w_qkv', 'b_qkv', 'w_out', 'b_out')}
    del _L0_tok_all

    def _L0_attn_setup():
        import jax, jax.numpy as jnp
        import numpy as np
        EMBED_DIM = 256
        NUM_HEADS = 16
        HEAD_DIM = EMBED_DIM // NUM_HEADS

        def _kernel_exp(x):
            return jnp.exp(x - jnp.max(x, axis=-1, keepdims=True))
        key = jax.random.key(seed)
        ks = jax.random.split(key, 9)
        s = 1.0 / np.sqrt(EMBED_DIM)
        inp = {'x': jax.random.normal(ks[0], (4, 2048, EMBED_DIM), dtype=jnp.float32)}
        for i, name in enumerate(['q', 'k', 'v', 'o']):
            inp[f'W{name}'] = jax.random.uniform(ks[1 + 2 * i], (EMBED_DIM, EMBED_DIM), jnp.float32, -s, s)
            inp[f'b{name}'] = jax.random.uniform(ks[2 + 2 * i], (EMBED_DIM,), jnp.float32, -s, s)
        return inp
    _L0_attn_all = _L0_attn_setup()
    _L0_attn_in = {k: v for k, v in _L0_attn_all.items() if k in ('Wq', 'bq', 'Wk', 'bk', 'Wv', 'bv', 'Wo', 'bo')}
    del _L0_attn_all

    def _L0_ffn_setup():
        import jax, jax.numpy as jnp
        import numpy as np
        B, S, D = (2, 512, 256)
        E, K, F = (16, 2, 128)
        FS = 256
        key = jax.random.key(seed)
        ks = jax.random.split(key, 8)

        def w(k, shape, fan_in):
            return jax.random.normal(k, shape, jnp.float32) / np.sqrt(fan_in).astype(np.float32)
        return {'x': jax.random.normal(ks[0], (B, S, D), jnp.float32), 'Wr': w(ks[1], (D, E), D), 'Wg': w(ks[2], (E, D, F), D), 'Wu': w(ks[3], (E, D, F), D), 'Wd': w(ks[4], (E, F, D), F), 'Sg': w(ks[5], (D, FS), D), 'Su': w(ks[6], (D, FS), D), 'Sd': w(ks[7], (FS, D), FS)}
    _L0_ffn_all = _L0_ffn_setup()
    _L0_ffn_in = {k: v for k, v in _L0_ffn_all.items() if k in ('Wr', 'Wg', 'Wu', 'Wd', 'Sg', 'Su', 'Sd')}
    del _L0_ffn_all

    def _L1_attn_setup():
        import jax, jax.numpy as jnp
        import numpy as np
        import math
        DIM = 256
        NUM_HEADS = 16
        HEAD_DIM = DIM // NUM_HEADS
        MAX_BIAS = 8.0
        SCALE = HEAD_DIM ** (-0.5)

        def _alibi_slopes(n):

            def pow2(n):
                start = 2.0 ** (-2.0 ** (-(math.log2(n) - 3)))
                return [start * start ** i for i in range(n)]
            if math.log2(n).is_integer():
                return pow2(n)
            c = 2 ** math.floor(math.log2(n))
            return pow2(c) + _alibi_slopes(2 * c)[0::2][:n - c]

        def _rotate_half(t):
            t1, t2 = jnp.split(t, 2, axis=-1)
            return jnp.concatenate([-t2, t1], axis=-1)
        key = jax.random.key(seed)
        k1, k2, k3, k4 = jax.random.split(key, 4)
        B, N, C = (2, 512, DIM)
        x = jax.random.normal(k1, (B, N, C), dtype=jnp.float32)
        qkv_w = jax.random.normal(k2, (3 * C, C), dtype=jnp.float32) * C ** (-0.5)
        proj_w = jax.random.normal(k3, (C, C), dtype=jnp.float32) * C ** (-0.5)
        proj_b = jax.random.normal(k4, (C,), dtype=jnp.float32) * 0.01
        slopes = jnp.asarray(np.array(_alibi_slopes(NUM_HEADS), dtype=np.float32))
        return {'x': x, 'qkv_w': qkv_w, 'proj_w': proj_w, 'proj_b': proj_b, 'slopes': slopes}
    _L1_attn_all = _L1_attn_setup()
    _L1_attn_in = {k: v for k, v in _L1_attn_all.items() if k in ('qkv_w', 'proj_w', 'proj_b', 'slopes')}
    del _L1_attn_all

    def _L1_ffn_setup():
        import jax, jax.numpy as jnp
        import numpy as np
        from jax import lax
        DIM = 256
        INTER = 128
        N_EXPERTS = 16
        TOPK = 4
        ROUTE_SCALE = 2.5
        VOCAB = 8000

        def _silu_and_mul(gu):
            gate, up = jnp.split(gu, 2, axis=-1)
            return jax.nn.silu(gate) * up
        key = jax.random.key(seed)
        ks = jax.random.split(key, 8)
        x = jax.random.normal(ks[0], (2, 128, DIM), dtype=jnp.float32)
        input_ids = jax.random.randint(ks[1], (2, 128), 0, VOCAB)
        s = 0.02
        gate_w = jax.random.normal(ks[2], (N_EXPERTS, DIM), dtype=jnp.float32) * s
        gate_b = jax.random.normal(ks[3], (N_EXPERTS,), dtype=jnp.float32) * s
        w13 = jax.random.normal(ks[4], (N_EXPERTS, 2 * INTER, DIM), dtype=jnp.float32) * s
        w2 = jax.random.normal(ks[5], (N_EXPERTS, DIM, INTER), dtype=jnp.float32) * s
        w13_s = jax.random.normal(ks[6], (2 * INTER, DIM), dtype=jnp.float32) * s
        w2_s = jax.random.normal(ks[7], (DIM, INTER), dtype=jnp.float32) * s
        return {'x': x, 'input_ids': input_ids, 'gate_w': gate_w, 'gate_b': gate_b, 'w13': w13, 'w2': w2, 'w13_s': w13_s, 'w2_s': w2_s}
    _L1_ffn_all = _L1_ffn_setup()
    _L1_ffn_in = {k: v for k, v in _L1_ffn_all.items() if k in ('input_ids', 'gate_w', 'gate_b', 'w13', 'w2', 'w13_s', 'w2_s')}
    del _L1_ffn_all

    def _L2_attn_setup():
        import jax, jax.numpy as jnp
        import numpy as np
        SEG = 4
        H = 8
        D = 256
        B = 8
        S = 1024
        key = jax.random.key(seed)
        ks = jax.random.split(key, 9)
        s = 0.02
        return {'x': jax.random.normal(ks[0], (B, S, D), dtype=jnp.float32), 'proj_qk_w': jax.random.normal(ks[1], (D, D), dtype=jnp.float32) * s, 'proj_qk_b': jax.random.normal(ks[2], (D,), dtype=jnp.float32) * s, 'proj_v_w': jax.random.normal(ks[3], (D, D), dtype=jnp.float32) * s, 'proj_v_b': jax.random.normal(ks[4], (D,), dtype=jnp.float32) * s, 'in_proj_w': jax.random.normal(ks[5], (3 * D, D), dtype=jnp.float32) * s, 'in_proj_b': jax.random.normal(ks[6], (3 * D,), dtype=jnp.float32) * s, 'out_proj_w': jax.random.normal(ks[7], (D, D), dtype=jnp.float32) * s, 'out_proj_b': jax.random.normal(ks[8], (D,), dtype=jnp.float32) * s}
    _L2_attn_all = _L2_attn_setup()
    _L2_attn_in = {k: v for k, v in _L2_attn_all.items() if k in ('proj_qk_w', 'proj_qk_b', 'proj_v_w', 'proj_v_b', 'in_proj_w', 'in_proj_b', 'out_proj_w', 'out_proj_b')}
    del _L2_attn_all

    def _L2_ffn_setup():
        import jax, jax.numpy as jnp
        import numpy as np
        E = 8
        D = 256
        H = 512
        TOP_K = 2
        key = jax.random.key(seed)
        k_x, k_g, k_w1, k_w2 = jax.random.split(key, 4)
        B, S = (4, 512)
        inp = {'input': jax.random.normal(k_x, (B, S, D), dtype=jnp.float32), 'Wg': jax.random.normal(k_g, (D, E), dtype=jnp.float32) * 0.02, 'W1': jax.random.normal(k_w1, (E, D, H), dtype=jnp.float32) * 0.02, 'b1': jnp.zeros((E, H), dtype=jnp.float32), 'W2': jax.random.normal(k_w2, (E, H, D), dtype=jnp.float32) * 0.02, 'b2': jnp.zeros((E, D), dtype=jnp.float32)}
        return inp
    _L2_ffn_all = _L2_ffn_setup()
    _L2_ffn_in = {k: v for k, v in _L2_ffn_all.items() if k in ('Wg', 'W1', 'b1', 'W2', 'b2')}
    del _L2_ffn_all

    def _L3_attn_setup():
        import jax, jax.numpy as jnp
        import numpy as np
        D_MODEL = 256
        QHEADS = 16
        KVHEADS = 4
        G = QHEADS // KVHEADS
        D_Q = D_MODEL // QHEADS
        D_KV = D_MODEL // QHEADS * KVHEADS
        BATCH, SEQ = (2, 512)

        def _xavier(key, shape):
            fan_out, fan_in = shape
            lim = (6.0 / (fan_in + fan_out)) ** 0.5
            return jax.random.uniform(key, shape, jnp.float32, -lim, lim)
        key = jax.random.key(seed)
        ks = jax.random.split(key, 5)
        x = jax.random.normal(ks[0], (BATCH, SEQ, D_MODEL), jnp.float32)
        wq = _xavier(ks[1], (D_MODEL, D_MODEL))
        bq = jnp.zeros((D_MODEL,), jnp.float32)
        wk = _xavier(ks[2], (D_KV, D_MODEL))
        bk = jnp.zeros((D_KV,), jnp.float32)
        wv = _xavier(ks[3], (D_KV, D_MODEL))
        bv = jnp.zeros((D_KV,), jnp.float32)
        wo = _xavier(ks[4], (D_MODEL, D_MODEL))
        bo = jnp.zeros((D_MODEL,), jnp.float32)
        return {'x': x, 'wq': wq, 'bq': bq, 'wk': wk, 'bk': bk, 'wv': wv, 'bv': bv, 'wo': wo, 'bo': bo}
    _L3_attn_all = _L3_attn_setup()
    _L3_attn_in = {k: v for k, v in _L3_attn_all.items() if k in ('wq', 'bq', 'wk', 'bk', 'wv', 'bv', 'wo', 'bo')}
    del _L3_attn_all

    def _L3_ffn_setup():
        import jax, jax.numpy as jnp
        import numpy as np
        EPS = 1e-06
        LN_EPS = 1e-05

        def _absmean_core(W):
            gamma = jnp.mean(jnp.abs(W)) + EPS
            Ws = W / gamma
            Wq = jnp.sign(Ws) * jnp.minimum(jnp.round(jnp.abs(Ws)), 1.0)
            return (Wq, gamma)

        @jax.custom_vjp
        def absmean(W):
            return _absmean_core(W)[0]

        def _absmean_fwd(W):
            Wq, gamma = _absmean_core(W)
            return (Wq, gamma)

        def _absmean_bwd(gamma, g):
            return (g / gamma,)
        absmean.defvjp(_absmean_fwd, _absmean_bwd)

        def layernorm(x, w, b, eps=LN_EPS):
            mu = jnp.mean(x, axis=-1, keepdims=True)
            var = jnp.mean((x - mu) ** 2, axis=-1, keepdims=True)
            return (x - mu) * jax.lax.rsqrt(var + eps) * w + b
        key = jax.random.key(seed)
        k1, k2, k3 = jax.random.split(key, 3)
        d, h = (256, 1024)
        B, T = (8, 512)
        return {'x': jax.random.normal(k1, (B, T, d), jnp.float32), 'W_fc': jax.random.normal(k2, (h, d), jnp.float32), 'ln_w': jnp.ones((h,), jnp.float32), 'ln_b': jnp.zeros((h,), jnp.float32), 'W_proj': jax.random.normal(k3, (d, h), jnp.float32)}
    _L3_ffn_all = _L3_ffn_setup()
    _L3_ffn_in = {k: v for k, v in _L3_ffn_all.items() if k in ('W_fc', 'ln_w', 'ln_b', 'W_proj')}
    del _L3_ffn_all
    return {'x': x, 'cls_tok': cls_tok, 'L0_tok_w_qkv': _L0_tok_in['w_qkv'], 'L0_tok_b_qkv': _L0_tok_in['b_qkv'], 'L0_tok_w_out': _L0_tok_in['w_out'], 'L0_tok_b_out': _L0_tok_in['b_out'], 'L0_attn_Wq': _L0_attn_in['Wq'], 'L0_attn_bq': _L0_attn_in['bq'], 'L0_attn_Wk': _L0_attn_in['Wk'], 'L0_attn_bk': _L0_attn_in['bk'], 'L0_attn_Wv': _L0_attn_in['Wv'], 'L0_attn_bv': _L0_attn_in['bv'], 'L0_attn_Wo': _L0_attn_in['Wo'], 'L0_attn_bo': _L0_attn_in['bo'], 'L0_ffn_Wr': _L0_ffn_in['Wr'], 'L0_ffn_Wg': _L0_ffn_in['Wg'], 'L0_ffn_Wu': _L0_ffn_in['Wu'], 'L0_ffn_Wd': _L0_ffn_in['Wd'], 'L0_ffn_Sg': _L0_ffn_in['Sg'], 'L0_ffn_Su': _L0_ffn_in['Su'], 'L0_ffn_Sd': _L0_ffn_in['Sd'], 'L1_attn_qkv_w': _L1_attn_in['qkv_w'], 'L1_attn_proj_w': _L1_attn_in['proj_w'], 'L1_attn_proj_b': _L1_attn_in['proj_b'], 'L1_attn_slopes': _L1_attn_in['slopes'], 'L1_ffn_input_ids': _L1_ffn_in['input_ids'], 'L1_ffn_gate_w': _L1_ffn_in['gate_w'], 'L1_ffn_gate_b': _L1_ffn_in['gate_b'], 'L1_ffn_w13': _L1_ffn_in['w13'], 'L1_ffn_w2': _L1_ffn_in['w2'], 'L1_ffn_w13_s': _L1_ffn_in['w13_s'], 'L1_ffn_w2_s': _L1_ffn_in['w2_s'], 'L2_attn_proj_qk_w': _L2_attn_in['proj_qk_w'], 'L2_attn_proj_qk_b': _L2_attn_in['proj_qk_b'], 'L2_attn_proj_v_w': _L2_attn_in['proj_v_w'], 'L2_attn_proj_v_b': _L2_attn_in['proj_v_b'], 'L2_attn_in_proj_w': _L2_attn_in['in_proj_w'], 'L2_attn_in_proj_b': _L2_attn_in['in_proj_b'], 'L2_attn_out_proj_w': _L2_attn_in['out_proj_w'], 'L2_attn_out_proj_b': _L2_attn_in['out_proj_b'], 'L2_ffn_Wg': _L2_ffn_in['Wg'], 'L2_ffn_W1': _L2_ffn_in['W1'], 'L2_ffn_b1': _L2_ffn_in['b1'], 'L2_ffn_W2': _L2_ffn_in['W2'], 'L2_ffn_b2': _L2_ffn_in['b2'], 'L3_attn_wq': _L3_attn_in['wq'], 'L3_attn_bq': _L3_attn_in['bq'], 'L3_attn_wk': _L3_attn_in['wk'], 'L3_attn_bk': _L3_attn_in['bk'], 'L3_attn_wv': _L3_attn_in['wv'], 'L3_attn_bv': _L3_attn_in['bv'], 'L3_attn_wo': _L3_attn_in['wo'], 'L3_attn_bo': _L3_attn_in['bo'], 'L3_ffn_W_fc': _L3_ffn_in['W_fc'], 'L3_ffn_ln_w': _L3_ffn_in['ln_w'], 'L3_ffn_ln_b': _L3_ffn_in['ln_b'], 'L3_ffn_W_proj': _L3_ffn_in['W_proj']}

def reference(x, cls_tok, L0_tok_w_qkv, L0_tok_b_qkv, L0_tok_w_out, L0_tok_b_out, L0_attn_Wq, L0_attn_bq, L0_attn_Wk, L0_attn_bk, L0_attn_Wv, L0_attn_bv, L0_attn_Wo, L0_attn_bo, L0_ffn_Wr, L0_ffn_Wg, L0_ffn_Wu, L0_ffn_Wd, L0_ffn_Sg, L0_ffn_Su, L0_ffn_Sd, L1_attn_qkv_w, L1_attn_proj_w, L1_attn_proj_b, L1_attn_slopes, L1_ffn_input_ids, L1_ffn_gate_w, L1_ffn_gate_b, L1_ffn_w13, L1_ffn_w2, L1_ffn_w13_s, L1_ffn_w2_s, L2_attn_proj_qk_w, L2_attn_proj_qk_b, L2_attn_proj_v_w, L2_attn_proj_v_b, L2_attn_in_proj_w, L2_attn_in_proj_b, L2_attn_out_proj_w, L2_attn_out_proj_b, L2_ffn_Wg, L2_ffn_W1, L2_ffn_b1, L2_ffn_W2, L2_ffn_b2, L3_attn_wq, L3_attn_bq, L3_attn_wk, L3_attn_bk, L3_attn_wv, L3_attn_bv, L3_attn_wo, L3_attn_bo, L3_ffn_W_fc, L3_ffn_ln_w, L3_ffn_ln_b, L3_ffn_W_proj):
    import jax
    import jax.numpy as jnp

    def _L0_tok_ref(x, w_qkv, b_qkv, w_out, b_out):
        import jax, jax.numpy as jnp
        import numpy as np
        import math
        EMBED_DIM = 256
        NUM_HEADS = 16
        HEAD_DIM = EMBED_DIM // NUM_HEADS
        INPUT_DIM = 256
        B, y, S, _ = x.shape
        qkv = jnp.einsum('bysd,ed->byse', x, w_qkv) + b_qkv
        qkv = qkv.reshape(B, S, NUM_HEADS, 3 * HEAD_DIM).transpose(0, 2, 1, 3)
        q, k, v = jnp.split(qkv, 3, axis=-1)
        logits = jnp.einsum('bhqd,bhkd->bhqk', q, k) / math.sqrt(HEAD_DIM)
        attn = jax.nn.softmax(logits, axis=-1)
        vals = jnp.einsum('bhqk,bhkd->bhqd', attn, v)
        vals = vals.transpose(0, 2, 1, 3).reshape(B, S, EMBED_DIM)
        return jnp.einsum('bse,oe->bso', vals, w_out) + b_out

    def _L0_attn_ref(x, Wq, bq, Wk, bk, Wv, bv, Wo, bo):
        import jax, jax.numpy as jnp
        import numpy as np
        EMBED_DIM = 256
        NUM_HEADS = 16
        HEAD_DIM = EMBED_DIM // NUM_HEADS

        def _kernel_exp(x):
            return jnp.exp(x - jnp.max(x, axis=-1, keepdims=True))
        b, s, e = x.shape

        def proj(W, bias):
            return (x @ W.T + bias).reshape(b, s, NUM_HEADS, HEAD_DIM).transpose(0, 2, 1, 3)
        q = proj(Wq, bq)
        k = proj(Wk, bk)
        v = proj(Wv, bv)
        q_kern = _kernel_exp(q)
        k_kern = _kernel_exp(k)
        kv = jnp.einsum('bhsd,bhse->bhde', k_kern, v)
        k_sum = jnp.sum(k_kern, axis=2)
        denom = jnp.einsum('bhqd,bhd->bhq', q_kern, k_sum) + 1e-06
        y = jnp.einsum('bhqd,bhde->bhqe', q_kern, kv) / denom[..., None]
        y = y.transpose(0, 2, 1, 3).reshape(b, s, e)
        return y @ Wo.T + bo

    def _L0_ffn_ref(x, Wr, Wg, Wu, Wd, Sg, Su, Sd):
        import jax, jax.numpy as jnp
        import numpy as np
        B, S, D = (2, 512, 256)
        E, K, F = (16, 2, 128)
        FS = 256
        b, s, d = x.shape
        T = b * s
        xf = x.reshape(T, d)
        shared = jax.nn.silu(xf @ Sg) * (xf @ Su) @ Sd
        probs = jax.nn.softmax(xf @ Wr, axis=-1)
        topk_p, topk_i = jax.lax.top_k(probs, K)
        n_exp = Wr.shape[1]
        cw = jnp.zeros((T, n_exp), x.dtype).at[jnp.arange(T)[:, None], topk_i].add(topk_p)

        def step(acc, ew):
            wg, wu, wd, c = ew
            y = jax.nn.silu(xf @ wg) * (xf @ wu) @ wd
            return (acc + y * c[:, None], None)
        routed, _ = jax.lax.scan(step, jnp.zeros_like(xf), (Wg, Wu, Wd, cw.T))
        return (routed + shared).reshape(b, s, d)

    def _L1_attn_ref(x, qkv_w, proj_w, proj_b, slopes):
        import jax, jax.numpy as jnp
        import numpy as np
        import math
        DIM = 256
        NUM_HEADS = 16
        HEAD_DIM = DIM // NUM_HEADS
        MAX_BIAS = 8.0
        SCALE = HEAD_DIM ** (-0.5)

        def _alibi_slopes(n):

            def pow2(n):
                start = 2.0 ** (-2.0 ** (-(math.log2(n) - 3)))
                return [start * start ** i for i in range(n)]
            if math.log2(n).is_integer():
                return pow2(n)
            c = 2 ** math.floor(math.log2(n))
            return pow2(c) + _alibi_slopes(2 * c)[0::2][:n - c]

        def _rotate_half(t):
            t1, t2 = jnp.split(t, 2, axis=-1)
            return jnp.concatenate([-t2, t1], axis=-1)
        B, N, C = x.shape
        H, D = (NUM_HEADS, HEAD_DIM)
        qkv = (x @ qkv_w.T).reshape(B, N, 3, H, D).transpose(2, 0, 3, 1, 4)
        q, k, v = (qkv[0], qkv[1], qkv[2])
        inv_freq = 1.0 / 10000.0 ** (jnp.arange(0, D, 2, dtype=jnp.float32) / D)
        freqs = jnp.arange(N, dtype=jnp.float32)[:, None] * inv_freq[None, :]
        sin = jnp.tile(jnp.sin(freqs), (1, 2))
        cos = jnp.tile(jnp.cos(freqs), (1, 2))
        q = q * cos + _rotate_half(q) * sin
        k = k * cos + _rotate_half(k) * sin
        attn = jnp.einsum('bhqd,bhkd->bhqk', q, k) * SCALE
        pos = jnp.arange(N, dtype=jnp.float32)
        diff = pos[None, :] - pos[:, None]
        diff = jnp.where(diff > 0, 0.0, diff)
        alibi = diff[None, :, :] * slopes[:, None, None] * MAX_BIAS
        attn = attn + alibi[None]
        w = jax.nn.softmax(attn, axis=-1)
        out = jnp.einsum('bhqk,bhkd->bhqd', w, v)
        out = out.transpose(0, 2, 1, 3).reshape(B, N, C)
        return out @ proj_w.T + proj_b

    def _L1_ffn_ref(x, input_ids, gate_w, gate_b, w13, w2, w13_s, w2_s):
        import jax, jax.numpy as jnp
        import numpy as np
        from jax import lax
        DIM = 256
        INTER = 128
        N_EXPERTS = 16
        TOPK = 4
        ROUTE_SCALE = 2.5
        VOCAB = 8000

        def _silu_and_mul(gu):
            gate, up = jnp.split(gu, 2, axis=-1)
            return jax.nn.silu(gate) * up
        B, S, D = x.shape
        xt = x.reshape(-1, D)
        T = xt.shape[0]
        scores = jax.nn.sigmoid(xt.astype(jnp.float32) @ gate_w.T)
        biased = scores + gate_b
        _, idx = lax.top_k(biased, TOPK)
        w = jnp.take_along_axis(scores, idx, axis=-1)
        w = w / jnp.sum(w, axis=-1, keepdims=True)
        w = w * ROUTE_SCALE
        comb = jnp.zeros((T, N_EXPERTS), jnp.float32)
        comb = comb.at[jnp.arange(T)[:, None], idx].add(w)
        comb = comb.astype(x.dtype)

        def expert_body(y, args):
            w13_e, w2_e, c_e = args
            h = _silu_and_mul(xt @ w13_e.T)
            return (y + c_e[:, None] * (h @ w2_e.T), None)
        y, _ = lax.scan(expert_body, jnp.zeros_like(xt), (w13, w2, comb.T))
        y = y + _silu_and_mul(xt @ w13_s.T) @ w2_s.T
        return y.astype(x.dtype).reshape(B, S, D)

    def _L2_attn_ref(x, proj_qk_w, proj_qk_b, proj_v_w, proj_v_b, in_proj_w, in_proj_b, out_proj_w, out_proj_b):
        import jax, jax.numpy as jnp
        import numpy as np
        SEG = 4
        H = 8
        D = 256
        B = 8
        S = 1024
        b, seq_len, d = x.shape
        hd = d // H
        pad = SEG - seq_len % SEG
        x = jnp.concatenate([x, x[:, :pad]], axis=1)
        T = seq_len + pad
        a = T // SEG
        xb = x.reshape(b, a, SEG, d).transpose(1, 0, 2, 3).reshape(a * b, SEG, d)
        qk_in = xb @ proj_qk_w.T + proj_qk_b
        v_in = xb @ proj_v_w.T + proj_v_b
        wq, wk, wv = jnp.split(in_proj_w, 3, axis=0)
        bq, bk, bv = jnp.split(in_proj_b, 3)
        q = (qk_in @ wq.T + bq).reshape(a * b, SEG, H, hd)
        k = (qk_in @ wk.T + bk).reshape(a * b, SEG, H, hd)
        v = (v_in @ wv.T + bv).reshape(a * b, SEG, H, hd)
        scale = 1.0 / np.sqrt(hd).astype(np.float32)
        scores = jnp.einsum('nqhd,nkhd->nhqk', q * scale, k)
        diag = jnp.eye(SEG, dtype=bool)
        scores = jnp.where(diag[None, None], jnp.finfo(scores.dtype).min, scores)
        attn = jax.nn.softmax(scores, axis=-1)
        o = jnp.einsum('nhqk,nkhd->nqhd', attn, v).reshape(a * b, SEG, d)
        o = o @ out_proj_w.T + out_proj_b
        out = o.reshape(a, b, SEG, d).transpose(1, 0, 2, 3).reshape(b, T, d)
        return out[:, :seq_len]

    def _L2_ffn_ref(input, Wg, W1, b1, W2, b2):
        import jax, jax.numpy as jnp
        import numpy as np
        E = 8
        D = 256
        H = 512
        TOP_K = 2
        logits = jnp.einsum('bsd,de->bse', input, Wg)
        probs = jax.nn.softmax(logits, axis=-1)
        top_vals, top_idx = jax.lax.top_k(probs, TOP_K)
        top_vals = top_vals / jnp.sum(top_vals, axis=-1, keepdims=True)
        onehot = jax.nn.one_hot(top_idx, E, dtype=input.dtype)
        mask = jnp.sum(onehot, axis=2)
        scores = jnp.sum(onehot * top_vals[..., None], axis=2)
        xm = input[None] * jnp.moveaxis(mask, -1, 0)[..., None]
        h = jnp.einsum('ebsd,edh->ebsh', xm, W1) + b1[:, None, None, :]
        h = jax.nn.relu(h)
        y = jnp.einsum('ebsh,ehd->ebsd', h, W2) + b2[:, None, None, :]
        out = jnp.sum(y * jnp.moveaxis(scores, -1, 0)[..., None], axis=0)
        return out

    def _L3_attn_ref(x, wq, bq, wk, bk, wv, bv, wo, bo):
        import jax, jax.numpy as jnp
        import numpy as np
        D_MODEL = 256
        QHEADS = 16
        KVHEADS = 4
        G = QHEADS // KVHEADS
        D_Q = D_MODEL // QHEADS
        D_KV = D_MODEL // QHEADS * KVHEADS
        BATCH, SEQ = (2, 512)

        def _xavier(key, shape):
            fan_out, fan_in = shape
            lim = (6.0 / (fan_in + fan_out)) ** 0.5
            return jax.random.uniform(key, shape, jnp.float32, -lim, lim)
        b, n, _ = x.shape
        scaling = D_Q ** (-0.5)
        q = (x @ wq.T + bq).reshape(b, n, QHEADS, D_Q).transpose(0, 2, 1, 3)
        k = (x @ wk.T + bk).reshape(b, n, KVHEADS, D_Q).transpose(0, 2, 1, 3)
        v = (x @ wv.T + bv).reshape(b, n, KVHEADS, D_Q).transpose(0, 2, 1, 3)
        q = q.reshape(b, KVHEADS, G, n, D_Q).transpose(0, 2, 1, 3, 4)
        attn = jnp.einsum('bghnd,bhsd->bghns', q, k) * scaling
        attn = jax.nn.softmax(attn, axis=-1)
        out = jnp.einsum('bghns,bhsd->bghnd', attn, v)
        out = out.transpose(0, 3, 2, 1, 4).reshape(b, n, D_MODEL)
        return out @ wo.T + bo

    def _L3_ffn_ref(x, W_fc, ln_w, ln_b, W_proj):
        import jax, jax.numpy as jnp
        import numpy as np
        EPS = 1e-06
        LN_EPS = 1e-05

        def _absmean_core(W):
            gamma = jnp.mean(jnp.abs(W)) + EPS
            Ws = W / gamma
            Wq = jnp.sign(Ws) * jnp.minimum(jnp.round(jnp.abs(Ws)), 1.0)
            return (Wq, gamma)

        @jax.custom_vjp
        def absmean(W):
            return _absmean_core(W)[0]

        def _absmean_fwd(W):
            Wq, gamma = _absmean_core(W)
            return (Wq, gamma)

        def _absmean_bwd(gamma, g):
            return (g / gamma,)
        absmean.defvjp(_absmean_fwd, _absmean_bwd)

        def layernorm(x, w, b, eps=LN_EPS):
            mu = jnp.mean(x, axis=-1, keepdims=True)
            var = jnp.mean((x - mu) ** 2, axis=-1, keepdims=True)
            return (x - mu) * jax.lax.rsqrt(var + eps) * w + b
        h = jnp.einsum('btd,hd->bth', x, absmean(W_fc))
        h = jax.nn.gelu(h, approximate=False)
        h = layernorm(h, ln_w, ln_b)
        return jnp.einsum('bth,dh->btd', h, absmean(W_proj))
    h = _L0_tok_ref(x, L0_tok_w_qkv, L0_tok_b_qkv, L0_tok_w_out, L0_tok_b_out)
    h = jnp.concatenate([jnp.broadcast_to(cls_tok, (h.shape[0], 1, h.shape[2])), h], axis=1)
    h = h + _L0_attn_ref(_layernorm(h, axis=-1), L0_attn_Wq, L0_attn_bq, L0_attn_Wk, L0_attn_bk, L0_attn_Wv, L0_attn_bv, L0_attn_Wo, L0_attn_bo)
    h = h + _L0_ffn_ref(_layernorm(h, axis=-1), L0_ffn_Wr, L0_ffn_Wg, L0_ffn_Wu, L0_ffn_Wd, L0_ffn_Sg, L0_ffn_Su, L0_ffn_Sd)
    h = h + _L1_attn_ref(_layernorm(h, axis=-1), L1_attn_qkv_w, L1_attn_proj_w, L1_attn_proj_b, L1_attn_slopes)
    h = h + _L1_ffn_ref(_layernorm(h, axis=-1), L1_ffn_input_ids, L1_ffn_gate_w, L1_ffn_gate_b, L1_ffn_w13, L1_ffn_w2, L1_ffn_w13_s, L1_ffn_w2_s)
    h = h + _L2_attn_ref(_layernorm(h, axis=-1), L2_attn_proj_qk_w, L2_attn_proj_qk_b, L2_attn_proj_v_w, L2_attn_proj_v_b, L2_attn_in_proj_w, L2_attn_in_proj_b, L2_attn_out_proj_w, L2_attn_out_proj_b)
    h = h + _L2_ffn_ref(_layernorm(h, axis=-1), L2_ffn_Wg, L2_ffn_W1, L2_ffn_b1, L2_ffn_W2, L2_ffn_b2)
    h = h + _L3_attn_ref(_layernorm(h, axis=-1), L3_attn_wq, L3_attn_bq, L3_attn_wk, L3_attn_bk, L3_attn_wv, L3_attn_bv, L3_attn_wo, L3_attn_bo)
    h = h + _L3_ffn_ref(_layernorm(h, axis=-1), L3_ffn_W_fc, L3_ffn_ln_w, L3_ffn_ln_b, L3_ffn_W_proj)
    return h

_drawn_inputs = setup_inputs


def setup_inputs(seed=0):
    import zlib

    import numpy as np

    out = dict(_drawn_inputs(seed))
    spreads = {'L0_tok_b_qkv': (0.0, 0.1),
     'L0_tok_b_out': (0.0, 0.1),
     'L2_ffn_b1': (0.0, 0.42),
     'L2_ffn_b2': (0.0, 0.1),
     'L3_attn_bq': (0.0, 0.8),
     'L3_attn_bk': (0.0, 2.0),
     'L3_attn_bv': (0.0, 0.1),
     'L3_attn_bo': (0.0, 0.1),
     'L3_ffn_ln_w': (1.0, 0.2),
     'L3_ffn_ln_b': (0.0, 0.1)}
    factors = {'cls_tok': 7.798,
     'L0_attn_Wq': 8.0,
     'L0_attn_bq': 8.0,
     'L0_attn_Wk': 3.396,
     'L0_attn_bk': 8.0,
     'L1_attn_proj_b': 3.933,
     'L1_attn_slopes': 4.345,
     'L1_ffn_gate_w': 3.888,
     'L1_ffn_gate_b': 8.0,
     'L1_ffn_w13': 3.772,
     'L1_ffn_w2': 3.695,
     'L1_ffn_w13_s': 6.029,
     'L1_ffn_w2_s': 4.407,
     'L2_attn_proj_qk_w': 64.0,
     'L2_attn_proj_qk_b': 200.0,
     'L2_attn_proj_v_b': 56.095,
     'L2_attn_in_proj_b': 7.817,
     'L2_attn_out_proj_b': 3.004,
     'L3_attn_wq': 3.038,
     'L3_attn_wk': 2.938,
     'L2_attn_proj_v_w': 3.765,
     'L2_attn_in_proj_w': 3.181}
    for name, (base, spread) in spreads.items():
        noise = np.random.default_rng([zlib.crc32(name.encode()), seed]).standard_normal(out[name].shape)
        drawn = base * np.exp(spread * noise) if base else spread * noise
        out[name] = jnp.asarray(drawn.astype(out[name].dtype))
    for name, factor in factors.items():
        out[name] = (out[name] * factor).astype(out[name].dtype)
    return out
```

```python
from contextlib import ExitStack

import numpy as np

import concourse.bass as bass
from concourse import mybir

F32 = mybir.dt.float32
BF16 = mybir.dt.bfloat16
U32 = mybir.dt.uint32
ALU = mybir.AluOpType
ACT = mybir.ActivationFunctionType
AX = mybir.AxisListType

P = 128
B = 4
S = 512
T = S + 1
D = 256
KB = D // P
TOK = B * T
TP = 114
NT = TOK // TP
CT = 3
CW = CT * TP
NCH = NT // CT
NH = 16
HD = D // NH
VW = 32
GH = 4
NG = NH // GH
NSLOT = 6
BIG = 3.0e38
LN_EPS = 1e-5
SLOTS_Q = (1, 1, 2, 2, 1, 3)
SLOTS_K = (1, 2, 1, 2, 3, 1)
NSTAGE_SEMS = 26

QCH = [(i * TP, min(TP, T - i * TP)) for i in range(-(-T // TP))]
HALF0 = T - 256
W0 = 512 - HALF0
HALVES = ((0, HALF0), (HALF0, 256))

SEG = 4
SH = 8
SHD = D // SH
TS = (T // SEG + 1) * SEG
SP = 86
NSEG = B * TS // SEG
NST = NSEG // SP
SW = SP * SEG


def build(nc, a, out, last_stage=99, from_step=None):
    ctx = ExitStack()
    with ctx:
        def sb(name, shape, dt=F32):
            return ctx.enter_context(nc.sbuf_tensor(name, shape, dt))

        def sem(name):
            return ctx.enter_context(nc.semaphore(name))

        H = sb("H", [TP, NT, D])
        XT = sb("XT", [P, KB, TOK])
        ATW = sb("ATW", [P, KB, 1792])
        ROWS = sb("ROWS", [P, 1040])
        COLS = sb("COLS", [P, 8])
        FW1 = sb("FW1", [P, KB, 4608])
        FW2 = sb("FW2", [P, 32, D])
        RW = sb("RW", [P, KB, 16])
        RB = sb("RB", [P, 16])
        B1 = sb("B1", [P, 32])
        B2 = sb("B2", [8, D])
        ident = sb("ident", [P, P])
        iota = sb("iota", [TP, CT, 16])
        eps = sb("eps", [P, 1])
        QSD = nc.dram_tensor("q_stacks", [KB, B, NSLOT, P, T], BF16, kind="Internal").ap()
        KSD = nc.dram_tensor("k_stacks", [KB, B, NSLOT, P, T], BF16, kind="Internal").ap()
        VD = nc.dram_tensor("v_rows", [KB, B, T, NH * VW // KB], F32, kind="Internal").ap()

        attn_loaded = [sem(f"attn_loaded{i}") for i in range(5)]
        ffn_loaded = [sem(f"ffn_loaded{i}") for i in range(4)]
        started = {}
        const_loaded = sem("const_loaded")
        out_stored = sem("out_stored")
        begun = sem("begun")
        pool_of_sems = [sem(f"stage_sem{i}") for i in range(NSTAGE_SEMS)]
        first, last = pool_of_sems[0].num, pool_of_sems[-1].num
        assert last - first == NSTAGE_SEMS - 1

        class Stage:

            number = 0

            def __init__(self):
                Stage.number += 1
                self.prefix = f"stage{Stage.number}_"
                self.taken = 0
                self.mem = ExitStack()

            def sem(self, name):
                self.taken += 1
                return pool_of_sems[self.taken - 1]

            def sb(self, name, shape, dt=F32):
                return self.mem.enter_context(nc.sbuf_tensor(self.prefix + name, shape, dt))

            def psum(self, name, shape, dt=F32):
                return self.mem.enter_context(nc.psum_tensor(self.prefix + name, shape, dt))

            def close(self):
                nc.all_engine_barrier(sems_to_clear=range(first, last + 1))
                self.mem.close()

        def cols_of(ap, t0, n):
            return ap[:, :, bass.ds(t0, n)]

        def load_attn(e, n, w, rows, cols):
            started[(attn_loaded[n],)] = 48
            e.dma_start(ATW[:, :, 0:w.shape[1]], w.rearrange("(k p) n -> p k n", p=P)).then_inc(attn_loaded[n], 16)
            e.dma_start(ROWS[:, 0:rows.shape[1]], rows).then_inc(attn_loaded[n], 16)
            e.dma_start(COLS[:, 0:cols.shape[1]], cols).then_inc(attn_loaded[n], 16)

        def load_ffn(e, n, w1, w2, rw=None, rb=None, b1=None, b2=None):
            s = ffn_loaded[n]
            started[(s,)] = load_counts(a, f"L{n}")
            c = 0
            w1v = w1.rearrange("(k p) n -> p k n", p=P)
            w2v = w2.rearrange("(c p) n -> p c n", p=P)
            for k in range(KB):
                e.dma_start(FW1[:, k, 0:w1.shape[1]], w1v[:, k]).then_inc(s, 16)
                c += 16
            e.dma_start(FW2[:, 0:w2v.shape[1], :], w2v).then_inc(s, 16)
            c += 16
            if rw is not None:
                e.dma_start(RW[:, :, 0:rw.shape[1]], rw.rearrange("(k p) n -> p k n", p=P)).then_inc(s, 16)
                c += 16
            if rb is not None:
                e.dma_start(RB[:, 0:rb.shape[1]], rb).then_inc(s, 16)
                c += 16
            if b1 is not None:
                e.dma_start(B1[:, :], b1).then_inc(s, 16)
                e.dma_start(B2[:, :], b2).then_inc(s, 16)
                c += 32
            return c

        class Norm:

            def __init__(self, st, n=CT, signals=1):
                self.n, self.signals = n, signals
                self.stats = st.sb("ln_stats", [TP, n, 6])
                self.mv = st.sb("ln_mv", [TP, n, 2])
                self.sd = st.sb("ln_sd", [TP, n])
                self.rstd = st.sb("ln_rstd", [TP, n])
                self.xn = st.sb("ln_xn", [TP, n, D])
                self.var_ready = st.sem("var_ready")
                self.sd_ready = st.sem("sd_ready")
                self.xn_ready = st.sem("xn_ready")
                self.tr_ready = st.sem("tr_ready")
                self.step = st.sem("ln_step")

            def vector(self, e, k):
                for j in range(self.n):
                    i = e.bn_stats(self.stats[:, j, :], H[:, self.n * k + j, :])
                i.then_inc(self.step, 1)
                e.wait_ge(self.step, k * 2 + 1)
                e.sem_inc(begun, 1)
                for j in range(self.n):
                    i = e.bn_aggr(self.mv[:, j, :], self.stats[:, j, :])
                i.then_inc(self.var_ready, 1)
                e.wait_ge(self.sd_ready, k + 1)
                e.reciprocal(self.rstd[:, :], self.sd[:, :]).then_inc(self.step, 1)
                e.wait_ge(self.step, k * 2 + 2)
                e.wait_ge(self.tr_ready, self.signals * k + 1)
                for j in range(self.n):
                    i = e.tensor_scalar(self.xn[:, j, :], H[:, self.n * k + j, :], self.mv[:, j, 0:1],
                                        self.rstd[:, j:j + 1], ALU.subtract, ALU.mult)
                i.then_inc(self.xn_ready, 1)

            def scalar(self, e, k):
                e.wait_ge(self.var_ready, k + 1)
                e.activation(self.sd[:, :], self.mv[:, :, 1], ACT.Sqrt, bias=eps[0:TP, :]).then_inc(self.sd_ready, 1)

        def stage_norm():
            st = Stage()
            ln = Norm(st)
            ps = [st.psum(f"tr{r}", [P, KB, 512]) for r in range(2)]
            tr_used = st.sem("tr_used")
            with nc.Block() as block:
                @block.vector
                def _(e):
                    with e.Fori(0, NCH // 2) as i:
                        for r in range(2):
                            ln.vector(e, 2 * i + r)

                @block.scalar
                def _(e):
                    e.sem_inc(tr_used, 2)
                    with e.Fori(0, NCH // 2) as i:
                        for r in range(2):
                            k = 2 * i + r
                            ln.scalar(e, k)
                            e.wait_ge(ln.tr_ready, 1 + k + 1)
                            e.activation(cols_of(XT, k * CW, CW), ps[r][:, :, 0:CW], ACT.Copy).then_inc(tr_used, 1)

                @block.tensor
                def _(e):
                    e.sem_inc(ln.tr_ready, 1)
                    with e.Fori(0, NCH // 2) as i:
                        for r in range(2):
                            k = 2 * i + r
                            e.wait_ge(ln.xn_ready, k + 1)
                            e.wait_ge(tr_used, k + 1)
                            for kb in range(KB):
                                for j in range(CT):
                                    t = e.transpose(ps[r][:, kb, TP * j:TP * j + TP],
                                                    ln.xn[:, j, kb * P:kb * P + P], ident[0:TP, 0:TP])
                            t.then_inc(ln.tr_ready, 1)
            st.close()

        def stage_project(wcol, bcol, first_layer, prefetch):
            st = Stage()
            xs = [st.sb(f"xs{r}", [P, KB, TP]) for r in range(2)]
            tmp = [st.sb(f"tmp{r}", [TP, D]) for r in range(2)]
            ps = [st.psum(f"o{r}", [TP, 512]) for r in range(2)]
            xs_ready = st.sem("xs_ready")
            o_ready = st.sem("o_ready")
            o_used = st.sem("o_used")
            t_used = st.sem("t_used")
            with nc.Block() as block:
                @block.scalar
                def _(e):
                    with e.Fori(0, NT // 2) as i:
                        for r in range(2):
                            t = 2 * i + r
                            e.wait_ge(o_ready, t + 1)
                            e.activation(xs[r][:, :, :], cols_of(XT, t * TP, TP), ACT.Copy).then_inc(xs_ready, 1)

                @block.tensor
                def _(e):
                    e.sem_inc(o_ready, 2)
                    with e.Fori(0, NT // 2) as i:
                        for r in range(2):
                            t = 2 * i + r
                            e.wait_ge(xs_ready, t + 1)
                            e.wait_ge(o_used, t + 1)
                            for kb in range(KB):
                                m = e.matmul(ps[r][:, 0:D], xs[r][:, kb, :], ATW[:, kb, wcol:wcol + D],
                                             start=kb == 0, stop=kb == KB - 1)
                            m.then_inc(o_ready, 1)

                @block.vector
                def _(e):
                    e.sem_inc(o_used, 2)
                    with e.Fori(0, NT // 2) as i:
                        for r in range(2):
                            t = 2 * i + r
                            e.wait_ge(o_ready, 2 + t + 1)
                            if first_layer:
                                e.tensor_tensor(H[:, t, :], ps[r][:, 0:D], ROWS[0:TP, bcol:bcol + D], ALU.add)\
                                    .then_inc(o_used, 1)
                            else:
                                e.wait_ge(t_used, t + 1)
                                e.tensor_tensor(tmp[r][:, :], ps[r][:, 0:D], ROWS[0:TP, bcol:bcol + D], ALU.add)\
                                    .then_inc(o_used, 1)

                @block.gpsimd
                def _(e):
                    if not first_layer:
                        e.sem_inc(t_used, 2)
                        with e.Fori(0, NT // 2) as i:
                            for r in range(2):
                                t = 2 * i + r
                                e.wait_ge(o_used, 2 + t + 1)
                                e.tensor_tensor(H[:, t, :], H[:, t, :], tmp[r][:, :], ALU.add).then_inc(t_used, 1)
            st.close()
            if first_layer:
                st = Stage()
                cls_in = st.sem("cls_in")
                with nc.Block() as block:
                    @block.sync
                    def _(e):
                        for b in range(B):
                            p, t = (b * T) % TP, (b * T) // TP
                            e.dma_start(H[p:p + 1, t, :], a["cls"]).then_inc(cls_in, 16)
                        e.wait_ge(cls_in, 16 * B)
                        prefetch(e)
                st.close()
            else:
                with nc.Block() as block:
                    @block.sync
                    def _(e):
                        prefetch(e)

        def stage_qkv(layer, rope):
            st = Stage()
            cos = st.sb("cos", [P, T]) if rope else None
            sin = st.sb("sin", [P, T]) if rope else None
            xf = [st.sb(f"xf{r}", [P, T]) for r in range(2)]
            rot = [st.sb(f"rot{r}", [P, T]) for r in range(2)] if rope else None
            rest = [st.sb(f"rest{r}", [P, T]) for r in range(2)]
            parts = [[st.sb(f"part{n}_{r}", [P, KB, T], BF16) for n in range(3)] for r in range(2)]
            xb = st.sb("xb", [P, KB, T])
            vs = [st.sb(f"vs{c}", [TP, NH * VW]) for c in range(len(QCH))]
            pq = [st.psum(f"pq{r}", [P, 1024]) for r in range(2)]
            pr = st.psum("pr", [P, 1024])
            pv = [st.psum(f"pv{r}", [TP, 512]) for r in range(2)]
            tab_in = st.sem("tab_in")
            q_ready = st.sem("q_ready")
            r_ready = st.sem("r_ready")
            q_used = st.sem("q_used")
            r_used = st.sem("r_used")
            x_ready = st.sem("x_ready")
            p1_ready = st.sem("p1_ready")
            r1_ready = st.sem("r1_ready")
            p2_ready = st.sem("p2_ready")
            p3_ready = st.sem("p3_ready")
            half = [st.sem(f"stack_out{r}") for r in range(2)]
            xb_ready = st.sem("xb_ready")
            xb_used = st.sem("xb_used")
            v_ready = st.sem("v_ready")
            v_used = st.sem("v_used")
            v_out = st.sem("v_out")
            NV = len(QCH)
            SLOT_DMA = 16 * NSLOT
            ORDER = [("qk", 0), ("qk", 1), ("v", 0), ("qk", 2), ("v", 1), ("qk", 3)] + [("v", c) for c in range(2, NV)]

            with nc.Block() as block:
                @block.tensor
                def _(e):
                    e.wait_ge(attn_loaded[layer], 48)
                    e.sem_inc(xb_used, 1)
                    with e.Fori(0, B) as b:
                        for what, n in ORDER:
                            if what == "v":
                                q0, qn = QCH[n]
                                if n == 0:
                                    e.wait_ge(xb_ready, b + 1)
                                e.wait_ge(v_used, (NV + 1) * b + n + 1)
                                for kb in range(KB):
                                    m = e.matmul(pv[n % 2][0:qn, :], xb[:, kb, q0:q0 + qn], ATW[:, kb, 512:1024],
                                                 start=kb == 0, stop=kb == KB - 1)
                                m.then_inc(v_ready, 1)
                                continue
                            r = n % 2
                            e.wait_ge(q_used, 4 * b + n + 1)
                            for h0, hw in HALVES:
                                for kb in range(KB):
                                    m = e.matmul(pq[r][:, W0 + h0:W0 + h0 + hw], ATW[:, kb, n * P:n * P + P],
                                                 XT[:, kb, bass.ds(b * T + h0, hw)],
                                                 start=kb == 0, stop=kb == KB - 1)
                            m.then_inc(q_ready, 1)
                            if rope:
                                e.wait_ge(r_used, 4 * b + n + 1)
                                for h0, hw in HALVES:
                                    for kb in range(KB):
                                        m = e.matmul(pr[:, W0 + h0:W0 + h0 + hw],
                                                     ATW[:, kb, 1280 + n * P:1280 + n * P + P],
                                                     XT[:, kb, bass.ds(b * T + h0, hw)],
                                                     start=kb == 0, stop=kb == KB - 1)
                                m.then_inc(r_ready, 1)
                        e.wait_ge(v_ready, (NV + 1) * b + NV)
                        e.sem_inc(v_ready, 1)
                        e.sem_inc(xb_used, 1)

                @block.gpsimd
                def _(e):
                    with e.Fori(0, B) as b:
                        e.wait_ge(xb_used, b + 1)
                        e.tensor_copy(xb[:, :, :], cols_of(XT, b * T, T)).then_inc(xb_ready, 1)

                @block.scalar
                def _(e):
                    e.wait_ge(attn_loaded[layer], 48)
                    if not rope:
                        e.sem_inc(q_used, 2)
                    with e.Fori(0, B) as b:
                        for n in range(4):
                            r, m, qk = n % 2, n % 2, n // 2
                            u = 4 * b + n
                            if rope:
                                e.wait_ge(x_ready, u + 1)
                            else:
                                e.wait_ge(q_ready, u + 1)
                                e.wait_ge(p3_ready, u + 1)
                                e.activation(xf[r][:, :], pq[r][:, W0:W0 + T], ACT.Identity,
                                             bias=COLS[:, n:n + 1]).then_inc(q_used, 1)
                                e.wait_ge(q_used, 2 + u + 1)
                            if m == 0:
                                e.wait_ge(half[qk], SLOT_DMA * b + 1)
                            e.activation(parts[qk][0][:, m, :], xf[r][:, :], ACT.Copy).then_inc(p1_ready, 1)
                            e.wait_ge(r1_ready, u + 1)
                            e.activation(parts[qk][1][:, m, :], rest[r][:, :], ACT.Copy).then_inc(p2_ready, 1)

                @block.vector
                def _(e):
                    e.sem_inc(v_used, 2)
                    e.sem_inc(p3_ready, 2)
                    e.wait_ge(attn_loaded[layer], 48)
                    if rope:
                        e.sem_inc(q_used, 2)
                        e.sem_inc(r_used, 1)
                        e.wait_ge(tab_in, 32)
                    with e.Fori(0, B) as b:
                        for what, n in ORDER:
                            if what == "v":
                                q0, qn = QCH[n]
                                e.wait_ge(v_ready, (NV + 1) * b + n + 1)
                                if n == 0:
                                    e.wait_ge(v_out, 16 * NV * b + 1)
                                e.tensor_tensor(vs[n][0:qn, :], pv[n % 2][0:qn, :], ROWS[0:qn, 0:512], ALU.add)\
                                    .then_inc(v_used, 1)
                                continue
                            r, m, qk = n % 2, n % 2, n // 2
                            u = 4 * b + n
                            if rope:
                                e.wait_ge(q_ready, u + 1)
                                e.tensor_tensor(xf[r][:, :], pq[r][:, W0:W0 + T], cos[:, :], ALU.mult)\
                                    .then_inc(q_used, 1)
                                e.wait_ge(r_ready, u + 1)
                                e.tensor_tensor(rot[r][:, :], pr[:, W0:W0 + T], sin[:, :], ALU.mult)\
                                    .then_inc(r_used, 1)
                                e.wait_ge(q_used, 2 + u + 1)
                                e.wait_ge(r_used, 1 + u + 1)
                                e.tensor_tensor(xf[r][:, :], xf[r][:, :], rot[r][:, :], ALU.add).then_inc(x_ready, 1)
                                e.wait_ge(x_ready, u + 1)
                            e.wait_ge(p1_ready, u + 1)
                            e.tensor_tensor(rest[r][:, :], xf[r][:, :], parts[qk][0][:, m, :], ALU.subtract)\
                                .then_inc(r1_ready, 1)
                            e.wait_ge(p2_ready, u + 1)
                            e.wait_ge(r1_ready, u + 1)
                            if m == 0:
                                e.wait_ge(half[qk], SLOT_DMA * b + 1)
                            e.tensor_tensor(parts[qk][2][:, m, :], rest[r][:, :], parts[qk][1][:, m, :], ALU.subtract)\
                                .then_inc(p3_ready, 1)
                        e.wait_ge(v_used, 2 + (NV + 1) * b + NV)
                        e.wait_ge(v_ready, (NV + 1) * (b + 1))
                        e.sem_inc(v_used, 1)

                @block.sync
                def _(e):
                    if rope:
                        e.dma_start(cos[:, :], a["cos"]).then_inc(tab_in, 16)
                        e.dma_start(sin[:, :], a["sin"]).then_inc(tab_in, 16)
                    for r in range(2):
                        e.sem_inc(half[r], 1)
                    e.sem_inc(v_out, 1)
                    with e.Fori(0, B) as b:
                        def stack_out(qk):
                            dst, slots = ((QSD, SLOTS_Q), (KSD, SLOTS_K))[qk]
                            e.wait_ge(p3_ready, 2 + 4 * b + 2 * qk + 2)
                            e.sem_inc(begun, 1)
                            e.wait_ge(p2_ready, 4 * b + 2 * qk + 2)
                            e.wait_ge(p1_ready, 4 * b + 2 * qk + 2)
                            for s in range(NSLOT):
                                e.dma_start(dst[:, :, s].rearrange("m b p t -> b p m t")[b],
                                            parts[qk][slots[s] - 1][:, :, :]).then_inc(half[qk], 16)

                        for what, n in ORDER:
                            if what == "qk" and n % 2:
                                stack_out(n // 2)
                            if what == "v":
                                q0, qn = QCH[n]
                                e.wait_ge(v_used, 2 + (NV + 1) * b + n + 1)
                                e.dma_start(VD.rearrange("m b t c -> b t m c")[b, q0:q0 + qn],
                                            vs[n][0:qn, :].rearrange("p (m c) -> p m c", m=KB)).then_inc(v_out, 16)
                    for r in range(2):
                        e.wait_ge(half[r], B * SLOT_DMA + 1)
                    e.wait_ge(v_out, B * 16 * NV + 1)
            st.close()

        def stage_attn(k0, alibi):
            st = Stage()
            NU = B * NG
            nk = T - k0
            KCH = [(c, min(P if k0 else TP, T - c)) for c in range(k0, T, P if k0 else TP)]
            NC = len(KCH)
            N2 = NC * GH
            KHALF = ((1, 512),) if k0 else HALVES
            KHN = len(KHALF)
            NP1 = len(QCH) * GH
            N1 = NP1 * KHN + 2
            NE = 8
            R0 = NSLOT * HD
            R1 = P
            RA = R1 - R0
            RP = R1 - 2 * GH
            PA = RA // GH - 2
            MT = ((0, 2), (2, len(QCH)))
            tiles1 = [(i, j) for j in range(GH) for i in range(len(QCH))]

            QS = [st.sb(f"QS{r}", [P, GH, T], BF16) for r in range(2)]
            KS = [st.sb(f"KS{r}", [P, GH, T], BF16) for r in range(2)]
            VG = [st.sb(f"VG{r}", [P, len(KCH), GH * VW]) for r in range(2)]
            E = [st.sb(f"E{n}", [P, T]) for n in range(NE)]
            OU = st.sb("OU", [P, T])
            ON = st.sb("ON", [TP, len(QCH), GH, HD])
            rec = st.sb("rec", [TP, len(QCH), GH])
            mx = st.sb("mx", [TP, len(QCH), GH, KHN])
            M = st.sb("M", [TP, len(QCH), RA // GH, GH])
            m1 = st.sb("m1", [TP, len(QCH), GH], BF16)
            hot = st.sb("hot", [P, GH, 1])
            slot = [st.psum(f"slot{r}", [P, 512]) for r in range(2)]
            S2 = [st.psum(f"S2_{r}", [P, 1024]) for r in range(2)]
            AV = st.psum("AV", [P, 1024])
            if alibi:
                D1 = st.sb("D1", [TP, 2 * T - (T - QCH[-1][0])])
                D2 = st.sb("D2", [TP, 2 * T - (T - QCH[-1][0])])
                slopes = st.sb("slopes", [P, NU * GH])
                slopes4 = st.sb("slopes4", [P, NU * GH])
                SL = [st.sb(f"SL{r}", [P, GH]) for r in range(2)]
                G1 = st.sb("G1", [TP, GH, 2 * T - (T - QCH[-1][0])])
                scr = [st.sb(f"scr{r}", [TP, HALF0]) for r in range(2)]
            C0 = QCH[-1][0]

            loaded = [st.sem(f"loaded{r}") for r in range(2)]
            v_loaded = [st.sem(f"v_loaded{r}") for r in range(2)]
            slot_ready = st.sem("slot_ready")
            slot_used = st.sem("slot_used")
            s2_ready = st.sem("s2_ready")
            e_ready = st.sem("e_ready")
            e_used = st.sem("e_used")
            ou_ready = st.sem("ou_ready")
            on_ready = st.sem("on_ready")
            m_ready = st.sem("m_ready")
            hot_ready = st.sem("hot_ready")
            own = st.sem("own")
            own_o = st.sem("own_o")
            if alibi:
                g_ready = st.sem("g_ready")
                g_used = st.sem("g_used")
                sa_ready = st.sem("sa_ready")
                pool_own = st.sem("pool_own")
                tables_in = st.sem("tables_in")

            def slots_before(u, mid):
                if mid:
                    return u * (N1 + 4) + (N1 - 4)
                return {-1: 0, 0: N1}.get(u, NU * N1 + (u - 1) * 4)

            def steps(e, step):
                step(-1, 1, -1, slots_before(-1, False), True, False, False)
                step(0, 0, 0, slots_before(0, False), True, True, False)
                with e.Fori(0, (NU - 2) // 2) as i:
                    step(2 * i + 1, 1, i, slots_before(2 * i + 1, True), True, True, True)
                    step(2 * i + 2, 0, i + 1, slots_before(2 * i + 2, True), True, True, True)
                step(NU - 1, 1, NU // 2 - 1, slots_before(NU - 1, False), False, True, True)
                step(NU, 0, NU // 2, slots_before(NU, False), False, False, True)

            P0, P1 = 3, N2 - 2

            def plan(do1, do2, do3):
                out, n1 = [], 0
                def pass1(until):
                    nonlocal n1
                    while do1 and n1 < NP1 * KHN and n1 * (P1 - P0) < NP1 * KHN * (until - P0):
                        out.append(("p1",) + tiles1[n1 // KHN] + (n1 % KHN,))
                        n1 += 1

                for s in range(N2):
                    pass1(s + 0.5)
                    if do1 and s == P1:
                        out.append(("mm",))
                    if do1 and s == P1 + 1:
                        out.append(("mt",))
                    if s == 0 and do3:
                        out.append(("av_last",))
                    if do2:
                        out.append(("s2", s // GH, s % GH))
                    pass1(s + 1)
                    if s % GH in (1, 2) and s > GH and do2:
                        out.append(("av", s // GH - 1, s % GH - 1))
                    if s == 1 and do3:
                        out.append(("o1",))
                    if s == GH and do3:
                        out.append(("o2",))
                return out

            def maxima_rows(copy, r, ps, i0, i1):
                q0, q1 = QCH[i0][0], sum(QCH[i1 - 1])
                return copy(QS[r][R0:R1, :, q0:q1], ps[0:RA, 0:q1 - q0].rearrange("p (o t) -> p o t", o=1)
                            .to_broadcast([RA, GH, q1 - q0]))

            with nc.Block() as block:
                @block.sync
                def _(e):
                    e.dma_start(hot[R0:R1, :, :], a["hot"]).then_inc(hot_ready, 16)
                    if alibi:
                        e.dma_start(D1[:, :], a["alibi_q"]).then_inc(tables_in, 16)
                        e.dma_start(D2[:, :], a["alibi_k"]).then_inc(tables_in, 16)
                        e.dma_start(slopes[:, :], a["slopes"]).then_inc(tables_in, 16)
                    def load(i, r, again):
                        if again:
                            e.wait_ge(s2_ready, (2 * i + r - 1) * N2)
                        for dst, src in ((QS, QSD), (KS, KSD)):
                            e.dma_start(dst[r][0:R0, :, :], src.rearrange(
                                "m b s (d g j) t -> (m b) (s d) g j t", d=HD, j=GH)[i, :, r]).then_inc(loaded[r], 16)
                        if again:
                            e.wait_ge(ou_ready, 2 * i + r + 1)
                        v = VD.rearrange("m b t c -> (m b) t c")
                        c0, cn = KCH[0][0], KCH[0][1]
                        full = sum(n == cn for _, n in KCH)
                        e.dma_start(VG[r][0:cn, 0:full, :],
                                    v[i, c0:c0 + full * cn, r * P:r * P + P].rearrange("(c t) f -> t c f", t=cn))\
                            .then_inc(v_loaded[r], 16)
                        if full < NC:
                            c0, cn = KCH[-1]
                            e.dma_start(VG[r][0:cn, NC - 1, :], v[i, c0:c0 + cn, r * P:r * P + P])\
                                .then_inc(v_loaded[r], 16)

                    load(0, 0, False)
                    load(0, 1, False)
                    with e.Fori(1, NU // 2) as i:
                        load(i, 0, True)
                        load(i, 1, True)

                LD = 32
                VLD = 32 if KCH[-1][1] != KCH[0][1] else 16

                @block.tensor
                def _(e):
                    e.sem_inc(e_used, 2)
                    e.wait_ge(own, 2)

                    def step(u, r, pair, n0, do1, do2, do3):
                        n = 0
                        r1 = 1 - r
                        pair1 = pair + (1 if r else 0)

                        def next_slot():
                            nonlocal n
                            e.wait_ge(slot_used, n0 + n + 1)
                            n += 1
                            return slot[(n - 1) % 2]

                        def values(u, r, c, h):
                            c0, cn = KCH[c]
                            if h == 0:
                                e.wait_ge(e_ready, 2 + u * N2 + c * GH + GH)
                                if c == 0:
                                    e.wait_ge(ou_ready, u + 2)
                                e.sem_inc(begun, 1)
                            for h0, hw in HALVES[h:h + 1]:
                                for j in range(GH):
                                    m = e.matmul(AV[VW * j:VW * j + VW, W0 + h0:W0 + h0 + hw],
                                                 VG[r][0:cn, c, VW * j:VW * j + VW],
                                                 E[(r * N2 + c * GH + j) % NE][0:cn, h0:h0 + hw],
                                                 start=c == 0, stop=c == NC - 1)
                            if h == 1:
                                m.then_inc(e_used, 1)

                        for what, *x in plan(do1, do2, do3):
                            if what == "p1":
                                i, j, h = x
                                q0, qn = QCH[i]
                                if i == j == h == 0:
                                    e.wait_ge(loaded[r1], LD * (pair1 + 1))
                                for h0, hw in KHALF[h:h + 1]:
                                    ps = next_slot()
                                    e.matmul(ps[0:qn, 0:hw], QS[r1][0:RP, j, q0:q0 + qn],
                                             KS[r1][0:RP, j, h0:h0 + hw], start=True, stop=True).then_inc(slot_ready, 1)
                            if what == "mt":
                                e.wait_ge(m_ready, u + 2)
                                for i0, i1 in MT:
                                    ps = next_slot()
                                    e.sem_inc(begun, 1)
                                    for i in range(i0, i1):
                                        q0, qn = QCH[i]
                                        m = e.transpose(ps[0:RA, TP * (i - i0):TP * (i - i0) + qn],
                                                        M[0:qn, i, :, :].rearrange("p a b -> p (a b)"), ident[0:qn, 0:qn])
                                    m.then_inc(slot_ready, 1)
                            if what == "o1":
                                e.wait_ge(ou_ready, 2 + u)
                                ps = next_slot()
                                for i in range(len(QCH) - 1):
                                    m = e.transpose(ps[0:TP, P * i:P * i + P], OU[:, TP * i:TP * i + TP], ident[:, :])
                                m.then_inc(slot_ready, 1)
                                q0, qn = QCH[-1]
                                ps = next_slot()
                                e.sem_inc(begun, 1)
                                e.transpose(ps[0:qn, 0:P], OU[:, q0:q0 + qn], ident[:, :]).then_inc(slot_ready, 1)
                            if what == "o2":
                                e.wait_ge(on_ready, 1 + u)
                                ps = next_slot()
                                e.sem_inc(begun, 1)
                                for i in range(len(QCH) - 1):
                                    m = e.transpose(ps[0:GH * HD, TP * i:TP * i + TP],
                                                    ON[:, i, :, :].rearrange("p a b -> p (a b)"), ident[0:TP, 0:TP])
                                m.then_inc(slot_ready, 1)
                                q0, qn = QCH[-1]
                                ps = next_slot()
                                e.sem_inc(begun, 1)
                                e.transpose(ps[0:GH * HD, 0:qn],
                                            ON[0:qn, len(QCH) - 1, :, :].rearrange("p a b -> p (a b)"),
                                            ident[0:qn, 0:qn]).then_inc(slot_ready, 1)
                            if what == "s2":
                                c, j = x
                                c0, cn = KCH[c]
                                s = c * GH + j
                                if s == 0:
                                    e.wait_ge(slot_used, 2 + n0)
                                    e.wait_ge(v_loaded[r], VLD * (pair + 1))
                                e.wait_ge(e_ready, u * N2 + s + 1)
                                for h0, hw in HALVES:
                                    m = e.matmul(S2[s % 2][0:cn, W0 + h0:W0 + h0 + hw], KS[r][0:R1, j, c0:c0 + cn],
                                                 QS[r][0:R1, j, h0:h0 + hw], start=True, stop=True)
                                m.then_inc(s2_ready, 1)
                            if what == "av":
                                values(u, r, x[0], x[1])
                            if what == "av_last":
                                values(u - 1, r1, NC - 1, 0)
                                values(u - 1, r1, NC - 1, 1)
                    steps(e, step)

                @block.vector
                def _(e):
                    e.memset(M[:, :, :, :], 0.0)
                    e.memset(mx[:, :, :, :], 0.0)
                    e.sem_inc(slot_used, 2)
                    e.wait_ge(hot_ready, 16)
                    e.sem_inc(on_ready, 1)
                    for r in range(2):
                        e.memset(QS[r][R0:R1, :, :], 0.0)
                        e.tensor_copy(KS[r][R0:R1, :, :], hot[R0:R1, :, :].to_broadcast([RA, GH, T])).then_inc(own, 1)
                    if alibi:
                        e.wait_ge(tables_in, 48)
                        e.sem_inc(g_used, 1)

                    def step(u, r, pair, n0, do1, do2, do3):
                        n = 0

                        def next_slot():
                            nonlocal n
                            e.wait_ge(slot_ready, n0 + n + 1)
                            n += 1
                            return slot[(n - 1) % 2]

                        for what, *x in plan(do1, do2, do3):
                            if what == "p1":
                                i, j, h = x
                                q0, qn = QCH[i]
                                if alibi and i == h == 0:
                                    if j:
                                        e.wait_ge(slot_used, 2 + n0 + n)
                                        e.sem_inc(g_used, 1)
                                    e.wait_ge(g_ready, GH * (u + 1) + j + 1)
                                for h0, hw in KHALF[h:h + 1]:
                                    ps = next_slot()
                                    if alibi:
                                        e.wait_ge(slot_used, n0 + n)
                                        e.sem_inc(begun, 1)
                                        e.tensor_tensor_reduce(scr[n % 2][0:qn, 0:hw], ps[0:qn, 0:hw],
                                                               G1[0:qn, j, C0 - q0 + h0:C0 - q0 + h0 + hw], 1.0, -BIG,
                                                               ALU.add, ALU.max, mx[0:qn, i, j, h:h + 1]).then_inc(slot_used, 1)
                                    else:
                                        e.tensor_reduce(mx[0:qn, i, j, h:h + 1], ps[0:qn, 0:hw], AX.X, ALU.max)\
                                            .then_inc(slot_used, 1)
                            if what == "mm":
                                e.wait_ge(slot_used, 2 + n0 + n)
                                e.tensor_reduce(M[:, :, PA, :], mx[:, :, :, :], AX.X, ALU.max, negate=True).then_inc(own, 1)
                                e.wait_ge(own, 2 + 2 * (u + 1) + 1)
                                e.tensor_copy(m1[:, :, :], M[:, :, PA, :]).then_inc(own, 1)
                                e.wait_ge(own, 2 + 2 * (u + 1) + 2)
                                e.tensor_tensor(M[:, :, PA + 1, :], M[:, :, PA, :], m1[:, :, :], ALU.subtract)\
                                    .then_inc(m_ready, 1)
                                if alibi:
                                    e.sem_inc(g_used, 1)
                            if what == "mt":
                                ps = next_slot()
                                maxima_rows(e.tensor_copy, 1 - r, ps, *MT[0]).then_inc(slot_used, 1)
                                n += 1
                            if what == "o1":
                                last = len(QCH) - 1
                                for k, (i0, i1, qn) in enumerate(((0, last, TP), (last, last + 1, QCH[-1][1]))):
                                    ps = next_slot()
                                    v = ps[0:qn, 0:P * (i1 - i0)].rearrange("p (i j c) -> p i j c", i=i1 - i0, j=GH)
                                    e.reciprocal(rec[0:qn, i0:i1, :], v[:, :, :, HD]).then_inc(own_o, 1)
                                    e.wait_ge(own_o, 2 * (u - 1) + k + 1)
                                    rb = rec[0:qn, i0:i1, :].rearrange("p i (j o) -> p i j o", o=1)
                                    e.tensor_tensor(ON[0:qn, i0:i1, :, :].rearrange("p i j c -> p (i j) c"),
                                                    v[:, :, :, 0:HD].rearrange("p i j c -> p (i j) c"),
                                                    rb.rearrange("p i j o -> p (i j) o").to_broadcast([qn, (i1 - i0) * GH, HD]),
                                                    ALU.mult).then_inc(slot_used, 1)
                                e.wait_ge(slot_used, 2 + n0 + n)
                                e.sem_inc(on_ready, 1)
                            if what == "o2":
                                rr = 1 - r
                                flat = XT[:, :, :].rearrange("p k t -> p (k t)")
                                base = (pair - (1 if r == 0 else 0)) * T
                                for i0, i1 in ((0, C0), (C0, T)):
                                    ps = next_slot()
                                    e.tensor_copy(flat[64 * rr:64 * rr + 64, bass.ds(base + i0, i1 - i0)],
                                                  ps[0:64, 0:i1 - i0]).then_inc(slot_used, 1)
                            if what == "s2" and alibi:
                                c, j = x
                                c0, cn = KCH[c]
                                s = c * GH + j
                                e.wait_ge(s2_ready, u * N2 + s + 1)
                                if c == j == 0:
                                    e.wait_ge(g_ready, GH * u + 1)
                                v = S2[s % 2][0:cn, W0 + c0:W0 + T]
                                e.scalar_tensor_tensor(out=v, in0=D2[0:cn, C0:C0 + T - c0],
                                                       scalar=SL[r][0:cn, j:j + 1], in1=v,
                                                       op0=ALU.mult, op1=ALU.add).then_inc(sa_ready, 1)
                    steps(e, step)

                @block.scalar
                def _(e):
                    e.sem_inc(e_ready, 2)
                    e.sem_inc(ou_ready, 2)

                    def step(u, r, pair, n0, do1, do2, do3):
                        for c in range(NC):
                            c0, cn = KCH[c]
                            if c == 0 and do3:
                                e.wait_ge(e_used, 2 + u * NC)
                                e.wait_ge(on_ready, u)
                                e.activation(OU[:, :], AV[:, W0:W0 + T], ACT.Copy).then_inc(ou_ready, 1)
                            if not do2:
                                continue
                            e.wait_ge(e_used, u * NC + c + 1)
                            for j in range(GH):
                                s = c * GH + j
                                e.wait_ge(sa_ready if alibi else s2_ready, u * N2 + s + 1)
                                e.activation(E[(r * N2 + s) % NE][0:cn, :], S2[s % 2][0:cn, W0:W0 + T], ACT.Exp,
                                             scale=HD ** -0.5).then_inc(e_ready, 1)
                        if do1:
                            e.wait_ge(slot_ready, n0 + N1 + (4 if do3 else 0))
                            maxima_rows(lambda out, x: e.activation(out, x, ACT.Copy), 1 - r, slot[1], *MT[1]).then_inc(slot_used, 1)
                    steps(e, step)

                @block.gpsimd
                def _(e):
                    if alibi:
                        e.wait_ge(tables_in, 48)
                        e.tensor_scalar(slopes4[:, :], slopes[:, :], 8.0 * HD ** 0.5, None, ALU.mult).then_inc(pool_own, 1)
                        e.wait_ge(pool_own, 1)

                    def step(u, r, pair, n0, do1, do2, do3):
                        if not (do1 and alibi):
                            return
                        r1 = 1 - r
                        if do3:
                            e.wait_ge(e_ready, u * N2 + 2)
                            e.wait_ge(g_ready, GH * (u + 1))
                        elif do2:
                            e.wait_ge(g_ready, GH)
                        e.sem_inc(begun, 1)
                        e.tensor_copy(SL[r1][:, :], slopes4[:, bass.ds(GH * (u + 1), GH)]).then_inc(pool_own, 1)
                        e.wait_ge(pool_own, 1 + u + 2)
                        for j in range(GH):
                            e.wait_ge(g_used, GH * u + j + 2 if do2 else 1)
                            if j:
                                e.wait_ge(g_ready, GH * (u + 1) + j)
                            e.sem_inc(begun, 1)
                            e.tensor_scalar(G1[:, j, :], D1[:, :], SL[r1][0:TP, j:j + 1], None, ALU.mult)\
                                .then_inc(g_ready, 1)
                    steps(e, step)
            st.close()


        def stage_linear(layer):
            st = Stage()
            EH = HD + 1
            VB = NH * EH // KB
            NV = len(QCH)
            xb = st.sb("xb", [P, KB, T])
            qk = [st.sb(f"qk{c}", [TP, 2 * D]) for c in range(NV)]
            vv = [st.sb(f"vv{c}", [TP, KB * VB]) for c in range(NV)]
            hm = st.sb("hm", [TP, NV, 2 * NH])
            qT = st.sb("qT", [P, KB, T])
            KV = st.sb("KV", [P, KB, VB])
            mask = st.sb("mask", [P, KB, VB])
            den = st.sb("den", [TP, NV, NH])
            rec = st.sb("rec", [TP, NV, NH])
            on = [st.sb(f"on{c}", [TP, NH, HD]) for c in range(NV)]
            pqk = [st.psum(f"pqk{r}", [TP, 512]) for r in range(2)]
            pv = [st.psum(f"pv{r}", [TP, 512]) for r in range(2)]
            pkv = [st.psum(f"pkv{r}", [P, 512]) for r in range(2)]
            pt = [st.psum(f"pt{r}", [P, 512]) for r in range(2)]
            mask_in = st.sem("mask_in")
            xb_ready = st.sem("xb_ready")
            qk_ready = st.sem("qk_ready")
            qk_used = st.sem("qk_used")
            v_ready = st.sem("v_ready")
            v_used = st.sem("v_used")
            x_ready = st.sem("x_ready")
            e_ready = st.sem("e_ready")
            t_ready = st.sem("t_ready")
            t_used = st.sem("t_used")
            kv_ready = st.sem("kv_ready")
            kvm_ready = st.sem("kvm_ready")
            on_ready = st.sem("on_ready")
            own = st.sem("own")
            OWN = 3 * NV + 3 * NV

            with nc.Block() as block:
                @block.sync
                def _(e):
                    e.dma_start(mask[:, :, :], a["kv_mask"]).then_inc(mask_in, 16)

                @block.gpsimd
                def _(e):
                    with e.Fori(0, B) as b:
                        e.wait_ge(v_ready, 2 * NV * b + 1)
                        e.tensor_copy(xb[:, :, :], cols_of(XT, b * T, T)).then_inc(xb_ready, 1)

                @block.tensor
                def _(e):
                    e.sem_inc(v_ready, 1)
                    e.wait_ge(attn_loaded[layer], 48)
                    with e.Fori(0, B) as b:
                        e.wait_ge(xb_ready, b + 1)

                        def project(c):
                            q0, qn = QCH[c]
                            r = c % 2
                            e.wait_ge(qk_used, NV * b + 1 + max(c - 1, 0))
                            for kb in range(KB):
                                m = e.matmul(pqk[r][0:qn, :], xb[:, kb, q0:q0 + qn], ATW[:, kb, 0:2 * D],
                                             start=kb == 0, stop=kb == KB - 1)
                            m.then_inc(qk_ready, 1)
                            e.wait_ge(v_used, 2 * NV * b + c + 1)
                            for kb in range(KB):
                                m = e.matmul(pv[r][0:qn, 0:KB * VB], xb[:, kb, q0:q0 + qn],
                                             ATW[:, kb, 2 * D:2 * D + KB * VB], start=kb == 0, stop=kb == KB - 1)
                            m.then_inc(v_ready, 1)

                        def keys(c):
                            q0, qn = QCH[c]
                            e.wait_ge(e_ready, NV * b + c + 1)
                            e.wait_ge(v_used, 2 + 2 * NV * b + c + 1)
                            e.wait_ge(t_used, 2 * NV * b + c + 1)
                            e.sem_inc(begun, 1)
                            for kb in range(KB):
                                m = e.transpose(pt[c % 2][:, kb * P:kb * P + qn], qk[c][0:qn, kb * P:kb * P + P],
                                                ident[0:qn, 0:qn])
                            m.then_inc(t_ready, 1)
                            for kb in range(KB):
                                m = e.matmul(pkv[kb][:, 0:VB], qk[c][0:qn, D + kb * P:D + kb * P + P],
                                             vv[c][0:qn, kb * VB:kb * VB + VB], start=c == 0, stop=c == NV - 1)
                            if c == NV - 1:
                                m.then_inc(kv_ready, 1)

                        def outputs(c):
                            q0, qn = QCH[c]
                            e.wait_ge(v_used, 2 * NV * b + NV + c + 1)
                            for kb in range(KB):
                                m = e.matmul(pv[(NV + c) % 2][0:qn, kb * VB:kb * VB + VB], qT[:, kb, q0:q0 + qn],
                                             KV[:, kb, :], start=True, stop=True)
                            m.then_inc(v_ready, 1)

                        def back(c):
                            q0, qn = QCH[c]
                            e.wait_ge(on_ready, NV * b + c + 1)
                            e.wait_ge(t_used, 2 * NV * b + NV + c + 1)
                            e.sem_inc(begun, 1)
                            for kb in range(KB):
                                m = e.transpose(pt[(NV + c) % 2][:, kb * P:kb * P + qn],
                                                on[c][0:qn, kb * 8:kb * 8 + 8, :].rearrange("p h d -> p (h d)"),
                                                ident[0:qn, 0:qn])
                            m.then_inc(t_ready, 1)

                        for c in range(NV + 1):
                            if c < NV:
                                project(c)
                            if c >= 1:
                                keys(c - 1)
                        e.wait_ge(kvm_ready, b + 1)
                        e.wait_ge(t_used, 2 + 2 * NV * b + NV)
                        for c in range(NV + 1):
                            if c < NV:
                                outputs(c)
                            if c >= 1:
                                back(c - 1)

                @block.vector
                def _(e):
                    e.sem_inc(qk_used, 1)
                    e.sem_inc(v_used, 2)
                    e.wait_ge(mask_in, 16)
                    e.wait_ge(attn_loaded[layer], 48)
                    with e.Fori(0, B) as b:
                        for c, (q0, qn) in enumerate(QCH):
                            o = OWN * b + 3 * c
                            e.wait_ge(qk_ready, NV * b + c + 1)
                            e.tensor_tensor(qk[c][0:qn, :], pqk[c % 2][0:qn, :], ROWS[0:qn, 0:2 * D], ALU.add)\
                                .then_inc(qk_used, 1)
                            e.wait_ge(v_ready, 1 + 2 * NV * b + c + 1)
                            e.tensor_tensor(vv[c][0:qn, :], pv[c % 2][0:qn, 0:KB * VB],
                                            ROWS[0:qn, 2 * D:2 * D + KB * VB], ALU.add).then_inc(v_used, 1)
                            e.wait_ge(qk_used, 1 + NV * b + c + 1)
                            heads = qk[c][0:qn, :].rearrange("p (h d) -> p h d", d=HD)
                            e.tensor_reduce(hm[0:qn, c, :], heads, AX.X, ALU.max).then_inc(own, 3)
                            e.wait_ge(own, o + 3)
                            e.tensor_tensor(heads, heads, hm[0:qn, c, :].rearrange("p (h o) -> p h o", o=1)
                                            .to_broadcast([qn, 2 * NH, HD]), ALU.subtract).then_inc(x_ready, 1)
                        e.wait_ge(kv_ready, b + 1)
                        for kb in range(KB):
                            m = e.tensor_tensor(KV[:, kb, :], pkv[kb][:, 0:VB], mask[:, kb, :], ALU.mult)
                        m.then_inc(kvm_ready, 1)
                        for c, (q0, qn) in enumerate(QCH):
                            o = OWN * b + 3 * NV + 3 * c
                            e.wait_ge(v_ready, 1 + 2 * NV * b + NV + c + 1)
                            y = pv[(NV + c) % 2][0:qn, 0:KB * VB].rearrange("p (h x) -> p h x", x=EH)
                            e.tensor_scalar(den[0:qn, c, :], y[:, :, HD], 1e-6, None, ALU.add).then_inc(own, 1)
                            e.wait_ge(own, o + 1)
                            e.reciprocal(rec[0:qn, c, :], den[0:qn, c, :]).then_inc(own, 2)
                            e.wait_ge(own, o + 3)
                            e.tensor_tensor(on[c][0:qn, :, :], y[:, :, 0:HD],
                                            rec[0:qn, c, :].rearrange("p (h o) -> p h o", o=1)
                                            .to_broadcast([qn, NH, HD]), ALU.mult).then_inc(v_used, 1)
                            e.wait_ge(v_used, 2 + 2 * NV * b + NV + c + 1)
                            e.sem_inc(on_ready, 1)

                @block.scalar
                def _(e):
                    e.sem_inc(t_used, 2)
                    with e.Fori(0, B) as b:
                        for c in range(NV + 1):
                            if c < NV:
                                q0, qn = QCH[c]
                                e.wait_ge(x_ready, NV * b + c + 1)
                                e.activation(qk[c][0:qn, :], qk[c][0:qn, :], ACT.Exp).then_inc(e_ready, 1)
                            if c >= 1:
                                q0, qn = QCH[c - 1]
                                e.wait_ge(t_ready, 2 * NV * b + c)
                                e.activation(qT[:, :, q0:q0 + qn],
                                             pt[(c - 1) % 2][:, 0:KB * P].rearrange("p (k t) -> p k t", k=KB)[:, :, 0:qn],
                                             ACT.Copy).then_inc(t_used, 1)
                        for c, (q0, qn) in enumerate(QCH):
                            e.wait_ge(t_ready, 2 * NV * b + NV + c + 1)
                            e.activation(cols_of(XT, b * T + q0, qn),
                                         pt[(NV + c) % 2][:, 0:KB * P].rearrange("p (k t) -> p k t", k=KB)[:, :, 0:qn],
                                         ACT.Copy).then_inc(t_used, 1)
            st.close()

        def stage_segments(layer):
            st = Stage()
            XP = st.sb("XP", [P, KB, B, TS])
            A = [[st.sb(f"A{n}_{r}", [P, KB, SW]) for n in range(2)] for r in range(2)]
            QKV = [st.sb(f"QKV{r}", [SP, SEG, 3, D]) for r in range(2)]
            prod = [st.sb(f"prod{n}", [SP, SEG, D]) for n in range(2)]
            SC = st.sb("SC", [SP, SEG, SEG, SH])
            PR = st.sb("PR", [SP, SEG, SEG, SH])
            smx = st.sb("smx", [SP, SEG, SH])
            ssum = st.sb("ssum", [SP, SEG, SH])
            srec = st.sb("srec", [SP, SEG, SH])
            O = st.sb("O", [SP, SEG, D])
            pa = [st.psum(f"pa{r}", [P, 512]) for r in range(2)]
            pqk = [st.psum(f"pqk{r}", [SP, 512]) for r in range(2)]
            pv = [st.psum(f"pv{r}", [SP, 512]) for r in range(2)]
            po = [st.psum(f"po{r}", [P, 512]) for r in range(2)]
            xp_ready = st.sem("xp_ready")
            a_ready = st.sem("a_ready")
            a_used = st.sem("a_used")
            q_ready = st.sem("q_ready")
            q_used = st.sem("q_used")
            m_ready = [st.sem(f"m_ready{n}") for n in range(2)]
            m_used = [st.sem(f"m_used{n}") for n in range(2)]
            d_ready = st.sem("d_ready")
            p_ready = st.sem("p_ready")
            pr_ready = st.sem("pr_ready")
            o_ready = st.sem("o_ready")
            t_ready = st.sem("t_ready")
            t_used = st.sem("t_used")
            own = st.sem("own")
            OWN = 6
            flat = XP[:, :, :, :].rearrange("p k b t -> p k (b t)")

            with nc.Block() as block:
                @block.gpsimd
                def _(e):
                    e.tensor_copy(XP[:, 0, :, 0:T], XT[:, 0, :].rearrange("p (b t) -> p b t", b=B)).then_inc(xp_ready, 1)

                    with e.Fori(0, NST // 2) as it:
                        for r in range(2):
                            k = 2 * it + r
                            e.wait_ge(q_used, 2 + SEG * k + SEG)
                            for n, i in enumerate((1, 3)):
                                e.wait_ge(m_used[1], 4 * k + n + 1)
                                e.tensor_tensor(prod[1][:, :, :], QKV[r][:, i:i + 1, 0, :].to_broadcast([SP, SEG, D]),
                                                QKV[r][:, :, 1, :], ALU.mult).then_inc(m_ready[1], 1)
                            e.wait_ge(pr_ready, k + 1)
                            for n, i in enumerate((1, 3)):
                                e.wait_ge(m_used[1], 4 * k + 2 + n + 1)
                                for j in range(SEG):
                                    m = e.tensor_tensor(prod[1][:, j, :].rearrange("p (h d) -> p h d", d=SHD),
                                                        QKV[r][:, j, 2, :].rearrange("p (h d) -> p h d", d=SHD),
                                                        PR[:, i, j, :].rearrange("p (h o) -> p h o", o=1)
                                                        .to_broadcast([SP, SH, SHD]), ALU.mult)
                                m.then_inc(m_ready[1], 1)

                @block.vector
                def _(e):
                    e.tensor_copy(XP[:, 1, :, 0:T], XT[:, 1, :].rearrange("p (b t) -> p b t", b=B))
                    e.tensor_copy(XP[:, :, :, T:TS].rearrange("p k b t -> p (k b) t"),
                                  XT[:, :, :].rearrange("p k (b t) -> p (k b) t", b=B)[:, :, 0:TS - T]).then_inc(xp_ready, 1)
                    e.sem_inc(q_used, 2)
                    for n in range(2):
                        e.sem_inc(m_used[n], 1)
                    e.wait_ge(attn_loaded[layer], 48)
                    with e.Fori(0, NST // 2) as it:
                        for r in range(2):
                            k = 2 * it + r
                            for i in range(SEG):
                                e.wait_ge(q_ready, 1 + SEG * k + i + 1)
                                e.tensor_tensor(QKV[r][:, i, 0:2, :].rearrange("p a b -> p (a b)"), pqk[i % 2][:, :],
                                                ROWS[0:SP, 0:512], ALU.add)
                                e.tensor_tensor(QKV[r][:, i, 2, :], pv[i % 2][:, 0:D], ROWS[0:SP, 512:768], ALU.add)\
                                    .then_inc(q_used, 1)
                            e.wait_ge(q_used, 2 + SEG * k + SEG)

                            def scores(n, i, x):
                                e.wait_ge(m_ready[n], 4 * k + x + 1)
                                e.tensor_reduce(SC[:, i, :, :].rearrange("p j h -> p (j h)"),
                                                prod[n][:, :, :].rearrange("p j (h d) -> p (j h) d", d=SHD),
                                                AX.X, ALU.add).then_inc(m_used[n], 1)

                            for x, i in enumerate((0, 2)):
                                e.wait_ge(m_used[0], 4 * k + x + 1)
                                e.tensor_tensor(prod[0][:, :, :], QKV[r][:, i:i + 1, 0, :].to_broadcast([SP, SEG, D]),
                                                QKV[r][:, :, 1, :], ALU.mult).then_inc(m_ready[0], 1)
                                scores(0, i, x)
                                scores(1, i + 1, x)
                            e.wait_ge(m_used[0], 1 + 4 * k + 2)
                            e.wait_ge(m_used[1], 1 + 4 * k + 2)
                            e.memset(SC[:, :, :, :].rearrange("p i j h -> p (i j) h")[:, 0:SEG * SEG:SEG + 1, :], -BIG)\
                                .then_inc(own, 1)
                            e.wait_ge(own, OWN * k + 1)
                            e.tensor_reduce(smx[:, :, :], SC[:, :, :, :].rearrange("p i j h -> p i h j"), AX.X, ALU.max)\
                                .then_inc(own, 1)
                            e.wait_ge(own, OWN * k + 2)
                            for i in range(SEG):
                                m = e.tensor_tensor(SC[:, i, :, :], SC[:, i, :, :],
                                                    smx[:, i:i + 1, :].to_broadcast([SP, SEG, SH]), ALU.subtract)
                            m.then_inc(d_ready, 1)
                            e.wait_ge(p_ready, k + 1)
                            e.tensor_reduce(ssum[:, :, :], PR[:, :, :, :].rearrange("p i j h -> p i h j"), AX.X, ALU.add)\
                                .then_inc(own, 1)
                            e.wait_ge(own, OWN * k + 3)
                            e.reciprocal(srec[:, :, :], ssum[:, :, :]).then_inc(own, 3)
                            e.wait_ge(own, OWN * k + 6)
                            for i in range(SEG):
                                m = e.tensor_tensor(PR[:, i, :, :], PR[:, i, :, :],
                                                    srec[:, i:i + 1, :].to_broadcast([SP, SEG, SH]), ALU.mult)
                            m.then_inc(pr_ready, 1)
                            e.wait_ge(pr_ready, k + 1)
                            e.wait_ge(t_ready, 2 * k + 2)

                            def outputs(n, i, x):
                                e.wait_ge(m_ready[n], 4 * k + 2 + x + 1)
                                return e.tensor_reduce(O[:, i, :], prod[n][:, :, :].rearrange("p j f -> p f j"),
                                                       AX.X, ALU.add).then_inc(m_used[n], 1)

                            for x, i in enumerate((0, 2)):
                                e.wait_ge(m_used[0], 4 * k + 2 + x + 1)
                                for j in range(SEG):
                                    m = e.tensor_tensor(prod[0][:, j, :].rearrange("p (h d) -> p h d", d=SHD),
                                                        QKV[r][:, j, 2, :].rearrange("p (h d) -> p h d", d=SHD),
                                                        PR[:, i, j, :].rearrange("p (h o) -> p h o", o=1)
                                                        .to_broadcast([SP, SH, SHD]), ALU.mult)
                                m.then_inc(m_ready[0], 1)
                                outputs(0, i, x)
                                outputs(1, i + 1, x)
                            e.wait_ge(m_used[1], 1 + 4 * k + 4)
                            e.sem_inc(o_ready, 1)

                @block.scalar
                def _(e):
                    e.sem_inc(a_used, 2)
                    e.sem_inc(t_used, 2)
                    e.wait_ge(attn_loaded[layer], 48)

                    def first(k, r):
                        for n in range(2):
                            for m in range(KB):
                                x = 2 * n + m
                                e.wait_ge(a_ready, 4 * k + x + 1)
                                e.activation(A[r][n][:, m, :], pa[x % 2][:, 0:SW], ACT.Identity,
                                             bias=COLS[:, x:x + 1]).then_inc(a_used, 1)

                    def last(k):
                        e.wait_ge(d_ready, k + 1)
                        e.activation(PR[:, :, :, :], SC[:, :, :, :], ACT.Exp, scale=SHD ** -0.5).then_inc(p_ready, 1)
                        for kb in range(KB):
                            e.wait_ge(t_ready, 2 + 2 * k + kb + 1)
                            e.activation(flat[:, kb, bass.ds(k * SW, SW)].rearrange("p (s i) -> p i s", i=SEG),
                                         po[kb][:, 0:SW].rearrange("p (i s) -> p i s", i=SEG), ACT.Copy).then_inc(t_used, 1)

                    first(0, 0)
                    with e.Fori(0, NST // 2 - 1) as it:
                        first(2 * it + 1, 1)
                        last(2 * it)
                        first(2 * it + 2, 0)
                        last(2 * it + 1)
                    first(NST - 1, 1)
                    last(NST - 2)
                    last(NST - 1)
                    e.wait_ge(t_used, 2 + 2 * NST)
                    for kb in range(KB):
                        e.activation(XT[:, kb, :].rearrange("p (b t) -> p b t", b=B), XP[:, kb, :, 0:T], ACT.Copy)

                @block.tensor
                def _(e):
                    e.sem_inc(q_ready, 1)
                    e.sem_inc(t_ready, 2)
                    e.wait_ge(xp_ready, 2)
                    e.wait_ge(attn_loaded[layer], 48)

                    def first(k):
                        for n in range(2):
                            for m in range(KB):
                                x = 2 * n + m
                                e.wait_ge(a_used, 4 * k + x + 1)
                                for kb in range(KB):
                                    mm = e.matmul(pa[x % 2][:, 0:SW], ATW[:, kb, n * D + m * P:n * D + m * P + P],
                                                  flat[:, kb, bass.ds(k * SW, SW)], start=kb == 0, stop=kb == KB - 1)
                                mm.then_inc(a_ready, 1)

                    def second(k, r):
                        e.wait_ge(a_used, 2 + 4 * k + 4)
                        for i in range(SEG):
                            e.wait_ge(q_used, SEG * k + i + 1)
                            for kb in range(KB):
                                e.matmul(pqk[i % 2][:, :], A[r][0][:, kb, i:SW:SEG], ATW[:, kb, 512:1024],
                                         start=kb == 0, stop=kb == KB - 1)
                            for kb in range(KB):
                                m = e.matmul(pv[i % 2][:, 0:D], A[r][1][:, kb, i:SW:SEG], ATW[:, kb, 1024:1280],
                                             start=kb == 0, stop=kb == KB - 1)
                            m.then_inc(q_ready, 1)

                    def last(k):
                        e.wait_ge(o_ready, k + 1)
                        for kb in range(KB):
                            e.wait_ge(t_used, 2 * k + kb + 1)
                            for i in range(SEG):
                                m = e.transpose(po[kb][:, SP * i:SP * i + SP], O[:, i, kb * P:kb * P + P], ident[0:SP, 0:SP])
                            m.then_inc(t_ready, 1)

                    first(0)
                    with e.Fori(0, NST // 2 - 1) as it:
                        second(2 * it, 0)
                        first(2 * it + 1)
                        last(2 * it)
                        second(2 * it + 1, 1)
                        first(2 * it + 2)
                        last(2 * it + 1)
                    second(NST - 2, 0)
                    first(NST - 1)
                    last(NST - 2)
                    second(NST - 1, 1)
                    last(NST - 1)
            st.close()

        def stage_moe(n_ffn, loads, NE, shared, NHB, kind):
            st = Stage()
            relu = kind == "relu"
            NX = NE + shared
            NG_ = NX * NHB
            NY = NX + relu
            topk = 4 if kind == "sigmoid" else 2
            POS = 2
            ln = Norm(st, CT, KB)
            xT = [st.sb(f"xT{r}", [P, KB, CW]) for r in range(2)]
            sg = [st.sb(f"sg{r}", [P, CW]) for r in range(2)]
            hb = [[st.sb(f"h{r}_{n}", [P, CW]) for n in range(NHB)] for r in range(2)]
            ya = [st.sb(f"ya{r}", [TP, CT, D]) for r in range(2)]
            C = [st.sb(f"C{r}", [TP, CT, NX]) for r in range(2)]
            lg = st.sb("lg", [TP, CT, NE])
            pb = st.sb("pb", [TP, CT, NE])
            sel = st.sb("sel", [TP, CT, NE])
            eq = st.sb("eq", [TP, CT, NE])
            big = st.sb("big", [TP, CT, NE])
            c1 = st.sb("c1", [TP, CT])
            c2 = st.sb("c2", [TP, CT])
            top = st.sb("top", [TP, CT, 8])
            tix = st.sb("tix", [TP, CT, 8], U32)
            tif = st.sb("tif", [TP, CT, 8])
            sT = [st.sb(f"sT{r}", [8, CW]) for r in range(2)] if relu else None
            gu = [[st.psum(f"gu{r}_{n}", [P, 512]) for n in range(2)] for r in range(2)]
            py = [st.psum(f"py{j}", [TP, 512]) for j in range(CT)]
            misc = st.psum("misc", [P, 512])

            x_ready = st.sem("x_ready")
            r_ready = st.sem("r_ready")
            lg_ready = st.sem("lg_ready")
            ex_in = st.sem("ex_in")
            ex_out = st.sem("ex_out")
            c_ready = st.sem("c_ready")
            ct_ready = st.sem("ct_ready")
            s_ready = st.sem("s_ready")
            gu_ready = st.sem("gu_ready")
            sg_ready = st.sem("sg_ready")
            h_made = st.sem("h_made")
            y_ready = st.sem("y_ready")
            y_used = st.sem("y_used")
            h_added = st.sem("h_added")
            own = st.sem("own")
            c_set = st.sem("c_set")

            def chunks(e, body, prologue):
                prologue()
                with e.Fori(0, NCH // 2 - 1) as i:
                    body(2 * i, 0, True)
                    body(2 * i + 1, 1, True)
                body(NCH - 2, 0, True)
                body(NCH - 1, 1, False)

            def pieces(prep, k, r, nxt, x):
                if nxt and x - POS + 1 in range(6):
                    prep(k + 1, 1 - r, x - POS + 1)

            with nc.Block() as block:
                @block.tensor
                def _(e):
                    e.sem_inc(ln.tr_ready, 1)
                    e.sem_inc(y_ready, 2 * CT)
                    e.wait_ge(ffn_loaded[n_ffn], loads)

                    def prep(k, r, part):
                        if part in (1, 2):
                            kb = part - 1
                            if kb == 0:
                                e.wait_ge(ln.xn_ready, k + 1)
                                e.wait_ge(s_ready if relu else lg_ready, k + 1)
                            else:
                                e.wait_ge(x_ready, KB * k + 1)
                            for j in range(CT):
                                m = e.transpose(misc[:, TP * j:TP * j + TP], ln.xn[:, j, kb * P:kb * P + P],
                                                ident[0:TP, 0:TP])
                            m.then_inc(ln.tr_ready, 1)
                        if part == 3:
                            e.wait_ge(x_ready, KB * k + 2)
                            for j in range(CT):
                                for kb in range(KB):
                                    m = e.matmul(misc[0:TP, 16 * j:16 * j + NE], xT[r][:, kb, TP * j:TP * j + TP],
                                                 RW[:, kb, 0:NE], start=kb == 0, stop=kb == KB - 1)
                            m.then_inc(r_ready, 1)
                        if part == 5 and relu:
                            e.wait_ge(c_ready, k + 1)
                            for j in range(CT):
                                m = e.transpose(misc[0:NE, TP * j:TP * j + TP], C[r][:, j, :], ident[0:TP, 0:TP])
                            m.then_inc(ct_ready, 1)

                    def gate_up(k, r, x):
                        for b in range(NHB):
                            n = x * NHB + b
                            slot = (r * NG_ + n) % 2
                            e.wait_ge(h_made, k * NG_ + n + 1)
                            for g in range(1 if relu else 2):
                                w0 = n * P if relu else (2 * x + g) * P
                                for kb in range(KB):
                                    m = e.matmul(gu[slot][g][:, 0:CW], FW1[:, kb, w0:w0 + P], xT[r][:, kb, :],
                                                 start=kb == 0, stop=kb == KB - 1)
                            m.then_inc(gu_ready, 1)

                    def down(k, r, x):
                        if x < NX:
                            e.wait_ge(h_made, 2 + k * NG_ + (x + 1) * NHB)
                        else:
                            e.wait_ge(s_ready, 1 + k + 1)
                        for j in range(CT):
                            y = py[j][:, 0:D]
                            e.wait_ge(y_used, (k * NY + x) * CT + j + 1)
                            if x == NX:
                                e.matmul(y, sT[r][0:NE, TP * j:TP * j + TP], B2[0:NE, :], start=True, stop=True)\
                                    .then_inc(y_ready, 1)
                                continue
                            for b in range(NHB):
                                m = e.matmul(y, hb[(r * NX + x) % 2][b][:, TP * j:TP * j + TP], FW2[:, x * NHB + b, :],
                                             start=b == 0, stop=b == NHB - 1)
                            m.then_inc(y_ready, 1)

                    def body(k, r, nxt):
                        e.wait_ge(x_ready, KB * k + 2)
                        for x in range(NX):
                            pieces(prep, k, r, nxt, x)
                            gate_up(k, r, x)
                            if x:
                                down(k, r, x - 1)
                        for x in range(NX - 1, NY):
                            down(k, r, x)
                    chunks(e, body, lambda: [prep(0, 0, part) for part in range(6)])

                @block.scalar
                def _(e):
                    if relu:
                        e.sem_inc(s_ready, 1)
                        e.sem_inc(h_made, 2)
                        e.wait_ge(ffn_loaded[n_ffn], loads)

                    def prep(k, r, part):
                        if part == 0:
                            ln.scalar(e, k)
                        if part in (1, 2):
                            kb = part - 1
                            e.wait_ge(ln.tr_ready, 1 + KB * k + kb + 1)
                            e.activation(xT[r][:, kb, :], misc[:, 0:CW], ACT.Copy).then_inc(x_ready, 1)
                        if part == 4:
                            e.wait_ge(ex_in, k + 1)
                            e.activation(pb[:, :, :], lg[:, :, :], ACT.Exp,
                                         scale=-1.0 if kind == "sigmoid" else 1.0).then_inc(ex_out, 1)
                        if part == 5 and relu:
                            e.wait_ge(ct_ready, k + 1)
                            e.activation(sT[r][0:NE, :], misc[0:NE, 0:CW], ACT.Copy).then_inc(s_ready, 1)

                    def body(k, r, nxt):
                        for x in range(NX):
                            pieces(prep, k, r, nxt, x)
                            for b in range(NHB):
                                n = x * NHB + b
                                slot = (r * NG_ + n) % 2
                                e.wait_ge(gu_ready, k * NG_ + n + 1)
                                if relu:
                                    if b == 0:
                                        e.wait_ge(y_ready, (k * NY + (x if x >= 2 else 0) + 1) * CT)
                                    e.activation(hb[(r * NX + x) % 2][b][:, :], gu[slot][0][:, 0:CW], ACT.Relu,
                                                 bias=B1[:, n:n + 1]).then_inc(h_made, 1)
                                else:
                                    e.wait_ge(h_made, k * NG_ + n + 1)
                                    e.activation(sg[slot][:, :], gu[slot][0][:, 0:CW], ACT.Silu).then_inc(sg_ready, 1)
                    chunks(e, body, lambda: [prep(0, 0, part) for part in range(6)])

                @block.vector
                def _(e):
                    e.sem_inc(lg_ready, 1)
                    e.sem_inc(y_used, CT)
                    if not relu:
                        e.sem_inc(h_made, 2)
                    e.wait_ge(ffn_loaded[n_ffn], loads)
                    for r in range(2):
                        m = e.memset(C[r][:, :, :], 1.0)
                    m.then_inc(c_set, 1)
                    e.wait_ge(c_set, 1)
                    OWN = {"probs": 10, "sigmoid": 17, "relu": 13}[kind]

                    def prep(k, r, part):
                        if part == 0:
                            ln.vector(e, k)
                        if part != 4:
                            return
                        done = 0

                        def then(m):
                            nonlocal done
                            done += 1
                            m.then_inc(own, 1)
                            e.wait_ge(own, k * OWN + done)

                        def wide(v):
                            return v.rearrange("p (j o) -> p j o", o=1).to_broadcast([TP, CT, NE])

                        e.wait_ge(r_ready, k + 1)
                        e.tensor_copy(lg[:, :, :], misc[0:TP, 0:16 * CT].rearrange("p (j n) -> p j n", n=16)[:, :, 0:NE])\
                            .then_inc(lg_ready, 1)
                        e.wait_ge(lg_ready, 1 + k + 1)
                        if kind == "sigmoid":
                            e.sem_inc(ex_in, 1)
                            e.wait_ge(ex_out, k + 1)
                            then(e.tensor_scalar(eq[:, :, :], pb[:, :, :], 1.0, None, ALU.add))
                            then(e.reciprocal(pb[:, :, :], eq[:, :, :]))
                            for j in range(CT):
                                m = e.tensor_tensor(big[:, j, :], pb[:, j, :], RB[0:TP, 0:NE], ALU.add)
                            then(m)
                            chosen = big
                        else:
                            then(e.tensor_reduce(c1[:, :], lg[:, :, :], AX.X, ALU.max))
                            e.tensor_tensor(lg[:, :, :], lg[:, :, :], wide(c1[:, :]), ALU.subtract).then_inc(ex_in, 1)
                            e.wait_ge(ex_out, k + 1)
                            then(e.tensor_reduce(c1[:, :], pb[:, :, :], AX.X, ALU.add))
                            then(e.reciprocal(c2[:, :], c1[:, :]))
                            then(e.tensor_tensor(pb[:, :, :], pb[:, :, :], wide(c2[:, :]), ALU.mult))
                            chosen = pb
                        e.sem_inc(begun, 1)
                        for j in range(CT):
                            m = e.max(top[:, j, :], chosen[:, j, :])
                        then(m)
                        e.sem_inc(begun, 1)
                        for j in range(CT):
                            m = e.max_index(tix[:, j, :], top[:, j, :], chosen[:, j, :])
                        then(m)
                        then(e.tensor_copy(tif[:, :, :], tix[:, :, :]))
                        then(e.tensor_tensor(sel[:, :, :], iota[:, :, 0:NE], wide(tif[:, :, 0]), ALU.is_equal))
                        for t in range(1, topk):
                            then(e.tensor_tensor(eq[:, :, :], iota[:, :, 0:NE], wide(tif[:, :, t]), ALU.is_equal))
                            if t < topk - 1 or kind != "probs":
                                then(e.tensor_tensor(sel[:, :, :], sel[:, :, :], eq[:, :, :], ALU.add))
                        w = C[r][:, :, 0:NE]
                        if kind == "probs":
                            then(e.tensor_tensor(sel[:, :, :], sel[:, :, :], eq[:, :, :], ALU.add))
                            e.tensor_tensor(w, sel[:, :, :], pb[:, :, :], ALU.mult).then_inc(c_ready, 1)
                        else:
                            then(e.tensor_tensor(sel[:, :, :], sel[:, :, :], pb[:, :, :], ALU.mult))
                            then(e.tensor_reduce(c1[:, :], sel[:, :, :], AX.X, ALU.add))
                            then(e.reciprocal(c2[:, :], c1[:, :]))
                            if kind == "sigmoid":
                                then(e.tensor_tensor(sel[:, :, :], sel[:, :, :], wide(c2[:, :]), ALU.mult))
                                e.tensor_scalar(w, sel[:, :, :], 2.5, None, ALU.mult).then_inc(c_ready, 1)
                            else:
                                e.tensor_tensor(w, sel[:, :, :], wide(c2[:, :]), ALU.mult).then_inc(c_ready, 1)
                        assert done == OWN, (kind, done)

                    def accumulate(k, r, x):
                        if x == 0:
                            e.wait_ge(c_ready, k + 1)
                            e.wait_ge(h_added, k + 1)
                        for j in range(CT):
                            n = (k * NY + x) * CT + j
                            y = py[j][:, 0:D]
                            e.wait_ge(y_ready, 2 * CT + n + 1)
                            if x:
                                e.wait_ge(y_used, n + 1)
                            if x == 0:
                                m = e.tensor_scalar(ya[r][:, j, :], y, C[r][:, j, 0:1], None, ALU.mult)
                            elif x == NX:
                                m = e.tensor_tensor(ya[r][:, j, :], y, ya[r][:, j, :], ALU.add)
                            else:
                                m = e.scalar_tensor_tensor(out=ya[r][:, j, :], in0=y, scalar=C[r][:, j, x:x + 1],
                                                           in1=ya[r][:, j, :], op0=ALU.mult, op1=ALU.add)
                            m.then_inc(y_used, 1)

                    def body(k, r, nxt):
                        for x in range(NX):
                            pieces(prep, k, r, nxt, x)
                            if not relu:
                                n = k * NG_ + x
                                slot = (r * NG_ + x) % 2
                                e.wait_ge(sg_ready, n + 1)
                                e.wait_ge(y_ready, (k * NY + x + 1) * CT)
                                e.tensor_tensor(hb[(r * NX + x) % 2][0][:, :], sg[slot][:, :], gu[slot][1][:, 0:CW],
                                                ALU.mult).then_inc(h_made, 1)
                            if x:
                                accumulate(k, r, x - 1)
                        for x in range(NX - 1, NY):
                            accumulate(k, r, x)
                    chunks(e, body, lambda: [prep(0, 0, part) for part in range(6)])

                @block.gpsimd
                def _(e):
                    e.sem_inc(h_added, 2)
                    with e.Fori(0, NCH // 2) as i:
                        for r in range(2):
                            k = 2 * i + r
                            e.wait_ge(y_used, CT + (k + 1) * NY * CT)
                            rows = H[:, bass.ds(CT * k, CT), :]
                            e.tensor_tensor(rows, rows, ya[r][:, :, :], ALU.add).then_inc(h_added, 1)
            st.close()

        def stage_ternary(n_ffn, loads):
            st = Stage()
            F = 1024
            NF = F // P
            ln = Norm(st, 1, 1)
            ones = st.sb("ones", [P, P])
            absum = st.sb("absum", [P, 2])
            thr = st.sb("thr", [P, 4])
            low = st.sb("low", [P, KB * F])
            xT = [st.sb(f"xT{r}", [P, KB, TP]) for r in range(2)]
            g = [st.sb(f"g{r}", [TP, F]) for r in range(2)]
            gn = [st.sb(f"gn{r}", [TP, F]) for r in range(2)]
            hT = [st.sb(f"hT{r}", [P, NF, TP]) for r in range(2)]
            fst = st.sb("fst", [TP, 2, 6])
            fmv = st.sb("fmv", [TP, 2])
            fsd = st.sb("fsd", [TP, 1])
            frs = st.sb("frs", [TP, 1])
            pf = [st.psum(f"pf{r}", [TP, F]) for r in range(2)]
            pt = [st.psum(f"pt{r}", [P, 512]) for r in range(2)]
            px = st.psum("px", [P, 512])
            po = st.psum("po", [TP, 512])
            sum_ready = st.sem("sum_ready")
            tot_ready = st.sem("tot_ready")
            own_q = st.sem("own_q")
            q_done = st.sem("q_done")
            x_ready = st.sem("x_ready")
            f_ready = st.sem("f_ready")
            g_ready = st.sem("g_ready")
            v_ready = st.sem("v_ready")
            s_ready = st.sem("s_ready")
            gn_ready = st.sem("gn_ready")
            t_ready = st.sem("t_ready")
            t_used = st.sem("t_used")
            o_ready = st.sem("o_ready")
            o_used = st.sem("o_used")
            own = st.sem("own")
            OWN = 2
            W1 = FW1[:, :, 0:F]
            W2 = FW2[:, 0:NF, :].rearrange("p c n -> p (c n)")

            with nc.Block() as block:
                @block.vector
                def _(e):
                    e.sem_inc(gn_ready, 2)
                    e.sem_inc(o_used, 1)
                    e.memset(ones[:, :], 1.0)
                    e.wait_ge(ffn_loaded[n_ffn], loads)
                    e.tensor_reduce(absum[:, 0:1], W1, AX.XY, ALU.add, apply_absolute_value=True)
                    e.tensor_reduce(absum[:, 1:2], W2, AX.X, ALU.add, apply_absolute_value=True).then_inc(sum_ready, 1)
                    e.wait_ge(tot_ready, 1)
                    e.tensor_scalar(thr[:, 0:2], px[:, 0:2], 1.0 / (D * F), 1e-6, ALU.mult, ALU.add).then_inc(own_q, 1)
                    e.wait_ge(own_q, 1)
                    e.tensor_scalar(thr[:, 2:4], thr[:, 0:2], -0.5, None, ALU.mult).then_inc(own_q, 1)
                    e.wait_ge(own_q, 2)
                    e.tensor_scalar(thr[:, 0:2], thr[:, 0:2], 0.5, None, ALU.mult).then_inc(own_q, 1)
                    e.wait_ge(own_q, 3)
                    lw = low[:, :].rearrange("p (k f) -> p k f", k=KB)
                    e.tensor_scalar(lw, W1, thr[:, 2:3], None, ALU.is_lt).then_inc(own_q, 1)
                    e.wait_ge(own_q, 4)
                    e.scalar_tensor_tensor(out=W1, in0=W1, scalar=thr[:, 0:1], in1=lw, op0=ALU.is_gt, op1=ALU.subtract)\
                        .then_inc(own_q, 1)
                    e.wait_ge(own_q, 5)
                    e.tensor_scalar(low[:, :], W2, thr[:, 3:4], None, ALU.is_lt).then_inc(own_q, 1)
                    e.wait_ge(own_q, 6)
                    e.scalar_tensor_tensor(out=W2, in0=W2, scalar=thr[:, 1:2], in1=low[:, :], op0=ALU.is_gt,
                                           op1=ALU.subtract).then_inc(q_done, 1)

                    def normalise(t, r):
                        e.wait_ge(g_ready, 2 + t + 1)
                        for h in range(2):
                            m = e.bn_stats(fst[:, h, :], g[r][:, 512 * h:512 * h + 512])
                        m.then_inc(own, 1)
                        e.wait_ge(own, OWN * t + 1)
                        e.sem_inc(begun, 1)
                        e.bn_aggr(fmv[:, :], fst[:, :, :].rearrange("p a b -> p (a b)")).then_inc(v_ready, 1)
                        e.wait_ge(s_ready, t + 1)
                        e.reciprocal(frs[:, :], fsd[:, :]).then_inc(own, 1)
                        e.wait_ge(own, OWN * t + 2)
                        e.wait_ge(t_ready, 2 * t + 1)
                        e.tensor_scalar(gn[r][:, :], g[r][:, :], fmv[:, 0:1], frs[:, 0:1], ALU.subtract, ALU.mult)\
                            .then_inc(gn_ready, 1)

                    def add(t):
                        e.wait_ge(o_ready, 2 + t + 1)
                        e.tensor_tensor(H[:, t, :], H[:, t, :], po[:, 0:D], ALU.add).then_inc(o_used, 1)

                    ln.vector(e, 0)
                    ln.vector(e, 1)
                    normalise(0, 0)
                    ln.vector(e, 2)
                    normalise(1, 1)
                    ln.vector(e, 3)
                    normalise(2, 0)
                    add(0)
                    with e.Fori(1, NT // 2 - 1) as i:
                        ln.vector(e, 2 * i + 2)
                        normalise(2 * i + 1, 1)
                        add(2 * i - 1)
                        ln.vector(e, 2 * i + 3)
                        normalise(2 * i + 2, 0)
                        add(2 * i)
                    normalise(NT - 1, 1)
                    add(NT - 3)
                    add(NT - 2)
                    add(NT - 1)

                @block.scalar
                def _(e):
                    e.sem_inc(x_ready, 1)
                    e.sem_inc(g_ready, 2)
                    e.sem_inc(t_used, 2)
                    e.wait_ge(ffn_loaded[n_ffn], loads)

                    def features(t, r):
                        ln.scalar(e, t)
                        e.wait_ge(ln.tr_ready, 1 + t + 1)
                        e.activation(xT[r][:, :, :], px[:, 0:KB * P].rearrange("p (k t) -> p k t", k=KB)[:, :, 0:TP],
                                     ACT.Copy).then_inc(x_ready, 1)

                    def gelu(t, r):
                        e.wait_ge(f_ready, t + 1)
                        e.wait_ge(gn_ready, t + 1)
                        e.activation(g[r][:, :], pf[r][:, :], ACT.Gelu).then_inc(g_ready, 1)

                    def root(t):
                        e.wait_ge(v_ready, t + 1)
                        e.activation(fsd[:, :], fmv[:, 1:2], ACT.Sqrt, bias=eps[0:TP, :]).then_inc(s_ready, 1)

                    def affine(t, r):
                        for h in range(2):
                            e.wait_ge(t_ready, 3 + 2 * t + h + 1)
                            if h == 0:
                                e.wait_ge(o_ready, t + 1)
                            for x in range(4):
                                c = 4 * h + x
                                m = e.activation(hT[r][:, c, :], pt[h][:, P * x:P * x + TP], ACT.Identity,
                                                 bias=B1[:, NF + c:NF + c + 1], scale=B1[:, c:c + 1])
                            m.then_inc(t_used, 1)

                    features(0, 0)
                    features(1, 1)
                    gelu(0, 0)
                    root(0)
                    with e.Fori(0, NT // 2 - 1) as i:
                        features(2 * i + 2, 0)
                        gelu(2 * i + 1, 1)
                        root(2 * i + 1)
                        affine(2 * i, 0)
                        features(2 * i + 3, 1)
                        gelu(2 * i + 2, 0)
                        root(2 * i + 2)
                        affine(2 * i + 1, 1)
                    gelu(NT - 1, 1)
                    root(NT - 1)
                    affine(NT - 2, 0)
                    affine(NT - 1, 1)

                @block.tensor
                def _(e):
                    e.sem_inc(ln.tr_ready, 1)
                    e.sem_inc(t_ready, 3)
                    e.sem_inc(o_ready, 2)
                    e.wait_ge(sum_ready, 1)
                    e.matmul(px[:, 0:2], ones[:, :], absum[:, :], start=True, stop=True).then_inc(tot_ready, 1)
                    e.wait_ge(own_q, 1)

                    def features(t):
                        e.wait_ge(ln.xn_ready, t + 1)
                        e.wait_ge(x_ready, t + 1)
                        for kb in range(KB):
                            m = e.transpose(px[:, kb * P:kb * P + TP], ln.xn[:, 0, kb * P:kb * P + P], ident[0:TP, 0:TP])
                        m.then_inc(ln.tr_ready, 1)

                    def hidden(t, r):
                        e.wait_ge(x_ready, 1 + t + 1)
                        e.wait_ge(g_ready, t + 1)
                        for h in range(2):
                            for kb in range(KB):
                                m = e.matmul(pf[r][:, 512 * h:512 * h + 512], xT[r][:, kb, :],
                                             FW1[:, kb, 512 * h:512 * h + 512], start=kb == 0, stop=kb == KB - 1)
                        m.then_inc(f_ready, 1)

                    def turn(t, r):
                        e.wait_ge(gn_ready, 2 + t + 1)
                        for h in range(2):
                            e.wait_ge(t_used, 2 * t + h + 1)
                            for x in range(4):
                                c = 4 * h + x
                                m = e.transpose(pt[h][:, P * x:P * x + TP], gn[r][:, P * c:P * c + P], ident[0:TP, 0:TP])
                            m.then_inc(t_ready, 1)

                    def project(t, r):
                        e.wait_ge(t_used, 2 + 2 * t + 2)
                        e.wait_ge(o_used, t + 1)
                        for c in range(NF):
                            m = e.matmul(po[:, 0:D], hT[r][:, c, :], FW2[:, c, :], start=c == 0, stop=c == NF - 1)
                        m.then_inc(o_ready, 1)

                    features(0)
                    features(1)
                    e.wait_ge(q_done, 1)
                    hidden(0, 0)
                    hidden(1, 1)
                    features(2)
                    turn(0, 0)
                    hidden(2, 0)
                    features(3)
                    project(0, 0)
                    turn(1, 1)
                    with e.Fori(1, NT // 2 - 1) as i:
                        hidden(2 * i + 1, 1)
                        features(2 * i + 2)
                        project(2 * i - 1, 1)
                        turn(2 * i, 0)
                        hidden(2 * i + 2, 0)
                        features(2 * i + 3)
                        project(2 * i, 0)
                        turn(2 * i + 1, 1)
                    hidden(NT - 1, 1)
                    project(NT - 3, 1)
                    turn(NT - 2, 0)
                    project(NT - 2, 0)
                    turn(NT - 1, 1)
                    project(NT - 1, 1)
            st.close()

        NL0 = load_counts(a, "L0")
        NL1, NL2, NL3 = load_counts(a, "L1"), load_counts(a, "L2"), load_counts(a, "L3")

        def prefetch_attn(n, name):
            return lambda e: load_attn(e, n, a[f"w_{name}"], a[f"rows_{name}"], a[f"cols_{name}"])

        def prefetch_ffn(n, name):
            def load(e):
                load_ffn(e, n, *(a.get(f"{name}_{x}") for x in ("w1", "w2", "rw", "rb", "b1", "b2")))
            return load

        def stage_load(*loads):
            with nc.Block() as block:
                @block.sync
                def _(e):
                    for f in loads:
                        f(e)

        st = Stage()
        with nc.Block() as block:
            @block.sync
            def _(e):
                e.dma_start(ident[:, :], a["ident"]).then_inc(const_loaded, 16)
                e.dma_start(iota[:, :, :], a["iota"]).then_inc(const_loaded, 16)
                if from_step is None:
                    e.dma_start(XT[:, :, :], a["xT"].rearrange("(k p) t -> p k t", p=P)).then_inc(const_loaded, 16)
                    prefetch_attn(0, "tok")(e)
                    prefetch_ffn(0, "L0")(e)
                else:
                    e.dma_start(H[:, :, :], a["h_in"].rearrange("(t p) d -> p t d", p=TP)).then_inc(const_loaded, 16)
                e.wait_ge(const_loaded, 48)

            @block.vector
            def _(e):
                e.memset(eps[:, :], LN_EPS)
        st.close()
        none = lambda e: None
        stages = [
            lambda: (stage_qkv(0, False), stage_attn(1, False), stage_project(1024, 512, True, none),
                     stage_load(prefetch_attn(1, "lin"))),
            lambda: None,
            lambda: (stage_norm(), stage_linear(1), stage_project(784, 784, False, none),
                     stage_load(prefetch_attn(2, "rope"))),
            lambda: (stage_moe(0, NL0, 16, 2, 1, "probs"), stage_load(prefetch_ffn(1, "L1"))),
            lambda: (stage_norm(), stage_qkv(2, True), stage_attn(0, True), stage_project(1024, 512, False, none),
                     stage_load(prefetch_attn(3, "seg"))),
            lambda: (stage_moe(1, NL1, 16, 1, 1, "sigmoid"), stage_load(prefetch_ffn(2, "L2"))),
            lambda: (stage_norm(), stage_segments(3), stage_project(1280, 768, False, none),
                     stage_load(prefetch_attn(4, "gqa"))),
            lambda: (stage_moe(2, NL2, 8, 0, 4, "relu"), stage_load(prefetch_ffn(3, "L3"))),
            lambda: (stage_norm(), stage_qkv(4, False), stage_attn(0, False), stage_project(1024, 512, False, none)),
            lambda: stage_ternary(3, NL3),
        ]
        first_stage = 0
        if from_step is not None:
            first_stage = from_step + 1
            att = {2: (1, "lin"), 4: (2, "rope"), 6: (3, "seg"), 8: (4, "gqa")}
            ffn = {3: 0, 5: 1, 7: 2, 9: 3}
            stage_load(*([prefetch_attn(*att[first_stage])] if first_stage in att else []),
                       *([prefetch_ffn(ffn[first_stage], f"L{ffn[first_stage]}")] if first_stage in ffn else []))
        for f in stages[first_stage:last_stage]:
            f()
        if last_stage < len(stages):
            with nc.Block() as block:
                @block.sync
                def _(e):
                    for x, n in started.items():
                        e.wait_ge(x[0], n)

        st = Stage()
        with nc.Block() as block:
            @block.sync
            def _(e):
                e.dma_start(out.rearrange("(t p) d -> p t d", p=TP), H[:, :, :]).then_inc(out_stored, 16)
                e.wait_ge(out_stored, 16)
        st.close()


def load_counts(a, name):
    return 16 * (KB + 1 + sum(f"{name}_{x}" in a for x in ("rw", "rb", "b1", "b2")))


def rows_of(*vectors):
    return np.ascontiguousarray(np.broadcast_to(np.concatenate(vectors)[None, :], (P, sum(map(len, vectors)))))


def to_head_rows(w):
    return w.reshape(KB, NH // KB, HD, -1).transpose(0, 2, 1, 3).reshape(w.shape)


def v_columns(w):
    return np.concatenate([w.reshape(-1, NH, HD), np.zeros((w.shape[0], NH, VW - HD), np.float32)], 2).reshape(-1, NH * VW)


def v_row(b):
    one = np.zeros((NH, VW - HD), np.float32)
    one[:, 0] = 1.0
    return np.concatenate([b.reshape(NH, HD), one], 1).reshape(-1)


def softmax_layer(wq, bq, wk, bk, wv, bv, wo, bo, rope=False):
    ws = [to_head_rows(wq).T, to_head_rows(wk).T, v_columns(wv.T), wo.T]
    if rope:
        swap = lambda w: w.reshape(NH, 2, HD // 2, -1)[:, ::-1].reshape(w.shape)
        ws += [to_head_rows(swap(wq)).T, to_head_rows(swap(wk)).T]
    cols = np.concatenate([to_head_rows(b[:, None]).reshape(KB, P).T for b in (bq, bk)], 1)
    return (np.ascontiguousarray(np.concatenate(ws, 1)), rows_of(v_row(bv), bo), np.ascontiguousarray(cols))


def constants():
    c = {"ident": np.eye(P, dtype=np.float32)}
    p, x = np.arange(P)[:, None, None], np.arange(NH // KB * (HD + 1))[None, None, :]
    c["kv_mask"] = np.broadcast_to(p // HD == x // (HD + 1), (P, KB, x.size)).astype(np.float32)
    c["iota"] = np.ascontiguousarray(np.broadcast_to(np.arange(16, dtype=np.float32), (TP, CT, 16)))
    rows = P - NSLOT * HD
    hot = np.zeros((rows, GH, 1), np.float32)
    for j in range(GH):
        hot[rows - 2 * GH + j, j] = hot[rows - GH + j, j] = 1.0
    c["hot"] = hot
    c0 = QCH[-1][0]
    p, x = np.arange(TP)[:, None], np.arange(T + c0)[None, :] - c0
    c["alibi_q"] = np.minimum(x - p, 0).astype(np.float32)
    c["alibi_k"] = np.minimum(p - x, 0).astype(np.float32)
    inv = (np.float32(1.0) / np.float32(10000.0) ** (np.arange(0, HD, 2, dtype=np.float32) / np.float32(HD))).astype(np.float32)
    f = (np.arange(T, dtype=np.float32)[None, :] * inv[:, None]).astype(np.float32)
    cos = np.concatenate([np.cos(f), np.cos(f)]).astype(np.float32)
    sin = np.concatenate([-np.sin(f), np.sin(f)]).astype(np.float32)
    c["cos"] = np.repeat(cos, P // HD, 0)
    c["sin"] = np.repeat(sin, P // HD, 0)
    return c


def laid_out(i):
    g = {k: np.asarray(v) for k, v in i.items()}
    a = constants()
    z = np.zeros((D,), np.float32)
    xs = np.zeros((D, B, T), np.float32)
    xs[:, :, 1:] = g["x"][:, 0].transpose(2, 0, 1)
    a["xT"] = xs.reshape(D, TOK)
    a["cls"] = g["cls_tok"].reshape(1, D)
    w, b = g["L0_tok_w_qkv"].reshape(NH, 3, HD, D), g["L0_tok_b_qkv"].reshape(NH, 3, HD)
    a["w_tok"], a["rows_tok"], a["cols_tok"] = softmax_layer(
        w[:, 0].reshape(D, D), b[:, 0].reshape(-1), w[:, 1].reshape(D, D), b[:, 1].reshape(-1),
        w[:, 2].reshape(D, D), b[:, 2].reshape(-1), g["L0_tok_w_out"], g["L0_tok_b_out"])

    def join(*ws):
        return np.concatenate(ws, 1)

    vw = np.concatenate([g["L0_attn_Wv"].T.reshape(D, NH, HD), np.zeros((D, NH, 1), np.float32)], 2).reshape(D, -1)
    vb = np.concatenate([g["L0_attn_bv"].reshape(NH, HD), np.ones((NH, 1), np.float32)], 1).reshape(-1)
    a["w_lin"] = join(g["L0_attn_Wq"].T, g["L0_attn_Wk"].T, vw, g["L0_attn_Wo"].T)
    a["rows_lin"] = rows_of(g["L0_attn_bq"], g["L0_attn_bk"], vb, g["L0_attn_bo"])
    a["cols_lin"] = np.zeros((P, 8), np.float32)
    a["L0_w1"] = join(*(m for e in range(16) for m in (g["L0_ffn_Wg"][e], g["L0_ffn_Wu"][e])),
                      *(m[:, P * n:P * n + P] for n in range(2) for m in (g["L0_ffn_Sg"], g["L0_ffn_Su"])))
    a["L0_w2"] = np.concatenate([g["L0_ffn_Wd"].reshape(-1, D), g["L0_ffn_Sd"]])
    a["L0_rw"] = g["L0_ffn_Wr"]

    w = g["L1_attn_qkv_w"].reshape(3, D, D)
    a["w_rope"], a["rows_rope"], a["cols_rope"] = softmax_layer(
        w[0], z, w[1], z, w[2], z, g["L1_attn_proj_w"], g["L1_attn_proj_b"], rope=True)
    heads = [4 * (2 * (u // 2 // B) + u % 2) + j for u in range(B * NG) for j in range(GH)]
    a["slopes"] = rows_of(g["L1_attn_slopes"][heads])
    a["L1_w1"] = join(*(g["L1_ffn_w13"][e].T for e in range(16)), g["L1_ffn_w13_s"].T)
    a["L1_w2"] = np.concatenate([g["L1_ffn_w2"][e].T for e in range(16)] + [g["L1_ffn_w2_s"].T])
    a["L1_rw"] = g["L1_ffn_gate_w"].T
    a["L1_rb"] = rows_of(g["L1_ffn_gate_b"])

    wi, bi = g["L2_attn_in_proj_w"].T, g["L2_attn_in_proj_b"]
    a["w_seg"] = join(g["L2_attn_proj_qk_w"].T, g["L2_attn_proj_v_w"].T, wi, g["L2_attn_out_proj_w"].T)
    a["rows_seg"] = rows_of(bi, g["L2_attn_out_proj_b"])
    a["cols_seg"] = join(*(b.reshape(KB, P).T for b in (g["L2_attn_proj_qk_b"], g["L2_attn_proj_v_b"])))
    a["L2_w1"] = join(*g["L2_ffn_W1"])
    a["L2_w2"] = g["L2_ffn_W2"].reshape(-1, D)
    a["L2_rw"] = g["L2_ffn_Wg"]
    a["L2_b1"] = g["L2_ffn_b1"].reshape(-1, P).T
    a["L2_b2"] = g["L2_ffn_b2"]

    def shared_heads(w):
        return np.repeat(w.reshape(4, 1, HD, -1), 4, 1).reshape(D, -1)

    a["w_gqa"], a["rows_gqa"], a["cols_gqa"] = softmax_layer(
        g["L3_attn_wq"], g["L3_attn_bq"], shared_heads(g["L3_attn_wk"]), shared_heads(g["L3_attn_bk"])[:, 0],
        shared_heads(g["L3_attn_wv"]), shared_heads(g["L3_attn_bv"])[:, 0], g["L3_attn_wo"], g["L3_attn_bo"])
    a["L3_w1"] = g["L3_ffn_W_fc"].T
    a["L3_w2"] = g["L3_ffn_W_proj"].T
    b1 = np.zeros((P, 32), np.float32)
    b1[:, 0:16] = join(g["L3_ffn_ln_w"].reshape(8, P).T, g["L3_ffn_ln_b"].reshape(8, P).T)
    a["L3_b1"] = b1
    a["L3_b2"] = np.zeros((8, D), np.float32)
    return {k: np.ascontiguousarray(v) for k, v in a.items()}


def kernel(**inputs):
    import concourse.bacc as bacc
    from concourse.bass_utils import run_bass_kernel_spmd

    nc = bacc.Bacc("TRN2", target_bir_lowering=False, num_devices=1)
    arrays, aps = {}, {}
    for name, v in laid_out(inputs).items():
        arrays[f"in_{name}"] = v
        aps[name] = nc.dram_tensor(f"in_{name}", v.shape, mybir.dt.from_np(v.dtype), kind="ExternalInput").ap()
    out = nc.dram_tensor("out", (TOK, D), F32, kind="ExternalOutput").ap()
    build(nc, aps, out)
    r = run_bass_kernel_spmd(nc, [arrays], core_ids=[0])
    return r.results[0]["out"].reshape(B, T, D)
```

```python
from contextlib import ExitStack

import numpy as np

import concourse.bass as bass
from concourse import mybir

F32 = mybir.dt.float32
BF16 = mybir.dt.bfloat16
U32 = mybir.dt.uint32
ALU = mybir.AluOpType
ACT = mybir.ActivationFunctionType
AX = mybir.AxisListType

P = 128
B = 4
S = 512
T = S + 1
D = 256
KB = D // P
TOK = B * T
TP = 114
NT = TOK // TP
CT = 3
CW = CT * TP
NCH = NT // CT
NH = 16
HD = D // NH
VW = 32
GH = 4
NG = NH // GH
NSLOT = 6
BIG = 3.0e38
LN_EPS = 1e-5
SLOTS_Q = (1, 1, 2, 2, 1, 3)
SLOTS_K = (1, 2, 1, 2, 3, 1)
NSTAGE_SEMS = 26

QCH = [(i * TP, min(TP, T - i * TP)) for i in range(-(-T // TP))]
HALF0 = T - 256
W0 = 512 - HALF0
HALVES = ((0, HALF0), (HALF0, 256))

SEG = 4
SH = 8
SHD = D // SH
TS = (T // SEG + 1) * SEG
SP = 86
NSEG = B * TS // SEG
NST = NSEG // SP
SW = SP * SEG


def build(nc, a, out):
    ctx = ExitStack()
    with ctx:
        def sb(name, shape, dt=F32):
            return ctx.enter_context(nc.sbuf_tensor(name, shape, dt))

        def sem(name):
            return ctx.enter_context(nc.semaphore(name))

        H = sb("H", [TP, NT, D])
        XT = sb("XT", [P, KB, TOK])
        ATW = sb("ATW", [P, KB, 1792])
        ROWS = sb("ROWS", [P, 1040])
        COLS = sb("COLS", [P, 8])
        FW1 = sb("FW1", [P, KB, 4608])
        FW2 = sb("FW2", [P, 32, D])
        RW = sb("RW", [P, KB, 16])
        RB = sb("RB", [P, 16])
        B1 = sb("B1", [P, 32])
        B2 = sb("B2", [8, D])
        ident = sb("ident", [P, P])
        iota = sb("iota", [TP, CT, 16])
        eps = sb("eps", [P, 1])
        QSD = nc.dram_tensor("q_stacks", [KB, B, NSLOT, P, T], BF16, kind="Internal").ap()
        KSD = nc.dram_tensor("k_stacks", [KB, B, NSLOT, P, T], BF16, kind="Internal").ap()
        VD = nc.dram_tensor("v_rows", [KB, B, T, NH * VW // KB], F32, kind="Internal").ap()

        attn_loaded = [sem(f"attn_loaded{i}") for i in range(5)]
        ffn_loaded = [sem(f"ffn_loaded{i}") for i in range(4)]
        const_loaded = sem("const_loaded")
        out_stored = sem("out_stored")
        begun = sem("begun")
        pool_of_sems = [sem(f"stage_sem{i}") for i in range(NSTAGE_SEMS)]
        first, last = pool_of_sems[0].num, pool_of_sems[-1].num
        assert last - first == NSTAGE_SEMS - 1

        class Stage:

            number = 0

            def __init__(self):
                Stage.number += 1
                self.prefix = f"stage{Stage.number}_"
                self.taken = 0
                self.mem = ExitStack()

            def sem(self, name):
                self.taken += 1
                return pool_of_sems[self.taken - 1]

            def sb(self, name, shape, dt=F32):
                return self.mem.enter_context(nc.sbuf_tensor(self.prefix + name, shape, dt))

            def psum(self, name, shape, dt=F32):
                return self.mem.enter_context(nc.psum_tensor(self.prefix + name, shape, dt))

            def close(self):
                nc.all_engine_barrier(sems_to_clear=range(first, last + 1))
                self.mem.close()

        def cols_of(ap, t0, n):
            return ap[:, :, bass.ds(t0, n)]

        def load_attn(e, n, w, rows, cols):
            e.dma_start(ATW[:, :, 0:w.shape[1]], w.rearrange("(k p) n -> p k n", p=P)).then_inc(attn_loaded[n], 16)
            e.dma_start(ROWS[:, 0:rows.shape[1]], rows).then_inc(attn_loaded[n], 16)
            e.dma_start(COLS[:, 0:cols.shape[1]], cols).then_inc(attn_loaded[n], 16)

        def load_ffn(e, n, w1, w2, rw=None, rb=None, b1=None, b2=None):
            s = ffn_loaded[n]
            c = 0
            w1v = w1.rearrange("(k p) n -> p k n", p=P)
            w2v = w2.rearrange("(c p) n -> p c n", p=P)
            for k in range(KB):
                e.dma_start(FW1[:, k, 0:w1.shape[1]], w1v[:, k]).then_inc(s, 16)
                c += 16
            e.dma_start(FW2[:, 0:w2v.shape[1], :], w2v).then_inc(s, 16)
            c += 16
            if rw is not None:
                e.dma_start(RW[:, :, 0:rw.shape[1]], rw.rearrange("(k p) n -> p k n", p=P)).then_inc(s, 16)
                c += 16
            if rb is not None:
                e.dma_start(RB[:, 0:rb.shape[1]], rb).then_inc(s, 16)
                c += 16
            if b1 is not None:
                e.dma_start(B1[:, :], b1).then_inc(s, 16)
                e.dma_start(B2[:, :], b2).then_inc(s, 16)
                c += 32
            return c

        class Norm:

            def __init__(self, st, n=CT, signals=1, bufs=1):
                self.n, self.signals, self.bufs = n, signals, bufs
                self.stats = [st.sb(f"ln_stats{r}", [TP, n, 6]) for r in range(bufs)]
                self.mv = [st.sb(f"ln_mv{r}", [TP, n, 2]) for r in range(bufs)]
                self.sd = [st.sb(f"ln_sd{r}", [TP, n]) for r in range(bufs)]
                self.rstd = [st.sb(f"ln_rstd{r}", [TP, n]) for r in range(bufs)]
                self.xn = [st.sb(f"ln_xn{r}", [TP, n, D]) for r in range(bufs)]
                self.var_ready = st.sem("var_ready")
                self.sd_ready = st.sem("sd_ready")
                self.xn_ready = st.sem("xn_ready")
                self.tr_ready = st.sem("tr_ready")
                self.credits = 1 + (bufs - 1) * signals
                self.stats_made = st.sem("stats_made")
                self.rstd_made = st.sem("rstd_made")

            def vector_stats(self, e, k, r=0):
                for j in range(self.n):
                    i = e.bn_stats(self.stats[r][:, j, :], H[:, self.n * k + j, :])
                i.then_inc(self.stats_made, 1)
                e.wait_ge(self.stats_made, k + 1)
                e.sem_inc(begun, 1)
                for j in range(self.n):
                    i = e.bn_aggr(self.mv[r][:, j, :], self.stats[r][:, j, :])
                i.then_inc(self.var_ready, 1)

            def vector_apply(self, e, k, r=0):
                e.wait_ge(self.sd_ready, k + 1)
                e.reciprocal(self.rstd[r][:, :], self.sd[r][:, :]).then_inc(self.rstd_made, 1)
                e.wait_ge(self.rstd_made, k + 1)
                e.wait_ge(self.tr_ready, self.signals * k + 1)
                for j in range(self.n):
                    i = e.tensor_scalar(self.xn[r][:, j, :], H[:, self.n * k + j, :], self.mv[r][:, j, 0:1],
                                        self.rstd[r][:, j:j + 1], ALU.subtract, ALU.mult)
                i.then_inc(self.xn_ready, 1)

            def vector(self, e, k):
                self.vector_stats(e, k)
                self.vector_apply(e, k)

            def scalar(self, e, k, r=0):
                e.wait_ge(self.var_ready, k + 1)
                e.activation(self.sd[r][:, :], self.mv[r][:, :, 1], ACT.Sqrt, bias=eps[0:TP, :])\
                    .then_inc(self.sd_ready, 1)

        def stage_norm():
            st = Stage()
            ln = Norm(st, bufs=2)
            ps = [st.psum(f"tr{r}", [P, KB, 512]) for r in range(2)]
            tr_used = st.sem("tr_used")
            with nc.Block() as block:
                @block.vector
                def _(e):
                    ln.vector_stats(e, 0, 0)
                    with e.Fori(0, NCH // 2 - 1) as i:
                        for r in range(2):
                            ln.vector_stats(e, 2 * i + r + 1, 1 - r)
                            ln.vector_apply(e, 2 * i + r, r)
                    ln.vector_stats(e, NCH - 1, 1)
                    ln.vector_apply(e, NCH - 2, 0)
                    ln.vector_apply(e, NCH - 1, 1)

                @block.scalar
                def _(e):
                    e.sem_inc(tr_used, 2)

                    def copy(k, r):
                        e.wait_ge(ln.tr_ready, ln.credits + k + 1)
                        e.activation(cols_of(XT, k * CW, CW), ps[r][:, :, 0:CW], ACT.Copy).then_inc(tr_used, 1)

                    ln.scalar(e, 0, 0)
                    with e.Fori(0, NCH // 2 - 1) as i:
                        for r in range(2):
                            ln.scalar(e, 2 * i + r + 1, 1 - r)
                            copy(2 * i + r, r)
                    ln.scalar(e, NCH - 1, 1)
                    copy(NCH - 2, 0)
                    copy(NCH - 1, 1)

                @block.tensor
                def _(e):
                    e.sem_inc(ln.tr_ready, ln.credits)
                    with e.Fori(0, NCH // 2) as i:
                        for r in range(2):
                            k = 2 * i + r
                            e.wait_ge(ln.xn_ready, k + 1)
                            e.wait_ge(tr_used, k + 1)
                            for kb in range(KB):
                                for j in range(CT):
                                    t = e.transpose(ps[r][:, kb, TP * j:TP * j + TP],
                                                    ln.xn[r][:, j, kb * P:kb * P + P], ident[0:TP, 0:TP])
                            t.then_inc(ln.tr_ready, 1)
            st.close()

        def stage_project(wcol, bcol, first_layer, prefetch):
            st = Stage()
            xs = [st.sb(f"xs{r}", [P, KB, TP]) for r in range(2)]
            tmp = [st.sb(f"tmp{r}", [TP, D]) for r in range(2)]
            ps = [st.psum(f"o{r}", [TP, 512]) for r in range(2)]
            xs_ready = st.sem("xs_ready")
            o_ready = st.sem("o_ready")
            o_used = st.sem("o_used")
            t_used = st.sem("t_used")
            with nc.Block() as block:
                @block.scalar
                def _(e):
                    with e.Fori(0, NT // 2) as i:
                        for r in range(2):
                            t = 2 * i + r
                            e.wait_ge(o_ready, t + 1)
                            e.activation(xs[r][:, :, :], cols_of(XT, t * TP, TP), ACT.Copy).then_inc(xs_ready, 1)

                @block.tensor
                def _(e):
                    e.sem_inc(o_ready, 2)
                    with e.Fori(0, NT // 2) as i:
                        for r in range(2):
                            t = 2 * i + r
                            e.wait_ge(xs_ready, t + 1)
                            e.wait_ge(o_used, t + 1)
                            for kb in range(KB):
                                m = e.matmul(ps[r][:, 0:D], xs[r][:, kb, :], ATW[:, kb, wcol:wcol + D],
                                             start=kb == 0, stop=kb == KB - 1)
                            m.then_inc(o_ready, 1)

                @block.vector
                def _(e):
                    e.sem_inc(o_used, 2)
                    with e.Fori(0, NT // 2) as i:
                        for r in range(2):
                            t = 2 * i + r
                            e.wait_ge(o_ready, 2 + t + 1)
                            if first_layer:
                                e.tensor_tensor(H[:, t, :], ps[r][:, 0:D], ROWS[0:TP, bcol:bcol + D], ALU.add)\
                                    .then_inc(o_used, 1)
                            else:
                                e.wait_ge(t_used, t + 1)
                                e.tensor_tensor(tmp[r][:, :], ps[r][:, 0:D], ROWS[0:TP, bcol:bcol + D], ALU.add)\
                                    .then_inc(o_used, 1)

                @block.gpsimd
                def _(e):
                    if not first_layer:
                        e.sem_inc(t_used, 2)
                        with e.Fori(0, NT // 2) as i:
                            for r in range(2):
                                t = 2 * i + r
                                e.wait_ge(o_used, 2 + t + 1)
                                e.tensor_tensor(H[:, t, :], H[:, t, :], tmp[r][:, :], ALU.add).then_inc(t_used, 1)
            st.close()
            if first_layer:
                st = Stage()
                cls_in = st.sem("cls_in")
                with nc.Block() as block:
                    @block.sync
                    def _(e):
                        for b in range(B):
                            p, t = (b * T) % TP, (b * T) // TP
                            e.dma_start(H[p:p + 1, t, :], a["cls"]).then_inc(cls_in, 16)
                        e.wait_ge(cls_in, 16 * B)
                        prefetch(e)
                st.close()
            else:
                with nc.Block() as block:
                    @block.sync
                    def _(e):
                        prefetch(e)

        def stage_qkv(layer, rope):
            st = Stage()
            cos = st.sb("cos", [P, T]) if rope else None
            sin = st.sb("sin", [P, T]) if rope else None
            xf = [st.sb(f"xf{r}", [P, T]) for r in range(2)]
            rot = [st.sb(f"rot{r}", [P, T]) for r in range(2)] if rope else None
            rest = [st.sb(f"rest{r}", [P, T]) for r in range(2)]
            parts = [[st.sb(f"part{n}_{r}", [P, KB, T], BF16) for n in range(3)] for r in range(2)]
            xb = st.sb("xb", [P, KB, T])
            vs = [st.sb(f"vs{c}", [TP, NH * VW]) for c in range(len(QCH))]
            pq = [st.psum(f"pq{r}", [P, 1024]) for r in range(2)]
            pr = st.psum("pr", [P, 1024])
            pv = [st.psum(f"pv{r}", [TP, 512]) for r in range(2)]
            tab_in = st.sem("tab_in")
            q_ready = st.sem("q_ready")
            r_ready = st.sem("r_ready")
            q_used = st.sem("q_used")
            r_used = st.sem("r_used")
            x_ready = st.sem("x_ready")
            p1_ready = st.sem("p1_ready")
            r1_ready = st.sem("r1_ready")
            p2_ready = st.sem("p2_ready")
            p3_ready = st.sem("p3_ready")
            half = [st.sem(f"stack_out{r}") for r in range(2)]
            xb_ready = st.sem("xb_ready")
            xb_used = st.sem("xb_used")
            v_ready = st.sem("v_ready")
            v_used = st.sem("v_used")
            v_out = st.sem("v_out")
            NV = len(QCH)
            SLOT_DMA = 16 * NSLOT
            ORDER = [("qk", 0), ("qk", 1), ("v", 0), ("qk", 2), ("v", 1), ("qk", 3)] + [("v", c) for c in range(2, NV)]

            with nc.Block() as block:
                @block.tensor
                def _(e):
                    e.wait_ge(attn_loaded[layer], 48)
                    e.sem_inc(xb_used, 1)
                    with e.Fori(0, B) as b:
                        for what, n in ORDER:
                            if what == "v":
                                q0, qn = QCH[n]
                                if n == 0:
                                    e.wait_ge(xb_ready, b + 1)
                                e.wait_ge(v_used, (NV + 1) * b + n + 1)
                                for kb in range(KB):
                                    m = e.matmul(pv[n % 2][0:qn, :], xb[:, kb, q0:q0 + qn], ATW[:, kb, 512:1024],
                                                 start=kb == 0, stop=kb == KB - 1)
                                m.then_inc(v_ready, 1)
                                continue
                            r = n % 2
                            e.wait_ge(q_used, 4 * b + n + 1)
                            for h0, hw in HALVES:
                                for kb in range(KB):
                                    m = e.matmul(pq[r][:, W0 + h0:W0 + h0 + hw], ATW[:, kb, n * P:n * P + P],
                                                 XT[:, kb, bass.ds(b * T + h0, hw)],
                                                 start=kb == 0, stop=kb == KB - 1)
                            m.then_inc(q_ready, 1)
                            if rope:
                                e.wait_ge(r_used, 4 * b + n + 1)
                                for h0, hw in HALVES:
                                    for kb in range(KB):
                                        m = e.matmul(pr[:, W0 + h0:W0 + h0 + hw],
                                                     ATW[:, kb, 1280 + n * P:1280 + n * P + P],
                                                     XT[:, kb, bass.ds(b * T + h0, hw)],
                                                     start=kb == 0, stop=kb == KB - 1)
                                m.then_inc(r_ready, 1)
                        e.wait_ge(v_ready, (NV + 1) * b + NV)
                        e.sem_inc(v_ready, 1)
                        e.sem_inc(xb_used, 1)

                @block.gpsimd
                def _(e):
                    with e.Fori(0, B) as b:
                        e.wait_ge(xb_used, b + 1)
                        e.tensor_copy(xb[:, :, :], cols_of(XT, b * T, T)).then_inc(xb_ready, 1)

                @block.scalar
                def _(e):
                    e.wait_ge(attn_loaded[layer], 48)
                    if not rope:
                        e.sem_inc(q_used, 2)
                    with e.Fori(0, B) as b:
                        for n in range(4):
                            r, m, qk = n % 2, n % 2, n // 2
                            u = 4 * b + n
                            if rope:
                                e.wait_ge(x_ready, u + 1)
                            else:
                                e.wait_ge(q_ready, u + 1)
                                e.wait_ge(p3_ready, u + 1)
                                e.activation(xf[r][:, :], pq[r][:, W0:W0 + T], ACT.Identity,
                                             bias=COLS[:, n:n + 1]).then_inc(q_used, 1)
                                e.wait_ge(q_used, 2 + u + 1)
                            if m == 0:
                                e.wait_ge(half[qk], SLOT_DMA * b + 1)
                            e.activation(parts[qk][0][:, m, :], xf[r][:, :], ACT.Copy).then_inc(p1_ready, 1)
                            e.wait_ge(r1_ready, u + 1)
                            e.activation(parts[qk][1][:, m, :], rest[r][:, :], ACT.Copy).then_inc(p2_ready, 1)

                @block.vector
                def _(e):
                    e.sem_inc(v_used, 2)
                    e.sem_inc(p3_ready, 2)
                    e.wait_ge(attn_loaded[layer], 48)
                    if rope:
                        e.sem_inc(q_used, 2)
                        e.sem_inc(r_used, 1)
                        e.wait_ge(tab_in, 32)
                    with e.Fori(0, B) as b:
                        for what, n in ORDER:
                            if what == "v":
                                q0, qn = QCH[n]
                                e.wait_ge(v_ready, (NV + 1) * b + n + 1)
                                if n == 0:
                                    e.wait_ge(v_out, 16 * NV * b + 1)
                                e.tensor_tensor(vs[n][0:qn, :], pv[n % 2][0:qn, :], ROWS[0:qn, 0:512], ALU.add)\
                                    .then_inc(v_used, 1)
                                continue
                            r, m, qk = n % 2, n % 2, n // 2
                            u = 4 * b + n
                            if rope:
                                e.wait_ge(q_ready, u + 1)
                                e.tensor_tensor(xf[r][:, :], pq[r][:, W0:W0 + T], cos[:, :], ALU.mult)\
                                    .then_inc(q_used, 1)
                                e.wait_ge(r_ready, u + 1)
                                e.tensor_tensor(rot[r][:, :], pr[:, W0:W0 + T], sin[:, :], ALU.mult)\
                                    .then_inc(r_used, 1)
                                e.wait_ge(q_used, 2 + u + 1)
                                e.wait_ge(r_used, 1 + u + 1)
                                e.tensor_tensor(xf[r][:, :], xf[r][:, :], rot[r][:, :], ALU.add).then_inc(x_ready, 1)
                                e.wait_ge(x_ready, u + 1)
                            e.wait_ge(p1_ready, u + 1)
                            e.tensor_tensor(rest[r][:, :], xf[r][:, :], parts[qk][0][:, m, :], ALU.subtract)\
                                .then_inc(r1_ready, 1)
                            e.wait_ge(p2_ready, u + 1)
                            e.wait_ge(r1_ready, u + 1)
                            if m == 0:
                                e.wait_ge(half[qk], SLOT_DMA * b + 1)
                            e.tensor_tensor(parts[qk][2][:, m, :], rest[r][:, :], parts[qk][1][:, m, :], ALU.subtract)\
                                .then_inc(p3_ready, 1)
                        e.wait_ge(v_used, 2 + (NV + 1) * b + NV)
                        e.wait_ge(v_ready, (NV + 1) * (b + 1))
                        e.sem_inc(v_used, 1)

                @block.sync
                def _(e):
                    if rope:
                        e.dma_start(cos[:, :], a["cos"]).then_inc(tab_in, 16)
                        e.dma_start(sin[:, :], a["sin"]).then_inc(tab_in, 16)
                    for r in range(2):
                        e.sem_inc(half[r], 1)
                    e.sem_inc(v_out, 1)
                    with e.Fori(0, B) as b:
                        def stack_out(qk):
                            dst, slots = ((QSD, SLOTS_Q), (KSD, SLOTS_K))[qk]
                            e.wait_ge(p3_ready, 2 + 4 * b + 2 * qk + 2)
                            e.sem_inc(begun, 1)
                            e.wait_ge(p2_ready, 4 * b + 2 * qk + 2)
                            e.wait_ge(p1_ready, 4 * b + 2 * qk + 2)
                            for s in range(NSLOT):
                                e.dma_start(dst[:, :, s].rearrange("m b p t -> b p m t")[b],
                                            parts[qk][slots[s] - 1][:, :, :]).then_inc(half[qk], 16)

                        for what, n in ORDER:
                            if what == "qk" and n % 2:
                                stack_out(n // 2)
                            if what == "v":
                                q0, qn = QCH[n]
                                e.wait_ge(v_used, 2 + (NV + 1) * b + n + 1)
                                e.dma_start(VD.rearrange("m b t c -> b t m c")[b, q0:q0 + qn],
                                            vs[n][0:qn, :].rearrange("p (m c) -> p m c", m=KB)).then_inc(v_out, 16)
                    for r in range(2):
                        e.wait_ge(half[r], B * SLOT_DMA + 1)
                    e.wait_ge(v_out, B * 16 * NV + 1)
            st.close()

        def stage_attn(k0, alibi):
            st = Stage()
            NU = B * NG
            nk = T - k0
            KCH = [(c, min(P, T - c)) for c in range(k0, T, P)]
            NC = len(KCH)
            over = KCH[-1][1] == 1
            N2 = (NC - over) * GH + over
            KHALF = ((1, 512),) if k0 else HALVES
            KHN = len(KHALF)
            QP = [(q, min(P, T - q)) for q in range(0, T, P)]
            NQ = len(QP)
            NB = GH + 1
            KOV = HALVES if k0 == 0 else ((1, 256), (257, 256))
            items1 = [(i, j, h) for j in range(GH) for i in range(NQ - 1) for h in range(KHN)]
            items1 += [(NQ - 1, 0, h) for h in range(2)]
            NI = len(items1)
            N1 = NI + 2
            OWN = 3
            R0 = NSLOT * HD
            R1 = P
            RA = R1 - R0
            RP = R1 - 2 * GH
            PA = RA // GH - 2
            MT = ((0, 2), (2, NQ))

            QS = [st.sb(f"QS{r}", [P, GH, T], BF16) for r in range(2)]
            KS = [st.sb(f"KS{r}", [P, GH, T], BF16) for r in range(2)]
            VG = [st.sb(f"VG{r}", [P, NC - over, GH * VW]) for r in range(2)]
            KL = [st.sb(f"KL{r}", [P, GH, VW], BF16) for r in range(2)]
            VL = [st.sb(f"VL{r}", [P, GH * VW]) for r in range(2)]
            E = [st.sb(f"E{n}", [P, T]) for n in range(2 * GH)]
            OU = st.sb("OU", [P, T])
            ON = st.sb("ON", [TP, len(QCH), GH, HD])
            rec = st.sb("rec", [TP, len(QCH), GH])
            mx = st.sb("mx", [P, NQ, GH, 2])
            M = st.sb("M", [P, NQ, RA // GH, GH])
            m1 = st.sb("m1", [P, NQ, GH], BF16)
            ML = st.sb("ML", [P, RA // GH, GH])
            over_rows = st.sb("over_rows", [P, GH + 1])
            hot = st.sb("hot", [P, GH, 1])
            slot = [st.psum(f"slot{r}", [P, 512]) for r in range(2)]
            S2 = [st.psum(f"S2_{r}", [P, 1024]) for r in range(2)]
            AV = st.psum("AV", [P, 1024])
            if alibi:
                D1 = st.sb("D1", [P, 2 * T - (T - QCH[-1][0])])
                D2 = st.sb("D2", [P, 2 * T - (T - QCH[-1][0])])
                slopes = st.sb("slopes", [P, NU * GH])
                slopes4 = st.sb("slopes4", [P, NU * GH])
                SL = [st.sb(f"SL{r}", [P, GH]) for r in range(2)]
                G1 = st.sb("G1", [P, GH, 2 * T - (T - QCH[-1][0])])
                scr = [st.sb(f"scr{r}", [P, HALF0]) for r in range(2)]
                DL = st.sb("DL", [P, T])
                slopes_over = st.sb("slopes_over", [P, NU])
                slopes_over4 = st.sb("slopes_over4", [P, NU])
                SO = st.sb("SO", [P, 1])
                GL = st.sb("GL", [P, T])
            C0 = QCH[-1][0]

            loaded = [st.sem(f"loaded{r}") for r in range(2)]
            v_loaded = [st.sem(f"v_loaded{r}") for r in range(2)]
            slot_ready = st.sem("slot_ready")
            slot_used = st.sem("slot_used")
            s2_ready = st.sem("s2_ready")
            e_ready = st.sem("e_ready")
            e_used = st.sem("e_used")
            ou_ready = st.sem("ou_ready")
            on_ready = st.sem("on_ready")
            m_ready = st.sem("m_ready")
            hot_ready = st.sem("hot_ready")
            own = st.sem("own")
            own_o = st.sem("own_o")
            if alibi:
                g_ready = st.sem("g_ready")
                g_used = st.sem("g_used")
                sa_ready = st.sem("sa_ready")
                pool_own = st.sem("pool_own")
                tables_in = st.sem("tables_in")

            def slots_before(u, mid):
                if mid:
                    return u * (N1 + 4) + (N1 - 4)
                return {-1: 0, 0: N1}.get(u, NU * N1 + (u - 1) * 4)

            def steps(e, step):
                step(-1, 1, -1, slots_before(-1, False), True, False, False)
                step(0, 0, 0, slots_before(0, False), True, True, False)
                with e.Fori(0, (NU - 2) // 2) as i:
                    step(2 * i + 1, 1, i, slots_before(2 * i + 1, True), True, True, True)
                    step(2 * i + 2, 0, i + 1, slots_before(2 * i + 2, True), True, True, True)
                step(NU - 1, 1, NU // 2 - 1, slots_before(NU - 1, False), False, True, True)
                step(NU, 0, NU // 2, slots_before(NU, False), False, False, True)

            P0, P1 = 3 if alibi else 4, N2 - 2

            def plan(do1, do2, do3):
                out, n1 = [], 0
                def pass1(until):
                    nonlocal n1
                    while do1 and n1 < NI and n1 * (P1 - P0) < NI * (until - P0):
                        out.append(("p1",) + items1[n1])
                        n1 += 1

                for s in range(N2):
                    pass1(s + 0.5)
                    if do1 and s == P1:
                        out.append(("mm",))
                    if do1 and s == P1 + 1:
                        out.append(("mt",))
                    if s == 0 and do3:
                        out.append(("av_last",))
                    if do2:
                        out.append(("s2", s // GH, s % GH))
                    pass1(s + 1)
                    if s % GH in (1, 2) and s > GH and do2:
                        out.append(("av", s // GH - 1, s % GH - 1))
                    if s == 1 and do3:
                        out.append(("o1",))
                    if s == (GH if alibi else GH + 3) and do3:
                        out.append(("o2",))
                return out

            def maxima_rows(copy, r, ps, i0, i1):
                q0, q1 = QP[i0][0], sum(QP[i1 - 1])
                return copy(QS[r][R0:R1, :, q0:q1], ps[0:RA, 0:q1 - q0].rearrange("p (o t) -> p o t", o=1)
                            .to_broadcast([RA, GH, q1 - q0]))

            with nc.Block() as block:
                @block.sync
                def _(e):
                    e.dma_start(hot[R0:R1, :, :], a["hot"]).then_inc(hot_ready, 16)
                    e.dma_start(over_rows[:, :], a["over_rows"]).then_inc(hot_ready, 16)
                    if alibi:
                        e.dma_start(D1[:, :], a["alibi_q"]).then_inc(tables_in, 16)
                        e.dma_start(D2[:, :], a["alibi_k"]).then_inc(tables_in, 16)
                        e.dma_start(slopes[:, :], a["slopes"]).then_inc(tables_in, 16)
                        e.dma_start(slopes_over[:, :], a["slopes_over"]).then_inc(tables_in, 16)
                        e.dma_start(DL[:, :], a["alibi_over"]).then_inc(tables_in, 16)
                    def load(i, r, again):
                        if again:
                            e.wait_ge(s2_ready, (2 * i + r - 1) * N2)
                        for dst, src in ((QS, QSD), (KS, KSD)):
                            e.dma_start(dst[r][0:R0, :, :], src.rearrange(
                                "m b s (d g j) t -> (m b) (s d) g j t", d=HD, j=GH)[i, :, r]).then_inc(loaded[r], 16)
                        if again:
                            e.wait_ge(ou_ready, 2 * i + r + 1)
                        v = VD.rearrange("m b t c -> (m b) t c")
                        c0, cn = KCH[0][0], KCH[0][1]
                        full = NC - over
                        e.dma_start(VG[r][0:cn, 0:full, :],
                                    v[i, c0:c0 + full * cn, r * P:r * P + P].rearrange("(c t) f -> t c f", t=cn))\
                            .then_inc(v_loaded[r], 16)
                        for j in range(GH * over):
                            e.dma_start(VL[r][VW * j + VW - 1:VW * j + VW, VW * j:VW * j + VW],
                                        v[i, T - 1:T, r * P + VW * j:r * P + VW * j + VW]).then_inc(v_loaded[r], 16)

                    if over:
                        e.wait_ge(own, 2)
                    load(0, 0, False)
                    load(0, 1, False)
                    with e.Fori(1, NU // 2) as i:
                        load(i, 0, True)
                        load(i, 1, True)

                LD = 32
                VLD = 16 + 16 * GH * over

                @block.tensor
                def _(e):
                    e.sem_inc(e_used, 2)
                    e.wait_ge(own, 2)

                    def step(u, r, pair, n0, do1, do2, do3):
                        n = 0
                        r1 = 1 - r
                        pair1 = pair + (1 if r else 0)

                        def next_slot():
                            nonlocal n
                            e.wait_ge(slot_used, n0 + n + 1)
                            n += 1
                            return slot[(n - 1) % 2]

                        def values(u, r, c, h):
                            c0, cn = KCH[c]
                            if h == 0:
                                e.wait_ge(e_ready, 2 + u * N2 + min(c * GH + GH, N2))
                                if c == 0:
                                    e.wait_ge(ou_ready, u + 2)
                                e.sem_inc(begun, 1)
                            for h0, hw in HALVES[h:h + 1]:
                                if over and c == NC - 1:
                                    m = e.matmul(AV[:, W0 + h0:W0 + h0 + hw], VL[r][:, :],
                                                 E[(r * NC + c) % 2 * GH][:, h0:h0 + hw], start=False, stop=True)
                                    continue
                                for j in range(GH):
                                    m = e.matmul(AV[VW * j:VW * j + VW, W0 + h0:W0 + h0 + hw],
                                                 VG[r][0:cn, c, VW * j:VW * j + VW],
                                                 E[(r * NC + c) % 2 * GH + j][0:cn, h0:h0 + hw],
                                                 start=c == 0, stop=c == NC - 1)
                            if h == 1:
                                m.then_inc(e_used, 1)

                        for what, *x in plan(do1, do2, do3):
                            if what == "p1":
                                i, j, h = x
                                q0, qn = QP[i]
                                if i == j == h == 0:
                                    e.wait_ge(loaded[r1], LD * (pair1 + 1))
                                if i == NQ - 1:
                                    h0, hw = KOV[h]
                                    ps = next_slot()
                                    e.sem_inc(begun, 1)
                                    for j in range(GH):
                                        m = e.matmul(ps[VW * j:VW * j + VW, 0:hw], QS[r1][0:RP, j, T - VW:T],
                                                     KS[r1][0:RP, j, h0:h0 + hw], start=True, stop=True)
                                    m.then_inc(slot_ready, 1)
                                    continue
                                for h0, hw in KHALF[h:h + 1]:
                                    ps = next_slot()
                                    e.matmul(ps[0:qn, 0:hw], QS[r1][0:RP, j, q0:q0 + qn],
                                             KS[r1][0:RP, j, h0:h0 + hw], start=True, stop=True).then_inc(slot_ready, 1)
                            if what == "mt":
                                e.wait_ge(m_ready, u + 2)
                                for i0, i1 in MT:
                                    ps = next_slot()
                                    e.sem_inc(begun, 1)
                                    for i in range(i0, i1):
                                        q0, qn = QP[i]
                                        q0 -= QP[i0][0]
                                        if i == NQ - 1:
                                            m = e.matmul(ps[0:RA, q0:q0 + 1], ML[:, :, :].rearrange("p a b -> p (a b)"),
                                                         over_rows[:, GH:GH + 1], start=True, stop=True)
                                            continue
                                        m = e.transpose(ps[0:RA, q0:q0 + qn],
                                                        M[0:qn, i, :, :].rearrange("p a b -> p (a b)"), ident[0:qn, 0:qn])
                                    m.then_inc(slot_ready, 1)
                            if what == "o1":
                                e.wait_ge(ou_ready, 2 + u)
                                ps = next_slot()
                                for i in range(len(QCH) - 1):
                                    m = e.transpose(ps[0:TP, P * i:P * i + P], OU[:, TP * i:TP * i + TP], ident[:, :])
                                m.then_inc(slot_ready, 1)
                                q0, qn = QCH[-1]
                                ps = next_slot()
                                e.sem_inc(begun, 1)
                                e.transpose(ps[0:qn, 0:P], OU[:, q0:q0 + qn], ident[:, :]).then_inc(slot_ready, 1)
                            if what == "o2":
                                e.wait_ge(on_ready, 1 + u)
                                ps = next_slot()
                                e.sem_inc(begun, 1)
                                for i in range(len(QCH) - 1):
                                    m = e.transpose(ps[0:GH * HD, TP * i:TP * i + TP],
                                                    ON[:, i, :, :].rearrange("p a b -> p (a b)"), ident[0:TP, 0:TP])
                                m.then_inc(slot_ready, 1)
                                q0, qn = QCH[-1]
                                ps = next_slot()
                                e.sem_inc(begun, 1)
                                e.transpose(ps[0:GH * HD, 0:qn],
                                            ON[0:qn, len(QCH) - 1, :, :].rearrange("p a b -> p (a b)"),
                                            ident[0:qn, 0:qn]).then_inc(slot_ready, 1)
                            if what == "s2":
                                c, j = x
                                c0, cn = KCH[c]
                                s = c * GH + j
                                if s == 0:
                                    e.wait_ge(slot_used, 2 + n0)
                                    e.wait_ge(v_loaded[r], VLD * (pair + 1))
                                e.wait_ge(e_ready, u * N2 + s + 1)
                                tile = S2[(r * N2 + s) % 2]
                                for h0, hw in HALVES:
                                    if over and c == NC - 1:
                                        e.sem_inc(begun, 1)
                                        for j in range(GH):
                                            m = e.matmul(tile[VW * j:VW * j + VW, W0 + h0:W0 + h0 + hw], KL[r][0:R1, j, :],
                                                         QS[r][0:R1, j, h0:h0 + hw], start=True, stop=True)
                                        continue
                                    m = e.matmul(tile[0:cn, W0 + h0:W0 + h0 + hw], KS[r][0:R1, j, c0:c0 + cn],
                                                 QS[r][0:R1, j, h0:h0 + hw], start=True, stop=True)
                                m.then_inc(s2_ready, 1)
                            if what == "av":
                                values(u, r, x[0], x[1])
                            if what == "av_last":
                                for c in range(NC - 1 - over, NC):
                                    values(u - 1, r1, c, 0)
                                    values(u - 1, r1, c, 1)
                    steps(e, step)

                @block.vector
                def _(e):
                    e.memset(M[:, :, :, :], 0.0)
                    e.memset(mx[:, :, :, 0:1], 0.0)
                    e.memset(mx[:, NQ - 1, :, 1:2], 0.0)
                    e.memset(mx[:, 0:NQ - 1, :, 1:2], -BIG)
                    e.memset(ML[:, :, :], 0.0)
                    e.sem_inc(slot_used, 2)
                    e.wait_ge(hot_ready, 32)
                    e.sem_inc(on_ready, 1)
                    for r in range(2):
                        e.memset(KL[r][:, :, :], 0.0)
                        e.memset(VL[r][:, :], 0.0)
                        e.memset(QS[r][R0:R1, :, :], 0.0)
                        e.tensor_copy(KS[r][R0:R1, :, :], hot[R0:R1, :, :].to_broadcast([RA, GH, T])).then_inc(own, 1)
                    if alibi:
                        e.wait_ge(tables_in, 80)
                        e.sem_inc(g_used, 1)

                    def step(u, r, pair, n0, do1, do2, do3):
                        n = 0

                        def next_slot():
                            nonlocal n
                            e.wait_ge(slot_ready, n0 + n + 1)
                            n += 1
                            return slot[(n - 1) % 2]

                        for what, *x in plan(do1, do2, do3):
                            if what == "p1":
                                i, j, h = x
                                q0, qn = QP[i]
                                if i == NQ - 1 and alibi:
                                    h0, hw = KOV[h]
                                    if h == 0:
                                        e.wait_ge(slot_used, 2 + n0 + n)
                                        e.sem_inc(g_used, 1)
                                        e.wait_ge(g_ready, NB * (u + 1) + NB)
                                    ps = next_slot()
                                    e.wait_ge(slot_used, n0 + n)
                                    e.sem_inc(begun, 1)
                                    e.tensor_tensor_reduce(scr[n % 2][:, 0:hw], ps[:, 0:hw], GL[:, h0:h0 + hw], 1.0, -BIG,
                                                           ALU.add, ALU.max, mx[:, i, 0, h:h + 1]).then_inc(slot_used, 1)
                                    continue
                                if i == NQ - 1:
                                    ps = next_slot()
                                    e.tensor_reduce(mx[:, i, 0, h:h + 1], ps[:, 0:KOV[h][1]], AX.X, ALU.max)\
                                        .then_inc(slot_used, 1)
                                    continue
                                if alibi and i == h == 0:
                                    if j:
                                        e.wait_ge(slot_used, 2 + n0 + n)
                                        e.sem_inc(g_used, 1)
                                    e.wait_ge(g_ready, NB * (u + 1) + j + 1)
                                for h0, hw in KHALF[h:h + 1]:
                                    ps = next_slot()
                                    if alibi:
                                        e.wait_ge(slot_used, n0 + n)
                                        e.sem_inc(begun, 1)
                                        e.tensor_tensor_reduce(scr[n % 2][0:qn, 0:hw], ps[0:qn, 0:hw],
                                                               G1[0:qn, j, C0 - q0 + h0:C0 - q0 + h0 + hw], 1.0, -BIG,
                                                               ALU.add, ALU.max, mx[0:qn, i, j, h:h + 1]).then_inc(slot_used, 1)
                                    else:
                                        e.tensor_reduce(mx[0:qn, i, j, h:h + 1], ps[0:qn, 0:hw], AX.X, ALU.max)\
                                            .then_inc(slot_used, 1)
                            if what == "mm":
                                e.wait_ge(slot_used, 2 + n0 + n)
                                e.tensor_reduce(M[:, :, PA, :], mx[:, :, :, :], AX.X, ALU.max, negate=True).then_inc(own, 1)
                                e.wait_ge(own, 2 + OWN * (u + 1) + 1)
                                e.tensor_copy(m1[:, :, :], M[:, :, PA, :]).then_inc(own, 1)
                                e.wait_ge(own, 2 + OWN * (u + 1) + 2)
                                e.tensor_tensor(M[:, :, PA + 1, :], M[:, :, PA, :], m1[:, :, :], ALU.subtract)\
                                    .then_inc(own, 1)
                                e.wait_ge(own, 2 + OWN * (u + 1) + 3)
                                for part in range(PA, PA + 2):
                                    m = e.tensor_scalar(ML[:, part, :], over_rows[:, 0:GH], M[:, NQ - 1, part, 0:1],
                                                        None, ALU.mult)
                                m.then_inc(m_ready, 1)
                                if alibi:
                                    e.sem_inc(g_used, 1)
                            if what == "mt":
                                ps = next_slot()
                                if over:
                                    e.wait_ge(loaded[1 - r], LD * (pair + (1 if r else 0) + 1))
                                    e.tensor_copy(KL[1 - r][:, :, VW - 1], KS[1 - r][:, :, T - 1])
                                maxima_rows(e.tensor_copy, 1 - r, ps, *MT[0]).then_inc(slot_used, 1)
                                n += 1
                            if what == "o1":
                                last = len(QCH) - 1
                                for k, (i0, i1, qn) in enumerate(((0, last, TP), (last, last + 1, QCH[-1][1]))):
                                    ps = next_slot()
                                    v = ps[0:qn, 0:P * (i1 - i0)].rearrange("p (i j c) -> p i j c", i=i1 - i0, j=GH)
                                    e.reciprocal(rec[0:qn, i0:i1, :], v[:, :, :, HD]).then_inc(own_o, 1)
                                    e.wait_ge(own_o, 2 * (u - 1) + k + 1)
                                    rb = rec[0:qn, i0:i1, :].rearrange("p i (j o) -> p i j o", o=1)
                                    e.tensor_tensor(ON[0:qn, i0:i1, :, :].rearrange("p i j c -> p (i j) c"),
                                                    v[:, :, :, 0:HD].rearrange("p i j c -> p (i j) c"),
                                                    rb.rearrange("p i j o -> p (i j) o").to_broadcast([qn, (i1 - i0) * GH, HD]),
                                                    ALU.mult).then_inc(slot_used, 1)
                                e.wait_ge(slot_used, 2 + n0 + n)
                                e.sem_inc(on_ready, 1)
                            if what == "o2":
                                rr = 1 - r
                                flat = XT[:, :, :].rearrange("p k t -> p (k t)")
                                base = (pair - (1 if r == 0 else 0)) * T
                                for i0, i1 in ((0, C0), (C0, T)):
                                    ps = next_slot()
                                    e.tensor_copy(flat[64 * rr:64 * rr + 64, bass.ds(base + i0, i1 - i0)],
                                                  ps[0:64, 0:i1 - i0]).then_inc(slot_used, 1)
                            if what == "s2" and alibi:
                                c, j = x
                                if over and c == NC - 1:
                                    continue
                                c0, cn = KCH[c]
                                s = c * GH + j
                                e.wait_ge(s2_ready, u * N2 + s + 1)
                                if c == j == 0:
                                    e.wait_ge(g_ready, NB * u + 1)
                                v = S2[(r * N2 + s) % 2][0:cn, W0 + c0:W0 + T]
                                e.scalar_tensor_tensor(out=v, in0=D2[0:cn, C0:C0 + T - c0],
                                                       scalar=SL[r][0:cn, j:j + 1], in1=v,
                                                       op0=ALU.mult, op1=ALU.add).then_inc(sa_ready, 1)
                    steps(e, step)

                @block.scalar
                def _(e):
                    e.sem_inc(e_ready, 2)
                    e.sem_inc(ou_ready, 2)

                    def step(u, r, pair, n0, do1, do2, do3):
                        for c in range(NC):
                            c0, cn = KCH[c]
                            if c == 0 and do3:
                                e.wait_ge(e_used, 2 + u * NC)
                                e.wait_ge(on_ready, u)
                                e.activation(OU[:, :], AV[:, W0:W0 + T], ACT.Copy).then_inc(ou_ready, 1)
                            if not do2:
                                continue
                            e.wait_ge(e_used, u * NC + c + 1)
                            alone = over and c == NC - 1
                            if alone:
                                cn = P
                            for j in range(1 if alone else GH):
                                s = c * GH + j
                                if alibi and not alone:
                                    e.wait_ge(sa_ready, u * (N2 - over) + s + 1)
                                else:
                                    e.wait_ge(s2_ready, u * N2 + s + 1)
                                e.activation(E[(r * NC + c) % 2 * GH + j][0:cn, :],
                                             S2[(r * N2 + s) % 2][0:cn, W0:W0 + T], ACT.Exp,
                                             scale=HD ** -0.5).then_inc(e_ready, 1)
                        if do1:
                            e.wait_ge(slot_ready, n0 + N1 + (4 if do3 else 0))
                            maxima_rows(lambda out, x: e.activation(out, x, ACT.Copy), 1 - r, slot[1], *MT[1]).then_inc(slot_used, 1)
                    steps(e, step)

                @block.gpsimd
                def _(e):
                    if alibi:
                        e.wait_ge(tables_in, 80)
                        e.tensor_scalar(slopes4[:, :], slopes[:, :], 8.0 * HD ** 0.5, None, ALU.mult).then_inc(pool_own, 1)
                        e.wait_ge(pool_own, 1)
                        e.tensor_scalar(slopes_over4[:, :], slopes_over[:, :], 8.0 * HD ** 0.5, None, ALU.mult)\
                            .then_inc(pool_own, 1)
                        e.wait_ge(pool_own, 2)

                    def step(u, r, pair, n0, do1, do2, do3):
                        if not (do1 and alibi):
                            return
                        r1 = 1 - r
                        if do3:
                            e.wait_ge(e_ready, u * N2 + 2)
                            e.wait_ge(g_ready, NB * (u + 1))
                        elif do2:
                            e.wait_ge(g_ready, NB)
                        e.sem_inc(begun, 1)
                        e.tensor_copy(SL[r1][:, :], slopes4[:, bass.ds(GH * (u + 1), GH)]).then_inc(pool_own, 1)
                        e.wait_ge(pool_own, 2 + 2 * (u + 1) + 1)
                        e.sem_inc(begun, 1)
                        e.tensor_copy(SO[:, :], slopes_over4[:, bass.ds(u + 1, 1)]).then_inc(pool_own, 1)
                        e.wait_ge(pool_own, 2 + 2 * (u + 1) + 2)
                        for j in range(NB):
                            e.wait_ge(g_used, NB * u + j + 2 if do2 else 1)
                            if j:
                                e.wait_ge(g_ready, NB * (u + 1) + j)
                            e.sem_inc(begun, 1)
                            if j == GH:
                                e.tensor_scalar(GL[:, :], DL[:, :], SO[:, 0:1], None, ALU.mult).then_inc(g_ready, 1)
                            else:
                                e.tensor_scalar(G1[:, j, :], D1[:, :], SL[r1][:, j:j + 1], None, ALU.mult)\
                                    .then_inc(g_ready, 1)
                    steps(e, step)
            st.close()


        def stage_linear(layer):
            st = Stage()
            EH = HD + 1
            VB = NH * EH // KB
            NV = len(QCH)
            xb = st.sb("xb", [P, KB, T])
            qk = [st.sb(f"qk{c}", [TP, 2 * D]) for c in range(NV)]
            vv = [st.sb(f"vv{c}", [TP, KB * VB]) for c in range(NV)]
            hm = st.sb("hm", [TP, NV, 2 * NH])
            qT = st.sb("qT", [P, KB, T])
            KV = st.sb("KV", [P, KB, VB])
            mask = st.sb("mask", [P, KB, VB])
            den = st.sb("den", [TP, NV, NH])
            rec = st.sb("rec", [TP, NV, NH])
            on = [st.sb(f"on{c}", [TP, NH, HD]) for c in range(NV)]
            pqk = [st.psum(f"pqk{r}", [TP, 512]) for r in range(2)]
            pv = [st.psum(f"pv{r}", [TP, 512]) for r in range(2)]
            pkv = [st.psum(f"pkv{r}", [P, 512]) for r in range(2)]
            pt = [st.psum(f"pt{r}", [P, 512]) for r in range(2)]
            mask_in = st.sem("mask_in")
            xb_ready = st.sem("xb_ready")
            qk_ready = st.sem("qk_ready")
            qk_used = st.sem("qk_used")
            v_ready = st.sem("v_ready")
            v_used = st.sem("v_used")
            x_ready = st.sem("x_ready")
            e_ready = st.sem("e_ready")
            t_ready = st.sem("t_ready")
            t_used = st.sem("t_used")
            kv_ready = st.sem("kv_ready")
            kvm_ready = st.sem("kvm_ready")
            on_ready = st.sem("on_ready")
            own = st.sem("own")
            OWN = 3 * NV + 3 * NV

            with nc.Block() as block:
                @block.sync
                def _(e):
                    e.dma_start(mask[:, :, :], a["kv_mask"]).then_inc(mask_in, 16)

                @block.gpsimd
                def _(e):
                    with e.Fori(0, B) as b:
                        e.wait_ge(v_ready, 2 * NV * b + 1)
                        e.tensor_copy(xb[:, :, :], cols_of(XT, b * T, T)).then_inc(xb_ready, 1)

                @block.tensor
                def _(e):
                    e.sem_inc(v_ready, 1)
                    e.wait_ge(attn_loaded[layer], 48)
                    with e.Fori(0, B) as b:
                        e.wait_ge(xb_ready, b + 1)

                        def project(c):
                            q0, qn = QCH[c]
                            r = c % 2
                            e.wait_ge(qk_used, NV * b + 1 + max(c - 1, 0))
                            for kb in range(KB):
                                m = e.matmul(pqk[r][0:qn, :], xb[:, kb, q0:q0 + qn], ATW[:, kb, 0:2 * D],
                                             start=kb == 0, stop=kb == KB - 1)
                            m.then_inc(qk_ready, 1)
                            e.wait_ge(v_used, 2 * NV * b + c + 1)
                            for kb in range(KB):
                                m = e.matmul(pv[r][0:qn, 0:KB * VB], xb[:, kb, q0:q0 + qn],
                                             ATW[:, kb, 2 * D:2 * D + KB * VB], start=kb == 0, stop=kb == KB - 1)
                            m.then_inc(v_ready, 1)

                        def keys(c):
                            q0, qn = QCH[c]
                            e.wait_ge(e_ready, NV * b + c + 1)
                            e.wait_ge(v_used, 2 + 2 * NV * b + c + 1)
                            e.wait_ge(t_used, 2 * NV * b + c + 1)
                            e.sem_inc(begun, 1)
                            for kb in range(KB):
                                m = e.transpose(pt[c % 2][:, kb * P:kb * P + qn], qk[c][0:qn, kb * P:kb * P + P],
                                                ident[0:qn, 0:qn])
                            m.then_inc(t_ready, 1)
                            for kb in range(KB):
                                m = e.matmul(pkv[kb][:, 0:VB], qk[c][0:qn, D + kb * P:D + kb * P + P],
                                             vv[c][0:qn, kb * VB:kb * VB + VB], start=c == 0, stop=c == NV - 1)
                            if c == NV - 1:
                                m.then_inc(kv_ready, 1)

                        def outputs(c):
                            q0, qn = QCH[c]
                            e.wait_ge(v_used, 2 * NV * b + NV + c + 1)
                            for kb in range(KB):
                                m = e.matmul(pv[(NV + c) % 2][0:qn, kb * VB:kb * VB + VB], qT[:, kb, q0:q0 + qn],
                                             KV[:, kb, :], start=True, stop=True)
                            m.then_inc(v_ready, 1)

                        def back(c):
                            q0, qn = QCH[c]
                            e.wait_ge(on_ready, NV * b + c + 1)
                            e.wait_ge(t_used, 2 * NV * b + NV + c + 1)
                            e.sem_inc(begun, 1)
                            for kb in range(KB):
                                m = e.transpose(pt[(NV + c) % 2][:, kb * P:kb * P + qn],
                                                on[c][0:qn, kb * 8:kb * 8 + 8, :].rearrange("p h d -> p (h d)"),
                                                ident[0:qn, 0:qn])
                            m.then_inc(t_ready, 1)

                        for c in range(NV + 1):
                            if c < NV:
                                project(c)
                            if c >= 1:
                                keys(c - 1)
                        e.wait_ge(kvm_ready, b + 1)
                        e.wait_ge(t_used, 2 + 2 * NV * b + NV)
                        for c in range(NV + 1):
                            if c < NV:
                                outputs(c)
                            if c >= 1:
                                back(c - 1)

                @block.vector
                def _(e):
                    e.sem_inc(qk_used, 1)
                    e.sem_inc(v_used, 2)
                    e.wait_ge(mask_in, 16)
                    e.wait_ge(attn_loaded[layer], 48)
                    with e.Fori(0, B) as b:
                        for c, (q0, qn) in enumerate(QCH):
                            o = OWN * b + 3 * c
                            e.wait_ge(qk_ready, NV * b + c + 1)
                            e.tensor_tensor(qk[c][0:qn, :], pqk[c % 2][0:qn, :], ROWS[0:qn, 0:2 * D], ALU.add)\
                                .then_inc(qk_used, 1)
                            e.wait_ge(v_ready, 1 + 2 * NV * b + c + 1)
                            e.tensor_tensor(vv[c][0:qn, :], pv[c % 2][0:qn, 0:KB * VB],
                                            ROWS[0:qn, 2 * D:2 * D + KB * VB], ALU.add).then_inc(v_used, 1)
                            e.wait_ge(qk_used, 1 + NV * b + c + 1)
                            heads = qk[c][0:qn, :].rearrange("p (h d) -> p h d", d=HD)
                            e.tensor_reduce(hm[0:qn, c, :], heads, AX.X, ALU.max).then_inc(own, 3)
                            e.wait_ge(own, o + 3)
                            e.tensor_tensor(heads, heads, hm[0:qn, c, :].rearrange("p (h o) -> p h o", o=1)
                                            .to_broadcast([qn, 2 * NH, HD]), ALU.subtract).then_inc(x_ready, 1)
                        e.wait_ge(kv_ready, b + 1)
                        for kb in range(KB):
                            m = e.tensor_tensor(KV[:, kb, :], pkv[kb][:, 0:VB], mask[:, kb, :], ALU.mult)
                        m.then_inc(kvm_ready, 1)
                        for c, (q0, qn) in enumerate(QCH):
                            o = OWN * b + 3 * NV + 3 * c
                            e.wait_ge(v_ready, 1 + 2 * NV * b + NV + c + 1)
                            y = pv[(NV + c) % 2][0:qn, 0:KB * VB].rearrange("p (h x) -> p h x", x=EH)
                            e.tensor_scalar(den[0:qn, c, :], y[:, :, HD], 1e-6, None, ALU.add).then_inc(own, 1)
                            e.wait_ge(own, o + 1)
                            e.reciprocal(rec[0:qn, c, :], den[0:qn, c, :]).then_inc(own, 2)
                            e.wait_ge(own, o + 3)
                            e.tensor_tensor(on[c][0:qn, :, :], y[:, :, 0:HD],
                                            rec[0:qn, c, :].rearrange("p (h o) -> p h o", o=1)
                                            .to_broadcast([qn, NH, HD]), ALU.mult).then_inc(v_used, 1)
                            e.wait_ge(v_used, 2 + 2 * NV * b + NV + c + 1)
                            e.sem_inc(on_ready, 1)

                @block.scalar
                def _(e):
                    e.sem_inc(t_used, 2)
                    with e.Fori(0, B) as b:
                        for c in range(NV + 1):
                            if c < NV:
                                q0, qn = QCH[c]
                                e.wait_ge(x_ready, NV * b + c + 1)
                                e.activation(qk[c][0:qn, :], qk[c][0:qn, :], ACT.Exp).then_inc(e_ready, 1)
                            if c >= 1:
                                q0, qn = QCH[c - 1]
                                e.wait_ge(t_ready, 2 * NV * b + c)
                                e.activation(qT[:, :, q0:q0 + qn],
                                             pt[(c - 1) % 2][:, 0:KB * P].rearrange("p (k t) -> p k t", k=KB)[:, :, 0:qn],
                                             ACT.Copy).then_inc(t_used, 1)
                        for c, (q0, qn) in enumerate(QCH):
                            e.wait_ge(t_ready, 2 * NV * b + NV + c + 1)
                            e.activation(cols_of(XT, b * T + q0, qn),
                                         pt[(NV + c) % 2][:, 0:KB * P].rearrange("p (k t) -> p k t", k=KB)[:, :, 0:qn],
                                         ACT.Copy).then_inc(t_used, 1)
            st.close()

        def stage_segments(layer):
            st = Stage()
            XP = st.sb("XP", [P, KB, B, TS])
            A = [[st.sb(f"A{n}_{r}", [P, KB, SW]) for n in range(2)] for r in range(2)]
            QKV = [st.sb(f"QKV{r}", [SP, SEG, 3, D]) for r in range(2)]
            prod = [st.sb(f"prod{n}", [SP, SEG, D]) for n in range(2)]
            SC = st.sb("SC", [SP, SEG, SEG, SH])
            PR = st.sb("PR", [SP, SEG, SEG, SH])
            smx = st.sb("smx", [SP, SEG, SH])
            ssum = st.sb("ssum", [SP, SEG, SH])
            srec = st.sb("srec", [SP, SEG, SH])
            O = st.sb("O", [SP, SEG, D])
            pa = [st.psum(f"pa{r}", [P, 512]) for r in range(2)]
            pqk = [st.psum(f"pqk{r}", [SP, 512]) for r in range(2)]
            pv = [st.psum(f"pv{r}", [SP, 512]) for r in range(2)]
            po = [st.psum(f"po{r}", [P, 512]) for r in range(2)]
            xp_ready = st.sem("xp_ready")
            a_ready = st.sem("a_ready")
            a_used = st.sem("a_used")
            q_ready = st.sem("q_ready")
            q_used = st.sem("q_used")
            m_ready = [st.sem(f"m_ready{n}") for n in range(2)]
            m_used = [st.sem(f"m_used{n}") for n in range(2)]
            d_ready = st.sem("d_ready")
            p_ready = st.sem("p_ready")
            pr_ready = st.sem("pr_ready")
            o_ready = st.sem("o_ready")
            t_ready = st.sem("t_ready")
            t_used = st.sem("t_used")
            own = st.sem("own")
            OWN = 6
            flat = XP[:, :, :, :].rearrange("p k b t -> p k (b t)")

            with nc.Block() as block:
                @block.gpsimd
                def _(e):
                    e.tensor_copy(XP[:, 0, :, 0:T], XT[:, 0, :].rearrange("p (b t) -> p b t", b=B)).then_inc(xp_ready, 1)

                    with e.Fori(0, NST // 2) as it:
                        for r in range(2):
                            k = 2 * it + r
                            e.wait_ge(q_used, 2 + SEG * k + SEG)
                            for n, i in enumerate((1, 3)):
                                e.wait_ge(m_used[1], 4 * k + n + 1)
                                e.tensor_tensor(prod[1][:, :, :], QKV[r][:, i:i + 1, 0, :].to_broadcast([SP, SEG, D]),
                                                QKV[r][:, :, 1, :], ALU.mult).then_inc(m_ready[1], 1)
                            e.wait_ge(pr_ready, k + 1)
                            for n, i in enumerate((1, 3)):
                                e.wait_ge(m_used[1], 4 * k + 2 + n + 1)
                                for j in range(SEG):
                                    m = e.tensor_tensor(prod[1][:, j, :].rearrange("p (h d) -> p h d", d=SHD),
                                                        QKV[r][:, j, 2, :].rearrange("p (h d) -> p h d", d=SHD),
                                                        PR[:, i, j, :].rearrange("p (h o) -> p h o", o=1)
                                                        .to_broadcast([SP, SH, SHD]), ALU.mult)
                                m.then_inc(m_ready[1], 1)

                @block.vector
                def _(e):
                    e.tensor_copy(XP[:, 1, :, 0:T], XT[:, 1, :].rearrange("p (b t) -> p b t", b=B))
                    e.tensor_copy(XP[:, :, :, T:TS].rearrange("p k b t -> p (k b) t"),
                                  XT[:, :, :].rearrange("p k (b t) -> p (k b) t", b=B)[:, :, 0:TS - T]).then_inc(xp_ready, 1)
                    e.sem_inc(q_used, 2)
                    for n in range(2):
                        e.sem_inc(m_used[n], 1)
                    e.wait_ge(attn_loaded[layer], 48)
                    def add(k, r, i):
                        e.wait_ge(q_ready, 1 + SEG * k + i + 1)
                        e.tensor_tensor(QKV[r][:, i, 0:2, :].rearrange("p a b -> p (a b)"), pqk[i % 2][:, :],
                                        ROWS[0:SP, 0:512], ALU.add)
                        e.tensor_tensor(QKV[r][:, i, 2, :], pv[i % 2][:, 0:D], ROWS[0:SP, 512:768], ALU.add)\
                            .then_inc(q_used, 1)

                    def step(k, r, nxt):
                        e.wait_ge(q_used, 2 + SEG * k + SEG)

                        def scores(n, i, x):
                            e.wait_ge(m_ready[n], 4 * k + x + 1)
                            e.tensor_reduce(SC[:, i, :, :].rearrange("p j h -> p (j h)"),
                                            prod[n][:, :, :].rearrange("p j (h d) -> p (j h) d", d=SHD),
                                            AX.X, ALU.add).then_inc(m_used[n], 1)

                        for x, i in enumerate((0, 2)):
                            e.wait_ge(m_used[0], 4 * k + x + 1)
                            e.tensor_tensor(prod[0][:, :, :], QKV[r][:, i:i + 1, 0, :].to_broadcast([SP, SEG, D]),
                                            QKV[r][:, :, 1, :], ALU.mult).then_inc(m_ready[0], 1)
                            scores(0, i, x)
                            scores(1, i + 1, x)
                            if nxt:
                                add(k + 1, 1 - r, x)
                        e.wait_ge(m_used[0], 1 + 4 * k + 2)
                        e.wait_ge(m_used[1], 1 + 4 * k + 2)
                        e.memset(SC[:, :, :, :].rearrange("p i j h -> p (i j) h")[:, 0:SEG * SEG:SEG + 1, :], -BIG)\
                            .then_inc(own, 1)
                        e.wait_ge(own, OWN * k + 1)
                        e.tensor_reduce(smx[:, :, :], SC[:, :, :, :].rearrange("p i j h -> p i h j"), AX.X, ALU.max)\
                            .then_inc(own, 1)
                        e.wait_ge(own, OWN * k + 2)
                        for i in range(SEG):
                            m = e.tensor_tensor(SC[:, i, :, :], SC[:, i, :, :],
                                                smx[:, i:i + 1, :].to_broadcast([SP, SEG, SH]), ALU.subtract)
                        m.then_inc(d_ready, 1)
                        if nxt:
                            add(k + 1, 1 - r, 2)
                        e.wait_ge(p_ready, k + 1)
                        e.tensor_reduce(ssum[:, :, :], PR[:, :, :, :].rearrange("p i j h -> p i h j"), AX.X, ALU.add)\
                            .then_inc(own, 1)
                        e.wait_ge(own, OWN * k + 3)
                        e.reciprocal(srec[:, :, :], ssum[:, :, :]).then_inc(own, 3)
                        e.wait_ge(own, OWN * k + 6)
                        for i in range(SEG):
                            m = e.tensor_tensor(PR[:, i, :, :], PR[:, i, :, :],
                                                srec[:, i:i + 1, :].to_broadcast([SP, SEG, SH]), ALU.mult)
                        m.then_inc(pr_ready, 1)
                        if nxt:
                            add(k + 1, 1 - r, 3)
                        e.wait_ge(pr_ready, k + 1)
                        e.wait_ge(t_ready, 2 * k + 2)

                        def outputs(n, i, x):
                            e.wait_ge(m_ready[n], 4 * k + 2 + x + 1)
                            return e.tensor_reduce(O[:, i, :], prod[n][:, :, :].rearrange("p j f -> p f j"),
                                                   AX.X, ALU.add).then_inc(m_used[n], 1)

                        for x, i in enumerate((0, 2)):
                            e.wait_ge(m_used[0], 4 * k + 2 + x + 1)
                            for j in range(SEG):
                                m = e.tensor_tensor(prod[0][:, j, :].rearrange("p (h d) -> p h d", d=SHD),
                                                    QKV[r][:, j, 2, :].rearrange("p (h d) -> p h d", d=SHD),
                                                    PR[:, i, j, :].rearrange("p (h o) -> p h o", o=1)
                                                    .to_broadcast([SP, SH, SHD]), ALU.mult)
                            m.then_inc(m_ready[0], 1)
                            outputs(0, i, x)
                            outputs(1, i + 1, x)
                        e.wait_ge(m_used[1], 1 + 4 * k + 4)
                        e.sem_inc(o_ready, 1)

                    for i in range(SEG):
                        add(0, 0, i)
                    with e.Fori(0, NST // 2 - 1) as it:
                        step(2 * it, 0, True)
                        step(2 * it + 1, 1, True)
                    step(NST - 2, 0, True)
                    step(NST - 1, 1, False)

                @block.scalar
                def _(e):
                    e.sem_inc(a_used, 2)
                    e.sem_inc(t_used, 2)
                    e.wait_ge(attn_loaded[layer], 48)

                    def first(k, r):
                        for n in range(2):
                            for m in range(KB):
                                x = 2 * n + m
                                e.wait_ge(a_ready, 4 * k + x + 1)
                                e.activation(A[r][n][:, m, :], pa[x % 2][:, 0:SW], ACT.Identity,
                                             bias=COLS[:, x:x + 1]).then_inc(a_used, 1)

                    def probs(k):
                        e.wait_ge(d_ready, k + 1)
                        e.activation(PR[:, :, :, :], SC[:, :, :, :], ACT.Exp, scale=SHD ** -0.5).then_inc(p_ready, 1)

                    def last(k):
                        for kb in range(KB):
                            e.wait_ge(t_ready, 2 + 2 * k + kb + 1)
                            e.activation(flat[:, kb, bass.ds(k * SW, SW)].rearrange("p (s i) -> p i s", i=SEG),
                                         po[kb][:, 0:SW].rearrange("p (i s) -> p i s", i=SEG), ACT.Copy).then_inc(t_used, 1)

                    first(0, 0)
                    first(1, 1)
                    with e.Fori(0, NST // 2 - 1) as it:
                        for r in range(2):
                            probs(2 * it + r)
                            first(2 * it + r + 2, r)
                            last(2 * it + r)
                    for k in (NST - 2, NST - 1):
                        probs(k)
                        last(k)
                    e.wait_ge(t_used, 2 + 2 * NST)
                    for kb in range(KB):
                        e.activation(XT[:, kb, :].rearrange("p (b t) -> p b t", b=B), XP[:, kb, :, 0:T], ACT.Copy)

                @block.tensor
                def _(e):
                    e.sem_inc(q_ready, 1)
                    e.sem_inc(t_ready, 2)
                    e.wait_ge(xp_ready, 2)
                    e.wait_ge(attn_loaded[layer], 48)

                    def first(k):
                        for n in range(2):
                            for m in range(KB):
                                x = 2 * n + m
                                e.wait_ge(a_used, 4 * k + x + 1)
                                for kb in range(KB):
                                    mm = e.matmul(pa[x % 2][:, 0:SW], ATW[:, kb, n * D + m * P:n * D + m * P + P],
                                                  flat[:, kb, bass.ds(k * SW, SW)], start=kb == 0, stop=kb == KB - 1)
                                mm.then_inc(a_ready, 1)

                    def second(k, r):
                        e.wait_ge(a_used, 2 + 4 * k + 4)
                        for i in range(SEG):
                            e.wait_ge(q_used, SEG * k + i + 1)
                            for kb in range(KB):
                                e.matmul(pqk[i % 2][:, :], A[r][0][:, kb, i:SW:SEG], ATW[:, kb, 512:1024],
                                         start=kb == 0, stop=kb == KB - 1)
                            for kb in range(KB):
                                m = e.matmul(pv[i % 2][:, 0:D], A[r][1][:, kb, i:SW:SEG], ATW[:, kb, 1024:1280],
                                             start=kb == 0, stop=kb == KB - 1)
                            m.then_inc(q_ready, 1)

                    def last(k):
                        e.wait_ge(o_ready, k + 1)
                        for kb in range(KB):
                            e.wait_ge(t_used, 2 * k + kb + 1)
                            for i in range(SEG):
                                m = e.transpose(po[kb][:, SP * i:SP * i + SP], O[:, i, kb * P:kb * P + P], ident[0:SP, 0:SP])
                            m.then_inc(t_ready, 1)

                    first(0)
                    second(0, 0)
                    first(1)
                    with e.Fori(0, NST // 2 - 1) as it:
                        second(2 * it + 1, 1)
                        first(2 * it + 2)
                        last(2 * it)
                        second(2 * it + 2, 0)
                        first(2 * it + 3)
                        last(2 * it + 1)
                    second(NST - 1, 1)
                    last(NST - 2)
                    last(NST - 1)
            st.close()

        def stage_moe(n_ffn, loads, NE, shared, NHB, kind):
            st = Stage()
            relu = kind == "relu"
            NX = NE + shared
            NG_ = NX * NHB
            NY = NX + relu
            topk = 4 if kind == "sigmoid" else 2
            POS = 2
            ln = Norm(st, CT, KB)
            xT = [st.sb(f"xT{r}", [P, KB, CW]) for r in range(2)]
            sg = [st.sb(f"sg{r}", [P, CW]) for r in range(2)]
            hb = [[st.sb(f"h{r}_{n}", [P, CW]) for n in range(NHB)] for r in range(2)]
            ya = [st.sb(f"ya{r}", [TP, CT, D]) for r in range(2)]
            C = [st.sb(f"C{r}", [TP, CT, NX]) for r in range(2)]
            lg = st.sb("lg", [TP, CT, NE])
            pb = st.sb("pb", [TP, CT, NE])
            sel = st.sb("sel", [TP, CT, NE])
            eq = st.sb("eq", [TP, CT, NE])
            big = st.sb("big", [TP, CT, NE])
            c1 = st.sb("c1", [TP, CT])
            c2 = st.sb("c2", [TP, CT])
            top = st.sb("top", [TP, CT, 8])
            tix = st.sb("tix", [TP, CT, 8], U32)
            tif = st.sb("tif", [TP, CT, 8])
            sT = [st.sb(f"sT{r}", [8, CW]) for r in range(2)] if relu else None
            gu = [[st.psum(f"gu{r}_{n}", [P, 512]) for n in range(2)] for r in range(2)]
            py = [st.psum(f"py{j}", [TP, 512]) for j in range(CT)]
            misc = st.psum("misc", [P, 512])

            x_ready = st.sem("x_ready")
            r_ready = st.sem("r_ready")
            lg_ready = st.sem("lg_ready")
            ex_in = st.sem("ex_in")
            ex_out = st.sem("ex_out")
            c_ready = st.sem("c_ready")
            ct_ready = st.sem("ct_ready")
            s_ready = st.sem("s_ready")
            gu_ready = st.sem("gu_ready")
            sg_ready = st.sem("sg_ready")
            h_made = st.sem("h_made")
            y_ready = st.sem("y_ready")
            y_used = st.sem("y_used")
            h_added = st.sem("h_added")
            own = st.sem("own")
            c_set = st.sem("c_set")

            def chunks(e, body, prologue):
                prologue()
                with e.Fori(0, NCH // 2 - 1) as i:
                    body(2 * i, 0, True)
                    body(2 * i + 1, 1, True)
                body(NCH - 2, 0, True)
                body(NCH - 1, 1, False)

            def pieces(prep, k, r, nxt, x):
                if nxt and x - POS + 1 in range(6):
                    prep(k + 1, 1 - r, x - POS + 1)

            with nc.Block() as block:
                @block.tensor
                def _(e):
                    e.sem_inc(ln.tr_ready, 1)
                    e.sem_inc(y_ready, 2 * CT)
                    e.wait_ge(ffn_loaded[n_ffn], loads)

                    def prep(k, r, part):
                        if part in (1, 2):
                            kb = part - 1
                            if kb == 0:
                                e.wait_ge(ln.xn_ready, k + 1)
                                e.wait_ge(s_ready if relu else lg_ready, k + 1)
                            else:
                                e.wait_ge(x_ready, KB * k + 1)
                            for j in range(CT):
                                m = e.transpose(misc[:, TP * j:TP * j + TP], ln.xn[0][:, j, kb * P:kb * P + P],
                                                ident[0:TP, 0:TP])
                            m.then_inc(ln.tr_ready, 1)
                        if part == 3:
                            e.wait_ge(x_ready, KB * k + 2)
                            for j in range(CT):
                                for kb in range(KB):
                                    m = e.matmul(misc[0:TP, 16 * j:16 * j + NE], xT[r][:, kb, TP * j:TP * j + TP],
                                                 RW[:, kb, 0:NE], start=kb == 0, stop=kb == KB - 1)
                            m.then_inc(r_ready, 1)
                        if part == 5 and relu:
                            e.wait_ge(c_ready, k + 1)
                            for j in range(CT):
                                m = e.transpose(misc[0:NE, TP * j:TP * j + TP], C[r][:, j, :], ident[0:TP, 0:TP])
                            m.then_inc(ct_ready, 1)

                    def gate_up(k, r, x):
                        for b in range(NHB):
                            n = x * NHB + b
                            slot = (r * NG_ + n) % 2
                            e.wait_ge(h_made, k * NG_ + n + 1)
                            for g in range(1 if relu else 2):
                                w0 = n * P if relu else (2 * x + g) * P
                                for kb in range(KB):
                                    m = e.matmul(gu[slot][g][:, 0:CW], FW1[:, kb, w0:w0 + P], xT[r][:, kb, :],
                                                 start=kb == 0, stop=kb == KB - 1)
                            m.then_inc(gu_ready, 1)

                    def down(k, r, x):
                        if x < NX:
                            e.wait_ge(h_made, 2 + k * NG_ + (x + 1) * NHB)
                        else:
                            e.wait_ge(s_ready, 1 + k + 1)
                        for j in range(CT):
                            y = py[j][:, 0:D]
                            e.wait_ge(y_used, (k * NY + x) * CT + j + 1)
                            if x == NX:
                                e.matmul(y, sT[r][0:NE, TP * j:TP * j + TP], B2[0:NE, :], start=True, stop=True)\
                                    .then_inc(y_ready, 1)
                                continue
                            for b in range(NHB):
                                m = e.matmul(y, hb[(r * NX + x) % 2][b][:, TP * j:TP * j + TP], FW2[:, x * NHB + b, :],
                                             start=b == 0, stop=b == NHB - 1)
                            m.then_inc(y_ready, 1)

                    def body(k, r, nxt):
                        e.wait_ge(x_ready, KB * k + 2)
                        for x in range(NX):
                            pieces(prep, k, r, nxt, x)
                            gate_up(k, r, x)
                            if x:
                                down(k, r, x - 1)
                        for x in range(NX - 1, NY):
                            down(k, r, x)
                    chunks(e, body, lambda: [prep(0, 0, part) for part in range(6)])

                @block.scalar
                def _(e):
                    if relu:
                        e.sem_inc(s_ready, 1)
                        e.sem_inc(h_made, 2)
                        e.wait_ge(ffn_loaded[n_ffn], loads)

                    def prep(k, r, part):
                        if part == 0:
                            ln.scalar(e, k)
                        if part in (1, 2):
                            kb = part - 1
                            e.wait_ge(ln.tr_ready, 1 + KB * k + kb + 1)
                            e.activation(xT[r][:, kb, :], misc[:, 0:CW], ACT.Copy).then_inc(x_ready, 1)
                        if part == 4:
                            e.wait_ge(ex_in, k + 1)
                            e.activation(pb[:, :, :], lg[:, :, :], ACT.Exp,
                                         scale=-1.0 if kind == "sigmoid" else 1.0).then_inc(ex_out, 1)
                        if part == 5 and relu:
                            e.wait_ge(ct_ready, k + 1)
                            e.activation(sT[r][0:NE, :], misc[0:NE, 0:CW], ACT.Copy).then_inc(s_ready, 1)

                    def body(k, r, nxt):
                        for x in range(NX):
                            pieces(prep, k, r, nxt, x)
                            for b in range(NHB):
                                n = x * NHB + b
                                slot = (r * NG_ + n) % 2
                                e.wait_ge(gu_ready, k * NG_ + n + 1)
                                if relu:
                                    if b == 0:
                                        e.wait_ge(y_ready, (k * NY + (x if x >= 2 else 0) + 1) * CT)
                                    e.activation(hb[(r * NX + x) % 2][b][:, :], gu[slot][0][:, 0:CW], ACT.Relu,
                                                 bias=B1[:, n:n + 1]).then_inc(h_made, 1)
                                else:
                                    e.wait_ge(h_made, k * NG_ + n + 1)
                                    e.activation(sg[slot][:, :], gu[slot][0][:, 0:CW], ACT.Silu).then_inc(sg_ready, 1)
                    chunks(e, body, lambda: [prep(0, 0, part) for part in range(6)])

                @block.vector
                def _(e):
                    e.sem_inc(lg_ready, 1)
                    e.sem_inc(y_used, CT)
                    if not relu:
                        e.sem_inc(h_made, 2)
                    e.wait_ge(ffn_loaded[n_ffn], loads)
                    for r in range(2):
                        m = e.memset(C[r][:, :, :], 1.0)
                    m.then_inc(c_set, 1)
                    e.wait_ge(c_set, 1)
                    OWN = {"probs": 10, "sigmoid": 17, "relu": 13}[kind]

                    def prep(k, r, part):
                        if part == 0:
                            ln.vector(e, k)
                        if part != 4:
                            return
                        done = 0

                        def then(m):
                            nonlocal done
                            done += 1
                            m.then_inc(own, 1)
                            e.wait_ge(own, k * OWN + done)

                        def wide(v):
                            return v.rearrange("p (j o) -> p j o", o=1).to_broadcast([TP, CT, NE])

                        e.wait_ge(r_ready, k + 1)
                        e.tensor_copy(lg[:, :, :], misc[0:TP, 0:16 * CT].rearrange("p (j n) -> p j n", n=16)[:, :, 0:NE])\
                            .then_inc(lg_ready, 1)
                        e.wait_ge(lg_ready, 1 + k + 1)
                        if kind == "sigmoid":
                            e.sem_inc(ex_in, 1)
                            e.wait_ge(ex_out, k + 1)
                            then(e.tensor_scalar(eq[:, :, :], pb[:, :, :], 1.0, None, ALU.add))
                            then(e.reciprocal(pb[:, :, :], eq[:, :, :]))
                            for j in range(CT):
                                m = e.tensor_tensor(big[:, j, :], pb[:, j, :], RB[0:TP, 0:NE], ALU.add)
                            then(m)
                            chosen = big
                        else:
                            then(e.tensor_reduce(c1[:, :], lg[:, :, :], AX.X, ALU.max))
                            e.tensor_tensor(lg[:, :, :], lg[:, :, :], wide(c1[:, :]), ALU.subtract).then_inc(ex_in, 1)
                            e.wait_ge(ex_out, k + 1)
                            then(e.tensor_reduce(c1[:, :], pb[:, :, :], AX.X, ALU.add))
                            then(e.reciprocal(c2[:, :], c1[:, :]))
                            then(e.tensor_tensor(pb[:, :, :], pb[:, :, :], wide(c2[:, :]), ALU.mult))
                            chosen = pb
                        e.sem_inc(begun, 1)
                        for j in range(CT):
                            m = e.max(top[:, j, :], chosen[:, j, :])
                        then(m)
                        e.sem_inc(begun, 1)
                        for j in range(CT):
                            m = e.max_index(tix[:, j, :], top[:, j, :], chosen[:, j, :])
                        then(m)
                        then(e.tensor_copy(tif[:, :, :], tix[:, :, :]))
                        then(e.tensor_tensor(sel[:, :, :], iota[:, :, 0:NE], wide(tif[:, :, 0]), ALU.is_equal))
                        for t in range(1, topk):
                            then(e.tensor_tensor(eq[:, :, :], iota[:, :, 0:NE], wide(tif[:, :, t]), ALU.is_equal))
                            if t < topk - 1 or kind != "probs":
                                then(e.tensor_tensor(sel[:, :, :], sel[:, :, :], eq[:, :, :], ALU.add))
                        w = C[r][:, :, 0:NE]
                        if kind == "probs":
                            then(e.tensor_tensor(sel[:, :, :], sel[:, :, :], eq[:, :, :], ALU.add))
                            e.tensor_tensor(w, sel[:, :, :], pb[:, :, :], ALU.mult).then_inc(c_ready, 1)
                        else:
                            then(e.tensor_tensor(sel[:, :, :], sel[:, :, :], pb[:, :, :], ALU.mult))
                            then(e.tensor_reduce(c1[:, :], sel[:, :, :], AX.X, ALU.add))
                            then(e.reciprocal(c2[:, :], c1[:, :]))
                            if kind == "sigmoid":
                                then(e.tensor_tensor(sel[:, :, :], sel[:, :, :], wide(c2[:, :]), ALU.mult))
                                e.tensor_scalar(w, sel[:, :, :], 2.5, None, ALU.mult).then_inc(c_ready, 1)
                            else:
                                e.tensor_tensor(w, sel[:, :, :], wide(c2[:, :]), ALU.mult).then_inc(c_ready, 1)
                        assert done == OWN, (kind, done)

                    def accumulate(k, r, x):
                        if x == 0:
                            e.wait_ge(c_ready, k + 1)
                            e.wait_ge(h_added, k + 1)
                        for j in range(CT):
                            n = (k * NY + x) * CT + j
                            y = py[j][:, 0:D]
                            e.wait_ge(y_ready, 2 * CT + n + 1)
                            if x:
                                e.wait_ge(y_used, n + 1)
                            if x == 0:
                                m = e.tensor_scalar(ya[r][:, j, :], y, C[r][:, j, 0:1], None, ALU.mult)
                            elif x == NX:
                                m = e.tensor_tensor(ya[r][:, j, :], y, ya[r][:, j, :], ALU.add)
                            else:
                                m = e.scalar_tensor_tensor(out=ya[r][:, j, :], in0=y, scalar=C[r][:, j, x:x + 1],
                                                           in1=ya[r][:, j, :], op0=ALU.mult, op1=ALU.add)
                            m.then_inc(y_used, 1)

                    def body(k, r, nxt):
                        for x in range(NX):
                            pieces(prep, k, r, nxt, x)
                            if not relu:
                                n = k * NG_ + x
                                slot = (r * NG_ + x) % 2
                                e.wait_ge(sg_ready, n + 1)
                                e.wait_ge(y_ready, (k * NY + x + 1) * CT)
                                e.tensor_tensor(hb[(r * NX + x) % 2][0][:, :], sg[slot][:, :], gu[slot][1][:, 0:CW],
                                                ALU.mult).then_inc(h_made, 1)
                            if x:
                                accumulate(k, r, x - 1)
                        for x in range(NX - 1, NY):
                            accumulate(k, r, x)
                    chunks(e, body, lambda: [prep(0, 0, part) for part in range(6)])

                @block.gpsimd
                def _(e):
                    e.sem_inc(h_added, 2)
                    with e.Fori(0, NCH // 2) as i:
                        for r in range(2):
                            k = 2 * i + r
                            e.wait_ge(y_used, CT + (k + 1) * NY * CT)
                            rows = H[:, bass.ds(CT * k, CT), :]
                            e.tensor_tensor(rows, rows, ya[r][:, :, :], ALU.add).then_inc(h_added, 1)
            st.close()

        def stage_ternary(n_ffn, loads):
            st = Stage()
            F = 1024
            NF = F // P
            ln = Norm(st, 1, 1)
            ones = st.sb("ones", [P, P])
            absum = st.sb("absum", [P, 2])
            thr = st.sb("thr", [P, 4])
            low = st.sb("low", [P, KB * F])
            xT = [st.sb(f"xT{r}", [P, KB, TP]) for r in range(2)]
            g = [st.sb(f"g{r}", [TP, F]) for r in range(2)]
            gn = [st.sb(f"gn{r}", [TP, F]) for r in range(2)]
            hT = [st.sb(f"hT{r}", [P, NF, TP]) for r in range(2)]
            fst = st.sb("fst", [TP, 2, 6])
            fmv = st.sb("fmv", [TP, 2])
            fsd = st.sb("fsd", [TP, 1])
            frs = st.sb("frs", [TP, 1])
            pf = [st.psum(f"pf{r}", [TP, F]) for r in range(2)]
            pt = [st.psum(f"pt{r}", [P, 512]) for r in range(2)]
            px = st.psum("px", [P, 512])
            po = st.psum("po", [TP, 512])
            sum_ready = st.sem("sum_ready")
            tot_ready = st.sem("tot_ready")
            own_q = st.sem("own_q")
            q_done = st.sem("q_done")
            x_ready = st.sem("x_ready")
            f_ready = st.sem("f_ready")
            g_ready = st.sem("g_ready")
            v_ready = st.sem("v_ready")
            s_ready = st.sem("s_ready")
            gn_ready = st.sem("gn_ready")
            t_ready = st.sem("t_ready")
            t_used = st.sem("t_used")
            o_ready = st.sem("o_ready")
            o_used = st.sem("o_used")
            own = st.sem("own")
            OWN = 2
            W1 = FW1[:, :, 0:F]
            W2 = FW2[:, 0:NF, :].rearrange("p c n -> p (c n)")

            with nc.Block() as block:
                @block.vector
                def _(e):
                    e.sem_inc(gn_ready, 2)
                    e.sem_inc(o_used, 1)
                    e.memset(ones[:, :], 1.0)
                    e.wait_ge(ffn_loaded[n_ffn], loads)
                    e.tensor_reduce(absum[:, 0:1], W1, AX.XY, ALU.add, apply_absolute_value=True)
                    e.tensor_reduce(absum[:, 1:2], W2, AX.X, ALU.add, apply_absolute_value=True).then_inc(sum_ready, 1)
                    e.wait_ge(tot_ready, 1)
                    e.tensor_scalar(thr[:, 0:2], px[:, 0:2], 1.0 / (D * F), 1e-6, ALU.mult, ALU.add).then_inc(own_q, 1)
                    e.wait_ge(own_q, 1)
                    e.tensor_scalar(thr[:, 2:4], thr[:, 0:2], -0.5, None, ALU.mult).then_inc(own_q, 1)
                    e.wait_ge(own_q, 2)
                    e.tensor_scalar(thr[:, 0:2], thr[:, 0:2], 0.5, None, ALU.mult).then_inc(own_q, 1)
                    e.wait_ge(own_q, 3)
                    lw = low[:, :].rearrange("p (k f) -> p k f", k=KB)
                    e.tensor_scalar(lw, W1, thr[:, 2:3], None, ALU.is_lt).then_inc(own_q, 1)
                    e.wait_ge(own_q, 4)
                    e.scalar_tensor_tensor(out=W1, in0=W1, scalar=thr[:, 0:1], in1=lw, op0=ALU.is_gt, op1=ALU.subtract)\
                        .then_inc(own_q, 1)
                    e.wait_ge(own_q, 5)
                    e.tensor_scalar(low[:, :], W2, thr[:, 3:4], None, ALU.is_lt).then_inc(own_q, 1)
                    e.wait_ge(own_q, 6)
                    e.scalar_tensor_tensor(out=W2, in0=W2, scalar=thr[:, 1:2], in1=low[:, :], op0=ALU.is_gt,
                                           op1=ALU.subtract).then_inc(q_done, 1)

                    def normalise(t, r):
                        e.wait_ge(g_ready, 2 + t + 1)
                        for h in range(2):
                            m = e.bn_stats(fst[:, h, :], g[r][:, 512 * h:512 * h + 512])
                        m.then_inc(own, 1)
                        e.wait_ge(own, OWN * t + 1)
                        e.sem_inc(begun, 1)
                        e.bn_aggr(fmv[:, :], fst[:, :, :].rearrange("p a b -> p (a b)")).then_inc(v_ready, 1)
                        e.wait_ge(s_ready, t + 1)
                        e.reciprocal(frs[:, :], fsd[:, :]).then_inc(own, 1)
                        e.wait_ge(own, OWN * t + 2)
                        e.wait_ge(t_ready, 2 * t + 1)
                        e.tensor_scalar(gn[r][:, :], g[r][:, :], fmv[:, 0:1], frs[:, 0:1], ALU.subtract, ALU.mult)\
                            .then_inc(gn_ready, 1)

                    def add(t):
                        e.wait_ge(o_ready, 2 + t + 1)
                        e.tensor_tensor(H[:, t, :], H[:, t, :], po[:, 0:D], ALU.add).then_inc(o_used, 1)

                    ln.vector(e, 0)
                    ln.vector(e, 1)
                    normalise(0, 0)
                    ln.vector(e, 2)
                    normalise(1, 1)
                    ln.vector(e, 3)
                    normalise(2, 0)
                    add(0)
                    with e.Fori(1, NT // 2 - 1) as i:
                        ln.vector(e, 2 * i + 2)
                        normalise(2 * i + 1, 1)
                        add(2 * i - 1)
                        ln.vector(e, 2 * i + 3)
                        normalise(2 * i + 2, 0)
                        add(2 * i)
                    normalise(NT - 1, 1)
                    add(NT - 3)
                    add(NT - 2)
                    add(NT - 1)

                @block.scalar
                def _(e):
                    e.sem_inc(x_ready, 1)
                    e.sem_inc(g_ready, 2)
                    e.sem_inc(t_used, 2)
                    e.wait_ge(ffn_loaded[n_ffn], loads)

                    def features(t, r):
                        ln.scalar(e, t)
                        e.wait_ge(ln.tr_ready, 1 + t + 1)
                        e.activation(xT[r][:, :, :], px[:, 0:KB * P].rearrange("p (k t) -> p k t", k=KB)[:, :, 0:TP],
                                     ACT.Copy).then_inc(x_ready, 1)

                    def gelu(t, r):
                        e.wait_ge(f_ready, t + 1)
                        e.wait_ge(gn_ready, t + 1)
                        e.activation(g[r][:, :], pf[r][:, :], ACT.Gelu).then_inc(g_ready, 1)

                    def root(t):
                        e.wait_ge(v_ready, t + 1)
                        e.activation(fsd[:, :], fmv[:, 1:2], ACT.Sqrt, bias=eps[0:TP, :]).then_inc(s_ready, 1)

                    def affine(t, r):
                        for h in range(2):
                            e.wait_ge(t_ready, 3 + 2 * t + h + 1)
                            if h == 0:
                                e.wait_ge(o_ready, t + 1)
                            for x in range(4):
                                c = 4 * h + x
                                m = e.activation(hT[r][:, c, :], pt[h][:, P * x:P * x + TP], ACT.Identity,
                                                 bias=B1[:, NF + c:NF + c + 1], scale=B1[:, c:c + 1])
                            m.then_inc(t_used, 1)

                    features(0, 0)
                    features(1, 1)
                    gelu(0, 0)
                    root(0)
                    with e.Fori(0, NT // 2 - 1) as i:
                        features(2 * i + 2, 0)
                        gelu(2 * i + 1, 1)
                        root(2 * i + 1)
                        affine(2 * i, 0)
                        features(2 * i + 3, 1)
                        gelu(2 * i + 2, 0)
                        root(2 * i + 2)
                        affine(2 * i + 1, 1)
                    gelu(NT - 1, 1)
                    root(NT - 1)
                    affine(NT - 2, 0)
                    affine(NT - 1, 1)

                @block.tensor
                def _(e):
                    e.sem_inc(ln.tr_ready, 1)
                    e.sem_inc(t_ready, 3)
                    e.sem_inc(o_ready, 2)
                    e.wait_ge(sum_ready, 1)
                    e.matmul(px[:, 0:2], ones[:, :], absum[:, :], start=True, stop=True).then_inc(tot_ready, 1)
                    e.wait_ge(own_q, 1)

                    def features(t):
                        e.wait_ge(ln.xn_ready, t + 1)
                        e.wait_ge(x_ready, t + 1)
                        for kb in range(KB):
                            m = e.transpose(px[:, kb * P:kb * P + TP], ln.xn[0][:, 0, kb * P:kb * P + P], ident[0:TP, 0:TP])
                        m.then_inc(ln.tr_ready, 1)

                    def hidden(t, r):
                        e.wait_ge(x_ready, 1 + t + 1)
                        e.wait_ge(g_ready, t + 1)
                        for h in range(2):
                            for kb in range(KB):
                                m = e.matmul(pf[r][:, 512 * h:512 * h + 512], xT[r][:, kb, :],
                                             FW1[:, kb, 512 * h:512 * h + 512], start=kb == 0, stop=kb == KB - 1)
                        m.then_inc(f_ready, 1)

                    def turn(t, r):
                        e.wait_ge(gn_ready, 2 + t + 1)
                        for h in range(2):
                            e.wait_ge(t_used, 2 * t + h + 1)
                            for x in range(4):
                                c = 4 * h + x
                                m = e.transpose(pt[h][:, P * x:P * x + TP], gn[r][:, P * c:P * c + P], ident[0:TP, 0:TP])
                            m.then_inc(t_ready, 1)

                    def project(t, r):
                        e.wait_ge(t_used, 2 + 2 * t + 2)
                        e.wait_ge(o_used, t + 1)
                        for c in range(NF):
                            m = e.matmul(po[:, 0:D], hT[r][:, c, :], FW2[:, c, :], start=c == 0, stop=c == NF - 1)
                        m.then_inc(o_ready, 1)

                    features(0)
                    features(1)
                    e.wait_ge(q_done, 1)
                    hidden(0, 0)
                    hidden(1, 1)
                    features(2)
                    turn(0, 0)
                    hidden(2, 0)
                    features(3)
                    project(0, 0)
                    turn(1, 1)
                    with e.Fori(1, NT // 2 - 1) as i:
                        hidden(2 * i + 1, 1)
                        features(2 * i + 2)
                        project(2 * i - 1, 1)
                        turn(2 * i, 0)
                        hidden(2 * i + 2, 0)
                        features(2 * i + 3)
                        project(2 * i, 0)
                        turn(2 * i + 1, 1)
                    hidden(NT - 1, 1)
                    project(NT - 3, 1)
                    turn(NT - 2, 0)
                    project(NT - 2, 0)
                    turn(NT - 1, 1)
                    project(NT - 1, 1)
            st.close()

        NL0 = load_counts(a, "L0")
        NL1, NL2, NL3 = load_counts(a, "L1"), load_counts(a, "L2"), load_counts(a, "L3")

        def prefetch_attn(n, name):
            return lambda e: load_attn(e, n, a[f"w_{name}"], a[f"rows_{name}"], a[f"cols_{name}"])

        def prefetch_ffn(n, name):
            def load(e):
                load_ffn(e, n, *(a.get(f"{name}_{x}") for x in ("w1", "w2", "rw", "rb", "b1", "b2")))
            return load

        def stage_load(*loads):
            with nc.Block() as block:
                @block.sync
                def _(e):
                    for f in loads:
                        f(e)

        st = Stage()
        with nc.Block() as block:
            @block.sync
            def _(e):
                e.dma_start(ident[:, :], a["ident"]).then_inc(const_loaded, 16)
                e.dma_start(iota[:, :, :], a["iota"]).then_inc(const_loaded, 16)
                e.dma_start(XT[:, :, :], a["xT"].rearrange("(k p) t -> p k t", p=P)).then_inc(const_loaded, 16)
                prefetch_attn(0, "tok")(e)
                prefetch_ffn(0, "L0")(e)
                e.wait_ge(const_loaded, 48)

            @block.vector
            def _(e):
                e.memset(eps[:, :], LN_EPS)
        st.close()
        none = lambda e: None
        stage_qkv(0, False)
        stage_attn(1, False)
        stage_project(1024, 512, True, none)
        stage_load(prefetch_attn(1, "lin"))
        stage_norm()
        stage_linear(1)
        stage_project(784, 784, False, none)
        stage_load(prefetch_attn(2, "rope"))
        stage_moe(0, NL0, 16, 2, 1, "probs")
        stage_load(prefetch_ffn(1, "L1"))
        stage_norm()
        stage_qkv(2, True)
        stage_attn(0, True)
        stage_project(1024, 512, False, none)
        stage_load(prefetch_attn(3, "seg"))
        stage_moe(1, NL1, 16, 1, 1, "sigmoid")
        stage_load(prefetch_ffn(2, "L2"))
        stage_norm()
        stage_segments(3)
        stage_project(1280, 768, False, none)
        stage_load(prefetch_attn(4, "gqa"))
        stage_moe(2, NL2, 8, 0, 4, "relu")
        stage_load(prefetch_ffn(3, "L3"))
        stage_norm()
        stage_qkv(4, False)
        stage_attn(0, False)
        stage_project(1024, 512, False, none)
        stage_ternary(3, NL3)

        st = Stage()
        with nc.Block() as block:
            @block.sync
            def _(e):
                e.dma_start(out.rearrange("(t p) d -> p t d", p=TP), H[:, :, :]).then_inc(out_stored, 16)
                e.wait_ge(out_stored, 16)
        st.close()


def load_counts(a, name):
    return 16 * (KB + 1 + sum(f"{name}_{x}" in a for x in ("rw", "rb", "b1", "b2")))


def rows_of(*vectors):
    return np.ascontiguousarray(np.broadcast_to(np.concatenate(vectors)[None, :], (P, sum(map(len, vectors)))))


def to_head_rows(w):
    return w.reshape(KB, NH // KB, HD, -1).transpose(0, 2, 1, 3).reshape(w.shape)


def v_columns(w):
    return np.concatenate([w.reshape(-1, NH, HD), np.zeros((w.shape[0], NH, VW - HD), np.float32)], 2).reshape(-1, NH * VW)


def v_row(b):
    one = np.zeros((NH, VW - HD), np.float32)
    one[:, 0] = 1.0
    return np.concatenate([b.reshape(NH, HD), one], 1).reshape(-1)


def softmax_layer(wq, bq, wk, bk, wv, bv, wo, bo, rope=False):
    ws = [to_head_rows(wq).T, to_head_rows(wk).T, v_columns(wv.T), wo.T]
    if rope:
        swap = lambda w: w.reshape(NH, 2, HD // 2, -1)[:, ::-1].reshape(w.shape)
        ws += [to_head_rows(swap(wq)).T, to_head_rows(swap(wk)).T]
    cols = np.concatenate([to_head_rows(b[:, None]).reshape(KB, P).T for b in (bq, bk)], 1)
    return (np.ascontiguousarray(np.concatenate(ws, 1)), rows_of(v_row(bv), bo), np.ascontiguousarray(cols))


def constants():
    c = {"ident": np.eye(P, dtype=np.float32)}
    p, x = np.arange(P)[:, None, None], np.arange(NH // KB * (HD + 1))[None, None, :]
    c["kv_mask"] = np.broadcast_to(p // HD == x // (HD + 1), (P, KB, x.size)).astype(np.float32)
    c["iota"] = np.ascontiguousarray(np.broadcast_to(np.arange(16, dtype=np.float32), (TP, CT, 16)))
    rows = P - NSLOT * HD
    hot = np.zeros((rows, GH, 1), np.float32)
    for j in range(GH):
        hot[rows - 2 * GH + j, j] = hot[rows - GH + j, j] = 1.0
    c["hot"] = hot
    c["alibi_over"] = np.broadcast_to(np.arange(T, dtype=np.float32) - (T - 1), (P, T))
    over_rows = np.zeros((P, GH + 1), np.float32)
    over_rows[:, GH] = 1.0
    for j in range(GH):
        over_rows[VW * j + VW - 1, j] = 1.0
    c["over_rows"] = over_rows
    c0 = QCH[-1][0]
    p, x = np.arange(P)[:, None], np.arange(T + c0)[None, :] - c0
    c["alibi_q"] = np.minimum(x - p, 0).astype(np.float32)
    c["alibi_k"] = np.minimum(p - x, 0).astype(np.float32)
    inv = (np.float32(1.0) / np.float32(10000.0) ** (np.arange(0, HD, 2, dtype=np.float32) / np.float32(HD))).astype(np.float32)
    f = (np.arange(T, dtype=np.float32)[None, :] * inv[:, None]).astype(np.float32)
    cos = np.concatenate([np.cos(f), np.cos(f)]).astype(np.float32)
    sin = np.concatenate([-np.sin(f), np.sin(f)]).astype(np.float32)
    c["cos"] = np.repeat(cos, P // HD, 0)
    c["sin"] = np.repeat(sin, P // HD, 0)
    return c


def laid_out(i):
    g = {k: np.asarray(v) for k, v in i.items()}
    a = constants()
    z = np.zeros((D,), np.float32)
    xs = np.zeros((D, B, T), np.float32)
    xs[:, :, 1:] = g["x"][:, 0].transpose(2, 0, 1)
    a["xT"] = xs.reshape(D, TOK)
    a["cls"] = g["cls_tok"].reshape(1, D)
    w, b = g["L0_tok_w_qkv"].reshape(NH, 3, HD, D), g["L0_tok_b_qkv"].reshape(NH, 3, HD)
    a["w_tok"], a["rows_tok"], a["cols_tok"] = softmax_layer(
        w[:, 0].reshape(D, D), b[:, 0].reshape(-1), w[:, 1].reshape(D, D), b[:, 1].reshape(-1),
        w[:, 2].reshape(D, D), b[:, 2].reshape(-1), g["L0_tok_w_out"], g["L0_tok_b_out"])

    def join(*ws):
        return np.concatenate(ws, 1)

    vw = np.concatenate([g["L0_attn_Wv"].T.reshape(D, NH, HD), np.zeros((D, NH, 1), np.float32)], 2).reshape(D, -1)
    vb = np.concatenate([g["L0_attn_bv"].reshape(NH, HD), np.ones((NH, 1), np.float32)], 1).reshape(-1)
    a["w_lin"] = join(g["L0_attn_Wq"].T, g["L0_attn_Wk"].T, vw, g["L0_attn_Wo"].T)
    a["rows_lin"] = rows_of(g["L0_attn_bq"], g["L0_attn_bk"], vb, g["L0_attn_bo"])
    a["cols_lin"] = np.zeros((P, 8), np.float32)
    a["L0_w1"] = join(*(m for e in range(16) for m in (g["L0_ffn_Wg"][e], g["L0_ffn_Wu"][e])),
                      *(m[:, P * n:P * n + P] for n in range(2) for m in (g["L0_ffn_Sg"], g["L0_ffn_Su"])))
    a["L0_w2"] = np.concatenate([g["L0_ffn_Wd"].reshape(-1, D), g["L0_ffn_Sd"]])
    a["L0_rw"] = g["L0_ffn_Wr"]

    w = g["L1_attn_qkv_w"].reshape(3, D, D)
    a["w_rope"], a["rows_rope"], a["cols_rope"] = softmax_layer(
        w[0], z, w[1], z, w[2], z, g["L1_attn_proj_w"], g["L1_attn_proj_b"], rope=True)
    heads = [4 * (2 * (u // 2 // B) + u % 2) + j for u in range(B * NG) for j in range(GH)]
    a["slopes"] = rows_of(g["L1_attn_slopes"][heads])
    by_unit = np.repeat(g["L1_attn_slopes"][heads].reshape(B * NG, GH), VW, 1)
    a["slopes_over"] = by_unit.T
    a["L1_w1"] = join(*(g["L1_ffn_w13"][e].T for e in range(16)), g["L1_ffn_w13_s"].T)
    a["L1_w2"] = np.concatenate([g["L1_ffn_w2"][e].T for e in range(16)] + [g["L1_ffn_w2_s"].T])
    a["L1_rw"] = g["L1_ffn_gate_w"].T
    a["L1_rb"] = rows_of(g["L1_ffn_gate_b"])

    wi, bi = g["L2_attn_in_proj_w"].T, g["L2_attn_in_proj_b"]
    a["w_seg"] = join(g["L2_attn_proj_qk_w"].T, g["L2_attn_proj_v_w"].T, wi, g["L2_attn_out_proj_w"].T)
    a["rows_seg"] = rows_of(bi, g["L2_attn_out_proj_b"])
    a["cols_seg"] = join(*(b.reshape(KB, P).T for b in (g["L2_attn_proj_qk_b"], g["L2_attn_proj_v_b"])))
    a["L2_w1"] = join(*g["L2_ffn_W1"])
    a["L2_w2"] = g["L2_ffn_W2"].reshape(-1, D)
    a["L2_rw"] = g["L2_ffn_Wg"]
    a["L2_b1"] = g["L2_ffn_b1"].reshape(-1, P).T
    a["L2_b2"] = g["L2_ffn_b2"]

    def shared_heads(w):
        return np.repeat(w.reshape(4, 1, HD, -1), 4, 1).reshape(D, -1)

    a["w_gqa"], a["rows_gqa"], a["cols_gqa"] = softmax_layer(
        g["L3_attn_wq"], g["L3_attn_bq"], shared_heads(g["L3_attn_wk"]), shared_heads(g["L3_attn_bk"])[:, 0],
        shared_heads(g["L3_attn_wv"]), shared_heads(g["L3_attn_bv"])[:, 0], g["L3_attn_wo"], g["L3_attn_bo"])
    a["L3_w1"] = g["L3_ffn_W_fc"].T
    a["L3_w2"] = g["L3_ffn_W_proj"].T
    b1 = np.zeros((P, 32), np.float32)
    b1[:, 0:16] = join(g["L3_ffn_ln_w"].reshape(8, P).T, g["L3_ffn_ln_b"].reshape(8, P).T)
    a["L3_b1"] = b1
    a["L3_b2"] = np.zeros((8, D), np.float32)
    return {k: np.ascontiguousarray(v) for k, v in a.items()}


def kernel(**inputs):
    import concourse.bacc as bacc
    from concourse.bass_utils import run_bass_kernel_spmd

    nc = bacc.Bacc("TRN2", target_bir_lowering=False, num_devices=1)
    arrays, aps = {}, {}
    for name, v in laid_out(inputs).items():
        arrays[f"in_{name}"] = v
        aps[name] = nc.dram_tensor(f"in_{name}", v.shape, mybir.dt.from_np(v.dtype), kind="ExternalInput").ap()
    out = nc.dram_tensor("out", (TOK, D), F32, kind="ExternalOutput").ap()
    build(nc, aps, out)
    r = run_bass_kernel_spmd(nc, [arrays], core_ids=[0])
    return r.results[0]["out"].reshape(B, T, D)
```
